# Optimizing a Trainium2 kernel written in Bass

```python
import numpy as np
import jax
import jax.numpy as jnp

def _softmax(x, axis=-1):
    return jax.nn.softmax(x, axis=axis)

def _gelu(x):
    return jax.nn.gelu(x, approximate=True)

def _silu(x):
    return jax.nn.silu(x)

def _sigmoid(x):
    return jax.nn.sigmoid(x)

def _layernorm(x, axis=-1, eps=1e-05):
    m = jnp.mean(x, axis=axis, keepdims=True)
    v = jnp.var(x, axis=axis, keepdims=True)
    return (x - m) / jnp.sqrt(v + eps)

def _scatter_add(tgt, idx, src, axis=0):
    return tgt.at[idx].add(src)

def _segment_sum(src, seg, n):
    return jax.ops.segment_sum(src, seg, n)
kernel_name = 'mk_decoder_postln_d1_seqx_r8_e72be9'

def setup_inputs(seed: int=0):
    np.random.seed(seed)
    _w = jnp.asarray

    def _rec_inputs():
        import jax
        import jax.numpy as jnp
        _rk = jax.random.key(seed)
        x = -0.0002928 + 1 * jax.random.normal(jax.random.fold_in(_rk, 1), (2, 512, 128), jnp.float32)
        _lenS = 512 - jax.random.randint(jax.random.fold_in(_rk, 7), (2,), 0, max(1, 512 // 4) + 1, jnp.int32)
        _lenS2 = 77 - jax.random.randint(jax.random.fold_in(_rk, 8), (2,), 0, max(1, 77 // 4) + 1, jnp.int32)
        _ctx_1024P = jax.random.normal(jax.random.fold_in(_rk, 11), (2, 16, 128), jnp.float32)
        _ctx_1024c = jax.random.dirichlet(jax.random.fold_in(_rk, 511), 0.3 * jnp.ones((16,), jnp.float32), (2, 77))
        _ctx_1024t = jnp.einsum('bsk,bkd->bsd', _ctx_1024c, _ctx_1024P)
        _ctx_1024t = _ctx_1024t * jax.lax.rsqrt(jnp.mean(jnp.square(_ctx_1024t)) + 1e-12) * 0.953939
        ctx_1024 = -1.39393e-06 + 0.999914 * (_ctx_1024t + 0.3 * jax.random.normal(jax.random.fold_in(_rk, 611), (2, 77, 128), jnp.float32))
        _validS = jnp.arange(512)[None, :] < _lenS[:, None]
        _validS2 = jnp.arange(77)[None, :] < _lenS2[:, None]
        _causal = jnp.tril(jnp.ones((512, 512), dtype=bool))
        mask_BxS2_ik0 = jnp.where(jnp.broadcast_to(_validS2[:, :], (2, 77)), 0, 1).astype(jnp.int32)
        return (x, ctx_1024, mask_BxS2_ik0)
    x, ctx_1024, mask_BxS2_ik0 = _rec_inputs()

    def _L0_attn_setup():
        import jax, jax.numpy as jnp
        import numpy as np
        B_, L, D_MODEL = (2, 256, 128)
        EXPAND, D_INNER, D_STATE, DT_RANK, D_CONV = (2, 256, 16, 64, 4)
        DT_MIN, DT_MAX = (0.001, 0.1)
        key = jax.random.key(seed)
        ks = jax.random.split(key, 8)
        s = lambda fan: 1.0 / np.sqrt(fan)
        A0 = jnp.broadcast_to(jnp.arange(1, D_STATE + 1, dtype=jnp.float32), (D_INNER, D_STATE))
        return {'x': jax.random.normal(ks[0], (B_, L, D_MODEL), jnp.float32), 'W_in': jax.random.normal(ks[1], (D_MODEL, 2 * D_INNER), jnp.float32) * s(D_MODEL), 'conv_k': jax.random.normal(ks[2], (D_CONV, D_INNER // EXPAND, D_INNER), jnp.float32) * s(D_CONV * D_INNER // EXPAND), 'conv_b': jnp.zeros((D_INNER,), jnp.float32), 'W_x': jax.random.normal(ks[3], (D_INNER, DT_RANK + 2 * D_STATE), jnp.float32) * s(D_INNER), 'W_dt': jax.random.normal(ks[4], (DT_RANK, D_INNER), jnp.float32) * s(DT_RANK), 'b_dt': jnp.zeros((D_INNER,), jnp.float32), 'A_log': jnp.log(A0), 'D': jnp.ones((D_INNER,), jnp.float32), 'W_out': jax.random.normal(ks[5], (D_INNER, D_MODEL), jnp.float32) * s(D_INNER)}
    _L0_attn_all = _L0_attn_setup()
    _L0_attn_in = {k: v for k, v in _L0_attn_all.items() if k in ('W_in', 'conv_k', 'conv_b', 'W_x', 'W_dt', 'b_dt', 'A_log', 'D', 'W_out')}
    del _L0_attn_all

    def _L0_xattn_setup():
        import jax, jax.numpy as jnp
        import numpy as np
        B, S, LATENT, HEADS = (2, 256, 128, 16)
        DEPTH = LATENT // HEADS
        NEG = 1000000000.0
        key = jax.random.key(seed)
        ks = jax.random.split(key, 7)
        scale = 1.0 / np.sqrt(LATENT)
        return {'q': jax.random.normal(ks[0], (B, S, LATENT), jnp.float32), 'k': jax.random.normal(ks[1], (B, S, LATENT), jnp.float32), 'v': jax.random.normal(ks[2], (B, S, LATENT), jnp.float32), 'v_mask': jax.random.randint(ks[3], (B, S), 0, 2, jnp.int32), 'Wq': jax.random.normal(ks[4], (LATENT, LATENT), jnp.float32) * scale, 'Wk': jax.random.normal(ks[5], (LATENT, LATENT), jnp.float32) * scale, 'Wv': jax.random.normal(ks[6], (LATENT, LATENT), jnp.float32) * scale}
    _L0_xattn_all = _L0_xattn_setup()
    _L0_xattn_in = {k: v for k, v in _L0_xattn_all.items() if k in ('Wq', 'Wk', 'Wv')}
    del _L0_xattn_all

    def _L0_ffn_setup():
        import jax, jax.numpy as jnp
        import numpy as np
        B, T, C = (4, 256, 128)
        H = 128
        E_ATT = 8
        E_MOE = 8
        I = 128
        MIN_ATT = 2
        MIN_MOE = 2
        EPS_LN = 1e-05

        def _normalize(x, axis):
            n = jnp.linalg.norm(x, axis=axis, keepdims=True)
            return x / jnp.maximum(n, 1e-12)

        def _layernorm(x, w, b):
            m = jnp.mean(x, axis=-1, keepdims=True)
            v = jnp.mean(jnp.square(x - m), axis=-1, keepdims=True)
            return (x - m) / jnp.sqrt(v + EPS_LN) * w + b

        def _gating(flat_hs, sim, gates, min_experts):
            logits = _normalize(flat_hs, -1) @ _normalize(sim, 0) - jax.nn.sigmoid(gates)
            gated = jax.nn.relu(logits)
            mask = (gated > 0).astype(gated.dtype)
            inactive = jnp.sum(mask, axis=1) == 0
            _, idx = jax.lax.top_k(logits, min_experts)
            onehot = jnp.sum(jax.nn.one_hot(idx, logits.shape[-1], dtype=gated.dtype), axis=1)
            put = inactive[:, None] & (onehot > 0)
            mask = jnp.where(put, 1.0, mask)
            masked = jnp.where(mask > 0, gated, -jnp.inf)
            return jax.nn.softmax(masked, axis=-1)
        key = jax.random.key(seed)
        ks = jax.random.split(key, 12)
        d = {}
        d['x'] = jax.random.normal(ks[0], (B, T, C), dtype=jnp.float32)
        d['ln1_w'] = jnp.ones((C,), jnp.float32)
        d['ln1_b'] = jnp.zeros((C,), jnp.float32)
        d['ln2_w'] = jnp.ones((C,), jnp.float32)
        d['ln2_b'] = jnp.zeros((C,), jnp.float32)
        d['smha_sim'] = jax.random.normal(ks[1], (C, E_ATT), dtype=jnp.float32)
        d['smha_gates'] = jnp.zeros((E_ATT,), jnp.float32)
        sq = 1.0 / np.sqrt(C + H)
        d['q_proj'] = jax.random.normal(ks[2], (E_ATT, C, H), dtype=jnp.float32) * sq
        d['k_proj'] = jax.random.normal(ks[3], (E_ATT, C, H), dtype=jnp.float32) * sq
        d['v_proj'] = jax.random.normal(ks[4], (E_ATT, C, H), dtype=jnp.float32) * sq
        d['o_proj'] = jax.random.normal(ks[5], (E_ATT, H, C), dtype=jnp.float32) * sq
        d['moe_sim'] = jax.random.normal(ks[6], (C, E_MOE), dtype=jnp.float32)
        d['moe_gates'] = jnp.zeros((E_MOE,), jnp.float32)
        d['w1'] = jax.random.normal(ks[7], (E_MOE, C, I), dtype=jnp.float32) * (1.0 / np.sqrt(C))
        d['w2'] = jax.random.normal(ks[8], (E_MOE, I, C), dtype=jnp.float32) * (1.0 / np.sqrt(I))
        return d
    _L0_ffn_all = _L0_ffn_setup()
    _L0_ffn_in = {k: v for k, v in _L0_ffn_all.items() if k in ('ln1_w', 'ln1_b', 'ln2_w', 'ln2_b', 'smha_sim', 'smha_gates', 'q_proj', 'k_proj', 'v_proj', 'o_proj', 'moe_sim', 'moe_gates', 'w1', 'w2')}
    del _L0_ffn_all
    return {'x': x, 'ctx_1024': ctx_1024, 'mask_BxS2_ik0': mask_BxS2_ik0, 'L0_attn_W_in': _L0_attn_in['W_in'], 'L0_attn_conv_k': _L0_attn_in['conv_k'], 'L0_attn_conv_b': _L0_attn_in['conv_b'], 'L0_attn_W_x': _L0_attn_in['W_x'], 'L0_attn_W_dt': _L0_attn_in['W_dt'], 'L0_attn_b_dt': _L0_attn_in['b_dt'], 'L0_attn_A_log': _L0_attn_in['A_log'], 'L0_attn_D': _L0_attn_in['D'], 'L0_attn_W_out': _L0_attn_in['W_out'], 'L0_xattn_Wq': _L0_xattn_in['Wq'], 'L0_xattn_Wk': _L0_xattn_in['Wk'], 'L0_xattn_Wv': _L0_xattn_in['Wv'], 'L0_ffn_ln1_w': _L0_ffn_in['ln1_w'], 'L0_ffn_ln1_b': _L0_ffn_in['ln1_b'], 'L0_ffn_ln2_w': _L0_ffn_in['ln2_w'], 'L0_ffn_ln2_b': _L0_ffn_in['ln2_b'], 'L0_ffn_smha_sim': _L0_ffn_in['smha_sim'], 'L0_ffn_smha_gates': _L0_ffn_in['smha_gates'], 'L0_ffn_q_proj': _L0_ffn_in['q_proj'], 'L0_ffn_k_proj': _L0_ffn_in['k_proj'], 'L0_ffn_v_proj': _L0_ffn_in['v_proj'], 'L0_ffn_o_proj': _L0_ffn_in['o_proj'], 'L0_ffn_moe_sim': _L0_ffn_in['moe_sim'], 'L0_ffn_moe_gates': _L0_ffn_in['moe_gates'], 'L0_ffn_w1': _L0_ffn_in['w1'], 'L0_ffn_w2': _L0_ffn_in['w2']}

def reference(x, ctx_1024, mask_BxS2_ik0, L0_attn_W_in, L0_attn_conv_k, L0_attn_conv_b, L0_attn_W_x, L0_attn_W_dt, L0_attn_b_dt, L0_attn_A_log, L0_attn_D, L0_attn_W_out, L0_xattn_Wq, L0_xattn_Wk, L0_xattn_Wv, L0_ffn_ln1_w, L0_ffn_ln1_b, L0_ffn_ln2_w, L0_ffn_ln2_b, L0_ffn_smha_sim, L0_ffn_smha_gates, L0_ffn_q_proj, L0_ffn_k_proj, L0_ffn_v_proj, L0_ffn_o_proj, L0_ffn_moe_sim, L0_ffn_moe_gates, L0_ffn_w1, L0_ffn_w2):
    import jax
    import jax.numpy as jnp

    def _L0_attn_ref(x, W_in, conv_k, conv_b, W_x, W_dt, b_dt, A_log, D, W_out):
        import jax, jax.numpy as jnp
        import numpy as np
        B_, L, D_MODEL = (2, 256, 128)
        EXPAND, D_INNER, D_STATE, DT_RANK, D_CONV = (2, 256, 16, 64, 4)
        DT_MIN, DT_MAX = (0.001, 0.1)
        xz = x @ W_in
        xs, res = jnp.split(xz, 2, axis=-1)
        xc = jax.lax.conv_general_dilated(xs, conv_k, window_strides=(1,), padding=[(D_CONV - 1, 0)], dimension_numbers=('NWC', 'WIO', 'NWC'), feature_group_count=EXPAND) + conv_b
        u = jax.nn.silu(xc)
        dbc = u @ W_x
        dt_raw = dbc[..., :DT_RANK]
        Bm = dbc[..., DT_RANK:DT_RANK + D_STATE]
        Cm = dbc[..., DT_RANK + D_STATE:]
        delta = jax.nn.softplus(dt_raw @ W_dt + b_dt)
        delta = jnp.clip(delta, DT_MIN, DT_MAX)
        A = -jnp.exp(A_log)
        dA = jnp.exp(delta[..., None] * A)
        dBu = delta[..., None] * u[..., None] * Bm[:, :, None, :]

        def step(h, inp):
            dA_t, dBu_t, C_t = inp
            h = dA_t * h + dBu_t
            y_t = jnp.einsum('bdn,bn->bd', h, C_t)
            return (h, y_t)
        h0 = jnp.zeros((x.shape[0], D_INNER, D_STATE), dA.dtype)
        _, y = jax.lax.scan(step, h0, (dA.transpose(1, 0, 2, 3), dBu.transpose(1, 0, 2, 3), Cm.transpose(1, 0, 2)))
        y = y.transpose(1, 0, 2) + u * D
        out = y * jax.nn.silu(res) @ W_out
        return out

    def _L0_xattn_ref(q, k, v, v_mask, Wq, Wk, Wv):
        import jax, jax.numpy as jnp
        import numpy as np
        B, S, LATENT, HEADS = (2, 256, 128, 16)
        DEPTH = LATENT // HEADS
        NEG = 1000000000.0
        b, sq, _ = q.shape
        sk = k.shape[1]
        wq = (q @ Wq).reshape(b, sq, HEADS, DEPTH).transpose(0, 2, 1, 3)
        wk = (k @ Wk).reshape(b, sk, HEADS, DEPTH).transpose(0, 2, 1, 3)
        wv = (v @ Wv).reshape(b, sk, HEADS, DEPTH).transpose(0, 2, 1, 3)
        scores = jnp.einsum('bhqd,bhkd->bhqk', wq, wk) / jnp.sqrt(jnp.asarray(DEPTH, jnp.float32))
        vm = v_mask.astype(jnp.float32)[:, None, None, :]
        scores = scores - (1.0 - vm) * NEG
        causal = (1.0 - jnp.tril(jnp.ones((sq, sk), jnp.float32))) * NEG
        scores = scores - causal[None, None, :, :]
        probs = jax.nn.softmax(scores, axis=-1)
        out = jnp.einsum('bhqk,bhkd->bhqd', probs, wv)
        return out.transpose(0, 2, 1, 3).reshape(b, sq, LATENT)

    def _L0_ffn_ref(x, ln1_w, ln1_b, ln2_w, ln2_b, smha_sim, smha_gates, q_proj, k_proj, v_proj, o_proj, moe_sim, moe_gates, w1, w2):
        import jax, jax.numpy as jnp
        import numpy as np
        B, T, C = (4, 256, 128)
        H = 128
        E_ATT = 8
        E_MOE = 8
        I = 128
        MIN_ATT = 2
        MIN_MOE = 2
        EPS_LN = 1e-05

        def _normalize(x, axis):
            n = jnp.linalg.norm(x, axis=axis, keepdims=True)
            return x / jnp.maximum(n, 1e-12)

        def _layernorm(x, w, b):
            m = jnp.mean(x, axis=-1, keepdims=True)
            v = jnp.mean(jnp.square(x - m), axis=-1, keepdims=True)
            return (x - m) / jnp.sqrt(v + EPS_LN) * w + b

        def _gating(flat_hs, sim, gates, min_experts):
            logits = _normalize(flat_hs, -1) @ _normalize(sim, 0) - jax.nn.sigmoid(gates)
            gated = jax.nn.relu(logits)
            mask = (gated > 0).astype(gated.dtype)
            inactive = jnp.sum(mask, axis=1) == 0
            _, idx = jax.lax.top_k(logits, min_experts)
            onehot = jnp.sum(jax.nn.one_hot(idx, logits.shape[-1], dtype=gated.dtype), axis=1)
            put = inactive[:, None] & (onehot > 0)
            mask = jnp.where(put, 1.0, mask)
            masked = jnp.where(mask > 0, gated, -jnp.inf)
            return jax.nn.softmax(masked, axis=-1)
        b, t, c = x.shape
        n1 = _layernorm(x, ln1_w, ln1_b)
        rw = _gating(n1.reshape(b * t, c), smha_sim, smha_gates, MIN_ATT).reshape(b, t, -1)
        q = jnp.einsum('btc,ech,bte->bth', n1, q_proj, rw)
        k = jnp.einsum('btc,ech,bte->bth', n1, k_proj, rw)
        v = jnp.einsum('btc,ech,bte->bth', n1, v_proj, rw)
        scale = 1.0 / jnp.sqrt(jnp.asarray(q.shape[-1], q.dtype))
        scores = jnp.einsum('bth,bsh->bts', q, k) * scale
        causal = jnp.tril(jnp.ones((t, t), dtype=bool))
        scores = jnp.where(causal, scores, -jnp.inf)
        attn = jnp.einsum('bts,bsh->bth', jax.nn.softmax(scores, axis=-1), v)
        attn_out = jnp.einsum('bth,ehc,bte->btc', attn, o_proj, rw)
        hs = x + attn_out
        n2 = _layernorm(hs, ln2_w, ln2_b)
        rw2 = _gating(n2.reshape(b * t, c), moe_sim, moe_gates, MIN_MOE).reshape(b, t, -1)
        inter = jax.nn.gelu(jnp.einsum('btc,eci->btei', n2, w1), approximate=False)
        moe_out = jnp.einsum('btei,eic,bte->btc', inter, w2, rw2)
        return hs + moe_out
    x = _layernorm(x + _L0_attn_ref(x, L0_attn_W_in, L0_attn_conv_k, L0_attn_conv_b, L0_attn_W_x, L0_attn_W_dt, L0_attn_b_dt, L0_attn_A_log, L0_attn_D, L0_attn_W_out), axis=-1)
    x = _layernorm(x + _L0_xattn_ref(x, ctx_1024, ctx_1024, mask_BxS2_ik0, L0_xattn_Wq, L0_xattn_Wk, L0_xattn_Wv), axis=-1)
    x = _layernorm(x + _L0_ffn_ref(x, L0_ffn_ln1_w, L0_ffn_ln1_b, L0_ffn_ln2_w, L0_ffn_ln2_b, L0_ffn_smha_sim, L0_ffn_smha_gates, L0_ffn_q_proj, L0_ffn_k_proj, L0_ffn_v_proj, L0_ffn_o_proj, L0_ffn_moe_sim, L0_ffn_moe_gates, L0_ffn_w1, L0_ffn_w2), axis=-1)
    return x

_drawn_inputs = setup_inputs


def setup_inputs(seed=0):
    import zlib

    import numpy as np

    out = dict(_drawn_inputs(seed))
    spreads = {'L0_attn_conv_b': (0.0, 0.1),
     'L0_attn_b_dt': (0.0, 2.0),
     'L0_attn_D': (1.0, 0.2),
     'L0_ffn_ln1_w': (1.0, 0.2),
     'L0_ffn_ln1_b': (0.0, 0.1),
     'L0_ffn_ln2_w': (1.0, 0.2),
     'L0_ffn_ln2_b': (0.0, 0.1),
     'L0_ffn_smha_gates': (0.0, 0.1),
     'L0_ffn_moe_gates': (0.0, 0.1)}
    factors = {'L0_attn_W_dt': 8.0, 'L0_ffn_k_proj': 3.578}
    for name, (base, spread) in spreads.items():
        noise = np.random.default_rng([zlib.crc32(name.encode()), seed]).standard_normal(out[name].shape)
        drawn = base * np.exp(spread * noise) if base else spread * noise
        out[name] = jnp.asarray(drawn.astype(out[name].dtype))
    for name, factor in factors.items():
        out[name] = (out[name] * factor).astype(out[name].dtype)
    return out
```

```python
from contextlib import ExitStack

import numpy as np

import concourse.bass as bass
from concourse import mybir

F32 = mybir.dt.float32
BF16 = mybir.dt.bfloat16
I32 = mybir.dt.int32
ALU = mybir.AluOpType
ACT = mybir.ActivationFunctionType
AX_X = mybir.AxisListType.X

P = 128
B, T, C = 2, 512, 128
K = T // P
DI = 256
HV = DI // P
NS = 16
DTR = 64
TAPS = 4
NH, HD = 16, 8
S2 = 77
FLAT = NH * S2
CH = -(-FLAT // P)
HD1 = HD + 1
E = 8
NEG = 1.0e9
LN_EPS = 1e-5
DT_MIN, DT_MAX = 0.001, 0.1
SOFTPLUS_CAP = 0.2
U = 4

WIDTHS = {"ident": P, "causal": P, "sel32": 32, "sel8": E, "tri": E * E, "headof": NH, "xcausal": S2,
          "pairhead": CH * NH}
AT = {}
_at = 0
for _name, _width in WIDTHS.items():
    AT[_name] = (_at, _at + _width)
    _at += _width
PAIR_COLS = CH * P
CONST_COLS = _at + PAIR_COLS
AT["pairtok"] = (_at, CONST_COLS)
CONST_FIRST = AT["causal"][0]


SMALL_COLS = 3 * HV + 4 + HV * NS + 4 * E


def shape_constants():
    c = np.zeros((P, CONST_COLS), np.float32)
    p = np.arange(P)[:, None]

    def put(name, values):
        c[:values.shape[0], AT[name][0]:AT[name][1]] = values

    put("ident", (p == np.arange(P)).astype(np.float32))
    put("causal", np.where(np.arange(P) > p, -1e30, 0.0).astype(np.float32))
    put("sel32", (p % 32 == np.arange(32)).astype(np.float32))
    put("sel8", ((p % E == np.arange(E)) & (p < 3 * E)).astype(np.float32))
    i, j = np.arange(E * E) // E, np.arange(E * E) % E
    put("tri", np.broadcast_to((j < i).astype(np.float32), (P, E * E)))
    put("headof", (p // HD == np.arange(NH)).astype(np.float32))
    put("xcausal", np.where(np.arange(S2) > p, -NEG, 0.0).astype(np.float32))
    flat = P * np.arange(CH)[None, :] + p
    put("pairhead", ((flat // S2)[:, :, None] == np.arange(NH)).astype(np.float32).reshape(P, CH * NH))
    f = np.arange(CH * P)
    put("pairtok", ((f % S2 == np.arange(S2)[:, None]) & (f < FLAT)).astype(np.float32))
    return c


def heads_of(j):
    rows = min(P, FLAT - P * j)
    return P * j // S2, (P * j + rows - 1) // S2, rows


def decoder_layer(nc, a, out):
    with ExitStack() as ctx:
        def sb(name, shape, dt=F32):
            return ctx.enter_context(nc.sbuf_tensor(name, shape, dt))

        def sem(name):
            return ctx.enter_context(nc.semaphore(name))

        ps = ctx.enter_context(nc.psum_tensor("ps", [P, 8, 512], F32))

        def bank(i, rows=P):
            return ps[0:rows, i, :]

        const = sb("const", [P, CONST_COLS - PAIR_COLS])

        def cst(name, rows=P):
            return const[0:rows, AT[name][0]:AT[name][1]]

        ident = cst("ident")
        ident_bf = sb("ident_bf", [P, P], BF16)
        causal_bf = sb("causal_bf", [P, P], BF16)
        sel32 = sb("sel32", [96, 32, P], BF16)
        sel8 = sb("sel8", [3 * E, E, P], BF16)
        ones = sb("ones", [P, P])
        ones_bf = sb("ones_bf", [96, P], BF16)
        minus_half = sb("minus_half", [P, 2 * E])
        w_in = sb("w_in", [P, 2 * DI])
        conv_k = sb("conv_k", [P, TAPS, DI])
        w_x = sb("w_x", [P, HV, DTR + 2 * NS])
        w_dt = sb("w_dt", [DTR, DI])
        w_out = sb("w_out", [P, HV, C])
        small = sb("small", [P, SMALL_COLS])
        conv_b, b_dt, skip_d = (small[:, i * HV:(i + 1) * HV] for i in range(3))
        ln_w, ln_b = small[:, 6:8], small[:, 8:10]
        a_log = small[:, 10:42].rearrange("p (h n) -> p h n", h=HV)
        sim = small[:, 42:58].rearrange("p (n e) -> p n e", n=2)
        gates_in = small[:, 58:74].rearrange("p (n e) -> p n e", n=2)
        neg_a = sb("neg_a", [P, HV, NS])
        exp_a = sb("exp_a", [P, HV, NS])
        diag_d = sb("diag_d", [P, HV, P])
        wq = sb("wq", [P, P])
        wk = sb("wk", [P, P])
        wv = sb("wv", [P, P])
        sim_sq = sb("sim_sq", [P, 2, E])
        sim_rn = sb("sim_rn", [P, 2, E])
        sim_ss = sb("sim_ss", [P, 2, E])
        simn = sb("simn", [P, 2, E])
        gates = sb("gates", [P, 2, E])
        gate_s = sb("gate_s", [P, 2, E])
        w_q = sb("w_q", [P, E, P])
        w_k = sb("w_k", [P, E, P])
        w_v = sb("w_v", [P, E, P])
        w_o = sb("w_o", [P, E, P])
        w_1 = sb("w_1", [P, E, P])
        w_2 = sb("w_2", [P, E, P])

        x = sb("x", [P, B, K, C])
        xT = sb("xT", [P, B, T])
        xsT = sb("xsT", [P, B, HV, TAPS - 1 + T])
        zT = sb("zT", [P, B, HV, T])
        uT = sb("uT", [P, B, HV, T])
        bc_parts = sb("bc_parts", [96, B, T], BF16)
        e_dt = sb("e_dt", [P, B, HV, T])
        log_dt = sb("log_dt", [P, B, HV, T])
        r_dt = sb("r_dt", [P, HV, T])
        delta = sb("delta", [P, B, HV, T])
        du = sb("du", [P, B, HV, T])
        decay = sb("decay", [P, 2, HV, T])
        states = sb("states", [P, 2, HV, T])
        c_rep = sb("c_rep", [P, 2, T])
        prod = sb("prod", [P, 2, HV, T])
        x1 = sb("x1", [P, B, K, C])
        ctx_sb = sb("ctx_sb", [S2, B, C])
        ctxT = sb("ctxT", [P, B, S2])
        kT = sb("kT", [P, B, S2])
        v_sb = sb("v_sb", [S2, B, P])
        v_rep = sb("v_rep", [P, B, CH, P])
        k_diag = sb("k_diag", [P, B, FLAT])
        v_diag = sb("v_diag", [P, B, CH, NH * HD1])
        mask_i = sb("mask_i", [1, B, S2], I32)
        mask_f = sb("mask_f", [1, B, S2])
        mask_rest = sb("mask_rest", [64, B, S2])
        mask_small = sb("mask_small", [96, B, S2], BF16)
        mask_parts = sb("mask_parts", [96, B, FLAT], BF16)
        xs_max = sb("xs_max", [P, NH])
        xrec = sb("xrec", [P, NH])
        xav = sb("xav", [P, P])
        stats = sb("stats", [P, K, 6])
        mv = sb("mv", [P, K, 2])
        var_eps = sb("var_eps", [P, K])
        rstd = sb("rstd", [P, K])
        g_ss = sb("g_ss", [P, K])
        g_rn = sb("g_rn", [P, K])
        g_l0 = sb("g_l0", [P, K, E])
        g_l = sb("g_l", [P, K, E])
        g_gt = sb("g_gt", [P, K, E, E])
        g_eq = sb("g_eq", [P, K, E, E])
        g_eqt = sb("g_eqt", [P, K, E, E])
        g_cmp = sb("g_cmp", [P, K, E, E])
        g_rank = sb("g_rank", [P, K, E])
        g_top = sb("g_top", [P, K, E])
        g_relu = sb("g_relu", [P, K, E])
        g_act = sb("g_act", [P, K, E])
        g_max = sb("g_max", [P, K])
        g_idle = sb("g_idle", [P, K])
        g_put = sb("g_put", [P, K, E])
        g_mask = sb("g_mask", [P, K, E])
        g_sh = sb("g_sh", [P, K, E])
        g_ex = sb("g_ex", [P, K, E])
        g_w = sb("g_w", [P, K, E])
        g_sum = sb("g_sum", [P, K])
        g_rs = sb("g_rs", [P, K])
        g_rw = sb("g_rw", [P, K, E])
        g_r1 = sb("g_r1", [P, K, E])
        rw_parts = sb("rw_parts", [P, K, 3, E], BF16)
        rwT = sb("rwT", [3 * E, 2, B, T], BF16)
        a_max = sb("a_max", [P, K])
        a_nmax = sb("a_nmax", [P, K])
        a_sum = sb("a_sum", [P, K])
        a_rec = sb("a_rec", [P, K])

        ap_ = e_dt[:].rearrange("p b h t -> p (b h) t")
        apT = log_dt[:].rearrange("p b h t -> p (b h) t")
        inter = states[:, 0]
        scaled = states[:, 1]
        xe = prod[:, 0]
        hs = du[:, 0].rearrange("p h (k c) -> p h k c", c=C)
        hx = du[:, 1].rearrange("p h (k c) -> p h k c", c=C)
        x3p = delta[:, 0].rearrange("p h (k c) -> p h k c", c=C)
        x3 = delta[:, 1].rearrange("p h (k c) -> p h k c", c=C)
        x1T = xT
        gT = r_dt
        aqT = zT[:, 0]
        akT = zT[:, 1]
        av = uT[:, 0].rearrange("p h (k c) -> p h k c", c=C)
        attnT = uT[:, 1]
        nT = decay[:, 0]
        nsq = decay[:, 1]
        x1p = xsT[:].rearrange("p b h t -> p (b h t)")[:, 0:B * T].rearrange("p (b k c) -> p b k c", b=B, c=C)
        x2p = xsT[:].rearrange("p b h t -> p (b h t)")[:, B * T:2 * B * T].rearrange("p (b k c) -> p b k c", b=B, c=C)
        xp = v_rep[:].rearrange("p b j c -> p (b j c)")[:, 0:2 * FLAT].rearrange("p (i f) -> p i f", i=2)
        xs_masked = delta[:].rearrange("p b h t -> p (b h t)")[:, 0:FLAT]
        xpT = du[:].rearrange("p b h t -> p (b h t)")[:, 0:CH * P].rearrange("p (j t) -> p j t", t=P)
        x2 = prod[:, 1].rearrange("p h (k c) -> p h k c", c=C)
        dt_raw = prod[0:DTR, 0]
        bc_rest = c_rep[:, 0, :]
        nrm = conv_k[:].rearrange("p a o -> p (a o)").rearrange("p (b k c) -> p b k c", b=B, c=C)
        pairtok = states[0:S2].rearrange("p i h t -> p (i h t)")[:, 0:PAIR_COLS]
        qT = c_rep
        SCALE_X = float(HD) ** -0.5
        SCALE_A = float(P) ** -0.5

        ld = {n: sem("ld_" + n) for n in ("x", "win", "conv", "small", "ctx", "masks", "qkv", "o", "moe")}
        s = {n: sem(n) for n in (
            "xT_psum", "xT_ready", "win_psum", "xs_ready", "z_ready", "conv_psum", "u_ready", "dbc_psum", "dtraw_ready",
            "bc_ready", "wdt_psum", "e_ready", "ecap_ready", "log_ready", "delta_ready", "fills_ready", "sel_ready",
            "diag_ready", "nega_ready", "b_psum", "c_psum", "dbu_done", "decay_ready", "scan_done", "crep_ready",
            "prod_done", "sum_done", "g_ready", "wout_psum", "x1p_ready", "dve_chain", "var_ready",
            "rstd_ready", "x1_ready", "x1T_psum", "x1T_ready", "q_psum", "qT_ready", "ctxT_psum", "ctxT_ready",
            "kv_psum", "kv_ready", "vrep_psum", "vrep_ready", "kdiag_ready", "vdiag_ready", "masks_ready", "masksmall_ready",
            "xs_psum", "xsub_done", "xexp_done", "xpT_psum", "xpT_ready", "xav_psum", "x2p_ready",
            "nrm_ready", "nT_psum", "nT_ready", "nsq_ready", "logit_psum", "norm_ready", "rnorm_ready", "gshift_ready",
            "gexp_ready", "rwparts_ready", "rwT_psum", "rwT_ready", "simsq_ready", "simss_psum", "simss_ready",
            "simrn_ready", "simn_ready", "gexpneg_ready", "gates_ready", "rwb_psum", "xe_ready", "xe_used", 
            "qkv_ready", "as_psum", "amax_ready", "aexp_done", "ap_ready", "apT_psum", "apT_ready", "att_psum",
            "att_ready", "rwo_psum", "oe_ready", "oe_used", "hs_ready", "h_psum", "inter_ready", "rwm_psum",
            "ge_ready", "ge_used", "moe_psum", "x3_ready", "stored", "expa_ready")}

        block = ctx.enter_context(nc.Block())

        @block.sync
        def _(sp):
            cc = a["consts"]
            sp.dma_start(x[:, 0], a["x"][0].rearrange("(k p) c -> p k c", p=P)).then_inc(ld["x"], 16)
            sp.dma_start(const[:, 0:CONST_FIRST], cc[:, 0:CONST_FIRST]).then_inc(ld["x"], 16)
            sp.dma_start(x[:, 1], a["x"][1].rearrange("(k p) c -> p k c", p=P)).then_inc(ld["x"], 16)
            sp.dma_start(w_in[:], a["L0_attn_W_in"]).then_inc(ld["win"], 16)
            sp.dma_start(conv_k[:], a["L0_attn_conv_k"].rearrange("k i o -> i k o")).then_inc(ld["conv"], 16)
            sp.dma_start(small[:], a["small"]).then_inc(ld["conv"], 16)
            sp.dma_start(w_x[:], a["L0_attn_W_x"].rearrange("(h p) n -> p h n", p=P)).then_inc(ld["small"], 16)
            sp.dma_start(w_dt[:], a["L0_attn_W_dt"]).then_inc(ld["small"], 16)
            sp.dma_start(w_out[:], a["L0_attn_W_out"].rearrange("(h p) n -> p h n", p=P)).then_inc(ld["small"], 16)
            sp.dma_start(const[:, CONST_FIRST:], cc[:, CONST_FIRST:CONST_COLS - PAIR_COLS]).then_inc(ld["masks"], 16)
            sp.dma_start(pairtok, cc[0:S2, CONST_COLS - PAIR_COLS:]).then_inc(ld["ctx"], 16)
            sp.dma_start(mask_i[:], a["mask_BxS2_ik0"].rearrange("(a b) n -> a b n", a=1)).then_inc(ld["masks"], 16)
            sp.dma_start(ctx_sb[:], a["ctx_1024"].rearrange("b n c -> n b c")).then_inc(ld["ctx"], 16)
            for dst, name in ((wq, "Wq"), (wk, "Wk"), (wv, "Wv")):
                sp.dma_start(dst[:], a["L0_xattn_" + name]).then_inc(ld["ctx"], 16)
            for dst, name, n in ((w_q, "q_proj", "qkv"), (w_k, "k_proj", "qkv"), (w_v, "v_proj", "qkv"),
                                 (w_o, "o_proj", "o"), (w_1, "w1", "moe"), (w_2, "w2", "moe")):
                sp.dma_start(dst[:], a["L0_ffn_" + name].rearrange("e i o -> i e o")).then_inc(ld[n], 16)
            sp.wait_ge(s["masksmall_ready"], 1)
            sp.wait_ge(s["fills_ready"], 6)
            for part in range(0, 96, 32):
                for b in range(B):
                    sp.dma_start(mask_parts[part:part + 1, b, :].rearrange("p (h t) -> p h t", h=NH),
                                 mask_small[part:part + 1, b, :].unsqueeze(1).to_broadcast([1, NH, S2])
                                 ).then_inc(s["masks_ready"], 16)
            for b in range(B):
                sp.wait_ge(s["x3_ready"], b + 1)
                sp.dma_start(out[b].rearrange("(k p) c -> p k c", p=P), x3[:, b]).then_inc(s["stored"], 16)
            sp.wait_ge(s["stored"], 16 * B)

        @block.tensor
        def _(pe):
            def transposes(dst, src, parts=K):
                for k in range(parts):
                    last = pe.transpose(dst[:, P * k:P * k + P], src[:, k, :], ident)
                return last

            for b in range(B):
                pe.wait_ge(ld["x"], 48)
                transposes(bank(b), x[:, b]).then_inc(s["xT_psum"], 1)
            pe.wait_ge(ld["win"], 16)
            for b in range(B):
                pe.wait_ge(s["xT_ready"], b + 1)
                for j in range(2 * HV):
                    if b:
                        pe.wait_ge(s["xs_ready"] if j < HV else s["z_ready"], j % HV + 1)
                    pe.matmul(bank(2 + j), w_in[:, P * j:P * j + P], xT[:, b, :], start=True,
                              stop=True).then_inc(s["win_psum"], 1)
            pe.wait_ge(ld["conv"], 32)
            pe.wait_ge(s["fills_ready"], 6)
            for b in range(B):
                for g in range(HV):
                    pe.wait_ge(s["xs_ready"], HV * b + g + 1)
                    if b:
                        pe.wait_ge(s["u_ready"], g + 1)
                    for t in range(TAPS):
                        mm = pe.matmul(bank(6 + g), conv_k[:, t, P * g:P * g + P], xsT[:, b, g, t:t + T],
                                       start=(t == 0), stop=(t == TAPS - 1))
                    mm.then_inc(s["conv_psum"], 1)
            pe.wait_ge(s["simsq_ready"], 1)
            pe.matmul(ps[:, 2, 0:2 * E], ones[:], sim_sq[:, :, :].rearrange("p n e -> p (n e)"), start=True,
                      stop=True).then_inc(s["simss_psum"], 1)
            pe.wait_ge(ld["small"], 48)
            for b in range(B):
                pe.wait_ge(s["u_ready"], HV * (b + 1))
                for h in range(HV):
                    mm = pe.matmul(bank(b, 96), w_x[:, h, :], uT[:, b, h, :], start=(h == 0), stop=(h == HV - 1))
                mm.then_inc(s["dbc_psum"], 1)
            pe.wait_ge(s["z_ready"], HV * B)
            pe.wait_ge(s["simss_ready"], 1)
            for b in range(B):
                pe.wait_ge(s["dtraw_ready"], b + 1)
                for h in range(HV):
                    pe.matmul(bank(2 + HV * b + h), w_dt[:, P * h:P * h + P], dt_raw[:, b, :], start=True,
                              stop=True).then_inc(s["wdt_psum"], 1)
            pe.wait_ge(ld["ctx"], 80)
            pe.wait_ge(ld["masks"], 32)
            for b in range(B):
                pe.transpose(ps[:, 6, P * b:P * b + S2], ctx_sb[:, b, :], ident[0:S2, 0:S2]).then_inc(s["ctxT_psum"], 1)
            pe.wait_ge(s["bc_ready"], B)
            for b in range(B):
                pe.wait_ge(s["ctxT_ready"], B)
                pe.matmul(ps[:, 7, P * b:P * b + S2], wk[:], ctxT[:, b, :], start=True, stop=True)
                pe.matmul(ps[0:S2, 7, 256 + P * b:256 + P * b + P], ctxT[:, b, :], wv[:], start=True,
                          stop=True).then_inc(s["kv_psum"], 1)
            for b in range(B):
                pe.wait_ge(s["kv_ready"], 2 * B)
                if b:
                    pe.wait_ge(s["vrep_ready"], 1)
                for j in range(CH):
                    mm = pe.matmul(ps[:, (0, 1, 6)[j // 4], P * (j % 4):P * (j % 4) + P],
                                   pairtok[:, P * j:P * j + P], v_sb[:, b, :],
                                   start=True, stop=True)
                mm.then_inc(s["vrep_psum"], 1)
            pe.wait_ge(s["e_ready"], HV * B)
            pe.wait_ge(s["vrep_ready"], B)
            pe.wait_ge(s["sel_ready"], 4)

            def spread(b, n, j):
                g = NS * b + n
                if b or not isinstance(n, int) or n >= 2:
                    pe.wait_ge(s["dbu_done"], 2 * (g - 1))
                pe.matmul(bank(j % 2), sel32[:, n, :], bc_parts[:, b, :], start=True, stop=True).then_inc(s["b_psum"], 1)
                if b or not isinstance(n, int) or n >= 1:
                    pe.wait_ge(s["crep_ready"], g)
                if isinstance(n, int):
                    c_sel = sel32[:, NS + n, :]
                else:
                    c_sel = sel32[:, NS:2 * NS, :][:, n, :]
                pe.matmul(bank(2), c_sel, bc_parts[:, b, :], start=True, stop=True).then_inc(s["c_psum"], 1)

            def add_state(b, n, j, stop=False):
                pe.wait_ge(s["prod_done"], NS * b + n + 1)
                for h in range(HV):
                    mm = pe.matmul(bank(6 + h), ident, prod[:, j % 2, h, :], start=False, stop=stop,
                                   skip_group_check=True)
                mm.then_inc(s["sum_done"], 1)

            for b in range(B):
                if b == 0:
                    pe.wait_ge(s["diag_ready"], HV)
                else:
                    pe.wait_ge(s["g_ready"], HV)
                for h in range(HV):
                    pe.matmul(bank(6 + h), diag_d[:, h, :], uT[:, b, h, :], start=True, stop=False,
                              skip_group_check=True)
                for n in range(2):
                    spread(b, n, n)
                with pe.Fori(0, (NS - 2) // 2) as i:
                    for j in range(2):
                        spread(b, i * 2 + (2 + j), j)
                        add_state(b, i * 2 + j, j)
                for n in range(NS - 2, NS):
                    add_state(b, n, n, stop=(n == NS - 1))
                for h in range(HV):
                    pe.wait_ge(s["g_ready"], HV * b + h + 1)
                if b:
                    pe.wait_ge(s["x1p_ready"], 1)
                for k in range(K):
                    for h in range(HV):
                        mm = pe.matmul(ps[:, 3, P * k:P * k + P], gT[:, h, P * k:P * k + P], w_out[:, h, :],
                                       start=(h == 0), stop=(h == HV - 1))
                mm.then_inc(s["wout_psum"], 1)

            for b in range(B):
                pe.wait_ge(s["x1_ready"], b + 1)
                transposes(bank(b), x1[:, b]).then_inc(s["x1T_psum"], 1)
            for b in range(B):
                pe.wait_ge(s["x1T_ready"], b + 1)
                pe.wait_ge(s["x1p_ready"], B)
                pe.matmul(bank(2 + b), wq[:], x1T[:, b, :], start=True, stop=True).then_inc(s["q_psum"], 1)
            pe.wait_ge(s["kdiag_ready"], B)
            pe.wait_ge(s["masks_ready"], 16 * 3 * B)

            def x_scores(i):
                b, k = divmod(i, K)
                pe.wait_ge(s["qT_ready"], b + 1)
                if i:
                    pe.wait_ge(s["xsub_done"], i)
                for c in range(0, FLAT, 512):
                    w = min(512, FLAT - c)
                    pe.matmul(ps[:, 4 + c // 512, 0:w], qT[:, b, P * k:P * k + P], k_diag[:, b, c:c + w],
                              start=True, stop=False)
                    mm = pe.matmul(ps[:, 4 + c // 512, 0:w], ones_bf[:], mask_parts[:, b, c:c + w],
                                   start=False, stop=True)
                mm.then_inc(s["xs_psum"], 1)

            def x_transposes(i):
                pe.wait_ge(s["xexp_done"], i + 1)
                if i:
                    pe.wait_ge(s["xpT_ready"], i)
                else:
                    pe.wait_ge(s["qT_ready"], B)
                for j in range(CH):
                    rows = heads_of(j)[2]
                    mm = pe.transpose(ps[0:rows, j // 4, P * (j % 4):P * (j % 4) + P],
                                      xp[:, i % 2, P * j:P * j + rows], ident)
                mm.then_inc(s["xpT_psum"], 1)

            def x_values(i):
                b = i // K
                pe.wait_ge(s["xpT_ready"], i + 1)
                if i:
                    pe.wait_ge(s["x2p_ready"], i)
                for j in range(CH):
                    h0, h1, rows = heads_of(j)
                    mm = pe.matmul(ps[:, 3, HD1 * h0:HD1 * (h1 + 1)],
                                   xpT[0:rows, j, :], v_diag[0:rows, b, j, HD1 * h0:HD1 * (h1 + 1)],
                                   start=(j == 0), stop=True, skip_group_check=True)
                mm.then_inc(s["xav_psum"], 1)

            def n_transposes(n, b):
                m = 2 * n + b
                pe.wait_ge(s["nrm_ready"], m + 1)
                if m:
                    pe.wait_ge(s["rwT_ready"], m)
                if n:
                    pe.wait_ge(s["att_ready"], B)
                transposes(bank(7), nrm[:, b]).then_inc(s["nT_psum"], 1)

            def logits(n, b):
                m = 2 * n + b
                pe.wait_ge(s["nsq_ready"], m + 1)
                pe.wait_ge(s["simn_ready"], 1)
                for k in range(K):
                    pe.matmul(ps[:, 7, 9 * k:9 * k + E], nT[:, b, P * k:P * k + P], simn[:, n, :], start=True, stop=True)
                    mm = pe.matmul(ps[:, 7, 9 * k + E:9 * k + 9], nsq[:, b, P * k:P * k + P], ones[:, 0:1],
                                   start=True, stop=True)
                mm.then_inc(s["logit_psum"], 1)

            def weights_t(n, b):
                m = 2 * n + b
                pe.wait_ge(s["rwparts_ready"], m + 1)
                for k in range(K):
                    mm = pe.transpose(ps[0:3 * E, 7, :].bitcast(BF16)[:, P * k:P * k + P],
                                      rw_parts[:, k, :, :].rearrange("p t e -> p (t e)"), ident_bf[:])
                mm.then_inc(s["rwT_psum"], 1)

            def spread_weight(dst, n, b, e):
                return pe.matmul(dst, sel8[:, e, :], rwT[:, n, b, :], start=True, stop=True)

            for i in range(K * B + 1):
                if i < K * B:
                    x_scores(i)
                if i:
                    x_transposes(i - 1)
                    x_values(i - 1)
                if i == K + 1:
                    n_transposes(0, 0)
                if i == K + 2:
                    logits(0, 0)
                if i == K + 3:
                    weights_t(0, 0)

            pe.wait_ge(ld["qkv"], 48)

            def spread_qkv(b, e):
                g = E * b + e
                pe.wait_ge(s["rwT_ready"], b + 1)
                if g >= 2:
                    pe.wait_ge(s["xe_ready"], g - 1)
                else:
                    pe.wait_ge(s["x2p_ready"], K * B)
                spread_weight(bank(2 + g % 2), 0, b, e).then_inc(s["rwb_psum"], 1)

            def qkv(b, e):
                g = E * b + e
                pe.wait_ge(s["xe_ready"], g + 1)
                if b and e == 0:
                    pe.wait_ge(s["qkv_ready"], 3)
                st, sp_ = e == 0, e == E - 1
                pe.matmul(bank(4), w_q[:, e, :], xe[:, g % 2, :], start=st, stop=sp_)
                pe.matmul(bank(5), w_k[:, e, :], xe[:, g % 2, :], start=st, stop=sp_)
                for k in range(K):
                    mm = pe.matmul(ps[:, 6, P * k:P * k + P], xe[:, g % 2, P * k:P * k + P], w_v[:, e, :],
                                   start=(st and k == 0), stop=sp_, skip_group_check=True)
                mm.then_inc(s["xe_used"], 1)

            def qkv_batch(b, between):
                spread_qkv(b, 0)
                for e in range(E):
                    if e + 1 < E:
                        spread_qkv(b, e + 1)
                    qkv(b, e)
                    if e in between:
                        between[e]()

            qkv_batch(0, {1: lambda: n_transposes(0, 1), 3: lambda: logits(0, 1), 6: lambda: weights_t(0, 1)})
            qkv_batch(1, {})

            def a_scores(b, i):
                m = K * b + i
                pe.wait_ge(s["qkv_ready"], 3 * (b + 1))
                if b:
                    pe.wait_ge(s["aexp_done"], i + 1)
                w = P * (i + 1)
                pe.matmul(ps[:, i, 0:w], aqT[:, b, P * i:P * i + P], akT[:, b, 0:w], start=True, stop=True)
                pe.matmul(ps[:, i, w - P:w], ident_bf[:], causal_bf[:], start=False, stop=True,
                          skip_group_check=True).then_inc(s["as_psum"], 1)

            def a_transposes(b, i):
                m = K * b + i
                pe.wait_ge(s["ap_ready"], m + 1)
                if b == 0 and i == 0:
                    pe.wait_ge(s["qkv_ready"], 3 * B)
                if b and i == 0:
                    pe.wait_ge(s["apT_ready"], 3)
                for j in range(i + 1):
                    at = P * (i - j) + (2 * P if j == 3 else 0)
                    mm = pe.transpose(ps[:, 4 + min(j, 2), at:at + P], ap_[:, i, P * j:P * j + P], ident)
                mm.then_inc(s["apT_psum"], 1)

            def a_values(b):
                pe.wait_ge(s["apT_ready"], 3 * (b + 1))
                if b:
                    pe.wait_ge(s["att_ready"], 1)
                else:
                    pe.wait_ge(s["rwT_ready"], B)
                for j in range(K):
                    mm = pe.matmul(ps[:, 7, P * j:T], av[:, b, j, :], apT[:, j, 0:T - P * j], start=(j == 0),
                                   stop=True, skip_group_check=True)
                mm.then_inc(s["att_psum"], 1)

            for i in range(K):
                a_scores(0, i)
            for i in range(K):
                a_transposes(0, i)
                a_scores(1, i)
            a_values(0)
            for i in range(K):
                a_transposes(1, i)
            a_values(1)

            pe.wait_ge(ld["o"], 16)

            def spread_o(b, e):
                g = E * b + e
                if g >= 2:
                    pe.wait_ge(s["oe_ready"], g - 1)
                else:
                    pe.wait_ge(s["aexp_done"], K * B)
                spread_weight(bank(2 + g % 2), 0, b, e).then_inc(s["rwo_psum"], 1)

            def o_proj(b, e):
                g = E * b + e
                pe.wait_ge(s["oe_ready"], g + 1)
                if g == 0:
                    pe.wait_ge(s["apT_ready"], 3 * B)
                for k in range(K):
                    mm = pe.matmul(ps[:, 4 + b, P * k:P * k + P], xe[:, g % 2, P * k:P * k + P], w_o[:, e, :],
                                   start=(e == 0 and k == 0), stop=(e == E - 1), skip_group_check=True)
                mm.then_inc(s["oe_used"], 1)

            def o_batch(b, between):
                spread_o(b, 0)
                for e in range(E):
                    if e + 1 < E:
                        spread_o(b, e + 1)
                    o_proj(b, e)
                    if e in between:
                        between[e]()

            o_batch(0, {})
            o_batch(1, {4: lambda: n_transposes(1, 0), 6: lambda: logits(1, 0)})
            weights_t(1, 0)

            pe.wait_ge(ld["moe"], 32)

            def moe_up(b, e):
                g = E * b + e
                pe.wait_ge(s["rwT_ready"], B + b + 1)
                if g >= 2:
                    pe.wait_ge(s["inter_ready"], g - 1)
                else:
                    pe.wait_ge(s["oe_ready"], E * B)
                pe.matmul(bank(2 + g % 2), w_1[:, e, :], nT[:, b, :], start=True, stop=True).then_inc(s["h_psum"], 1)
                if g >= 2:
                    pe.wait_ge(s["ge_ready"], g - 1)
                spread_weight(bank(g % 2), 1, b, e).then_inc(s["rwm_psum"], 1)

            def moe_down(b, e):
                g = E * b + e
                pe.wait_ge(s["ge_ready"], g + 1)
                if e == 0:
                    pe.wait_ge(s["hs_ready"], b + 1)
                for k in range(K):
                    mm = pe.matmul(ps[:, 4 + b, P * k:P * k + P], scaled[:, g % 2, P * k:P * k + P], w_2[:, e, :],
                                   start=(e == 0 and k == 0), stop=(e == E - 1), skip_group_check=True)
                mm.then_inc(s["ge_used"], 1)

            def moe_batch(b, between):
                moe_up(b, 0)
                for e in range(E):
                    if e + 1 < E:
                        moe_up(b, e + 1)
                    moe_down(b, e)
                    if e in between:
                        between[e]()

            moe_batch(0, {1: lambda: n_transposes(1, 1), 3: lambda: logits(1, 1), 6: lambda: weights_t(1, 1)})
            moe_batch(1, {})

        @block.vector
        def _(dve):
            chain = [0]

            def link(ins):
                chain[0] += 1
                ins.then_inc(s["dve_chain"], 1)
                dve.wait_ge(s["dve_chain"], chain[0])

            for b in range(B):
                dve.wait_ge(s["xT_psum"], b + 1)
                dve.tensor_copy(xT[:, b, :], bank(b)).then_inc(s["xT_ready"], 1)
            for b in range(B):
                for g in range(HV):
                    dve.wait_ge(s["win_psum"], 2 * HV * b + g + 1)
                    dve.tensor_copy(xsT[:, b, g, TAPS - 1:], bank(2 + g)).then_inc(s["xs_ready"], 1)
            dve.wait_ge(ld["conv"], 32)
            for h in range(HV):
                dve.tensor_scalar(diag_d[:, h, :], ident, skip_d[:, h:h + 1], None, ALU.mult).then_inc(s["diag_ready"], 1)
            dve.tensor_tensor(sim_sq[:], sim, sim, ALU.mult).then_inc(s["simsq_ready"], 1)
            dve.wait_ge(s["simss_psum"], 1)
            dve.tensor_scalar(sim_ss[:].rearrange("p n e -> p (n e)"), ps[:, 2, 0:2 * E], 1e-24, None,
                              ALU.max).then_inc(s["simss_ready"], 1)
            for b in range(B):
                dve.wait_ge(s["dbc_psum"], b + 1)
                dve.tensor_copy(dt_raw[:, b, :], bank(b)[0:DTR]).then_inc(s["dtraw_ready"], 1)
                bc = bank(b)[DTR:96]
                link(dve.tensor_copy(bc_parts[0:32, b, :], bc))
                link(dve.tensor_tensor(bc_rest[32:64, :], bc, bc_parts[0:32, b, :], ALU.subtract))
                link(dve.tensor_copy(bc_parts[32:64, b, :], bc_rest[32:64, :]))
                dve.tensor_tensor(bc_parts[64:96, b, :], bc_rest[32:64, :], bc_parts[32:64, b, :],
                                  ALU.subtract).then_inc(s["bc_ready"], 1)
            dve.wait_ge(ld["masks"], 32)
            link(dve.tensor_copy(mask_f[:], mask_i[:]))
            link(dve.tensor_scalar(mask_f[:], mask_f[:], -1.0, NEG, ALU.add, ALU.mult))
            link(dve.tensor_copy(mask_small[0:1], mask_f[:]))
            link(dve.tensor_tensor(mask_rest[32:33], mask_f[:], mask_small[0:1], ALU.subtract))
            link(dve.tensor_copy(mask_small[32:33], mask_rest[32:33]))
            dve.tensor_tensor(mask_small[64:65], mask_rest[32:33], mask_small[32:33],
                              ALU.subtract).then_inc(s["masksmall_ready"], 1)
            dve.wait_ge(s["expa_ready"], 1)
            dve.tensor_scalar(neg_a[:], exp_a[:], -1.0, None, ALU.mult).then_inc(s["nega_ready"], 1)
            dve.wait_ge(s["gexpneg_ready"], 1)
            link(dve.tensor_scalar(gate_s[:], gate_s[:], 1.0, None, ALU.add))
            dve.reciprocal(gates[:], gate_s[:]).then_inc(s["gates_ready"], 1)
            for b in range(B):
                dve.wait_ge(s["e_ready"], HV * (b + 1))
                dve.tensor_scalar(e_dt[:, b], e_dt[:, b], SOFTPLUS_CAP, None, ALU.min).then_inc(s["ecap_ready"], 1)
                dve.wait_ge(s["ecap_ready"], b + 1)
                link(dve.tensor_scalar(r_dt[:], e_dt[:, b], 1.0, -1.0, ALU.add, ALU.add))
                link(dve.tensor_tensor(r_dt[:], e_dt[:, b], r_dt[:], ALU.subtract))
                dve.wait_ge(s["log_ready"], b + 1)
                link(dve.tensor_tensor(r_dt[:], log_dt[:, b], r_dt[:], ALU.add))
                dve.tensor_scalar(delta[:, b], r_dt[:], DT_MIN, DT_MAX, ALU.max, ALU.min).then_inc(s["delta_ready"], 1)
                dve.wait_ge(s["delta_ready"], b + 1)
                link(dve.tensor_tensor(du[:, b], delta[:, b], uT[:, b], ALU.mult))

            dve.wait_ge(s["simrn_ready"], 1)
            dve.tensor_tensor(simn[:], sim, sim_rn[:], ALU.mult).then_inc(s["simn_ready"], 1)

            def scan_state(b, n, j):
                g = NS * b + n
                dve.wait_ge(s["b_psum"], g + 1)
                for h in range(HV):
                    if b or not isinstance(n, int) or n >= 1:
                        dve.wait_ge(s["scan_done"], 2 * g - 1 + h)
                    dve.tensor_tensor(bank(4 + h), du[:, b, h, :], bank(j % 2), ALU.mult).then_inc(s["dbu_done"], 1)
                for h in range(HV):
                    dve.wait_ge(s["dbu_done"], 2 * g + 1 + h)
                    dve.wait_ge(s["decay_ready"], 2 * g + 1 + h)
                    if h == 0 and (b or not isinstance(n, int) or n >= 2):
                        dve.wait_ge(s["prod_done"], g - 1)
                    dve.tensor_tensor_scan(states[:, j % 2, h, :], decay[:, j % 2, h, :], bank(4 + h), 0.0, ALU.mult,
                                           ALU.add).then_inc(s["scan_done"], 1)

            for b in range(B):
                if b == 0:
                    for n in range(U):
                        scan_state(0, n, n)
                with dve.Fori(1 if b == 0 else 0, NS // U) as i:
                    for j in range(U):
                        scan_state(b, i * U + j, j)
                dve.wait_ge(s["sum_done"], NS * (b + 1))
                if b:
                    dve.wait_ge(s["wout_psum"], 1)
                for h in range(HV):
                    dve.tensor_tensor(gT[:, h, :], zT[:, b, h, :], bank(6 + h), ALU.mult).then_inc(s["g_ready"], 1)
                dve.wait_ge(s["wout_psum"], b + 1)
                dve.tensor_tensor(x1p[:, b].rearrange("p k c -> p (k c)"), x[:, b].rearrange("p k c -> p (k c)"), bank(3),
                                  ALU.add).then_inc(s["x1p_ready"], 1)

            roots = [0]

            def layer_norm(dst, src, ready):
                for k in range(K):
                    last = dve.bn_stats(stats[:, k, :], src[:, k, :])
                link(last)
                for k in range(K):
                    last = dve.bn_aggr(mv[:, k, :], stats[:, k, :])
                link(last)
                dve.tensor_scalar(var_eps[:], mv[:, :, 1], LN_EPS, None, ALU.add).then_inc(s["var_ready"], 1)
                roots[0] += 1
                dve.wait_ge(s["rstd_ready"], roots[0])
                for k in range(K):
                    last = dve.tensor_scalar(dst[:, k, :], src[:, k, :], mv[:, k, 0:1], rstd[:, k:k + 1], ALU.subtract,
                                             ALU.mult)
                if ready is None:
                    link(last)
                else:
                    last.then_inc(s[ready], 1)

            for b in range(B):
                dve.wait_ge(s["x1p_ready"], b + 1)
                layer_norm(x1[:, b], x1p[:, b], "x1_ready")

            def x_softmax(i):
                b, k = divmod(i, K)
                dve.wait_ge(s["xs_psum"], i + 1)
                scores = ps[:, 4:7, :].rearrange("p a n -> p (a n)")[:, 0:FLAT].rearrange("p (h t) -> p h t", h=NH)
                if k == 0:
                    masked = xs_masked.rearrange("p (h t) -> p h t", h=NH)
                    link(dve.tensor_tensor(masked, scores, cst("xcausal").unsqueeze(1).to_broadcast([P, NH, S2]), ALU.add))
                    scores = masked
                link(dve.tensor_reduce(xs_max[:], scores, AX_X, ALU.max))
                if i >= 2:
                    dve.wait_ge(s["xpT_psum"], i - 1)
                dve.tensor_tensor(xp[:, i % 2, :].rearrange("p (h t) -> p h t", h=NH), scores,
                                  xs_max[:].unsqueeze(2).to_broadcast([P, NH, S2]), ALU.subtract).then_inc(s["xsub_done"], 1)

            def x_finish(i):
                b, k = divmod(i, K)
                dve.wait_ge(s["xav_psum"], i + 1)
                heads = ps[:, 3, 0:NH * HD1].rearrange("p (h d) -> p h d", h=NH)
                link(dve.reciprocal(xrec[:], heads[:, :, HD]))
                link(dve.tensor_tensor(xav[:].rearrange("p (h d) -> p h d", h=NH), heads[:, :, 0:HD],
                                       xrec[:].unsqueeze(2).to_broadcast([P, NH, HD]), ALU.mult))
                dve.tensor_tensor(x2p[:, b, k, :], xav[:], x1[:, b, k, :], ALU.add).then_inc(s["x2p_ready"], 1)

            def gate(n, b):
                m = 2 * n + b
                dve.wait_ge(s["logit_psum"], m + 1)
                got = ps[:, 7, 0:9 * K].rearrange("p (k e) -> p k e", k=K)
                dve.tensor_scalar(g_ss[:], got[:, :, E], 1e-24, None, ALU.max).then_inc(s["norm_ready"], 1)
                dve.wait_ge(s["rnorm_ready"], m + 1)
                link(dve.tensor_tensor(g_l0[:], got[:, :, 0:E], g_rn[:].unsqueeze(2).to_broadcast([P, K, E]), ALU.mult))
                dve.wait_ge(s["gates_ready"], 1)
                link(dve.tensor_tensor(g_l[:], g_l0[:], gates[:, n, :].unsqueeze(1).to_broadcast([P, K, E]), ALU.subtract))
                dve.tensor_scalar(g_act[:], g_l[:], 0.0, None, ALU.is_gt)
                link(dve.tensor_scalar(g_relu[:], g_l[:], 0.0, None, ALU.max))
                link(dve.tensor_reduce(g_max[:], g_relu[:], AX_X, ALU.max))
                dve.tensor_tensor(g_sh[:], g_relu[:], g_max[:].unsqueeze(2).to_broadcast([P, K, E]),
                                  ALU.subtract).then_inc(s["gshift_ready"], 1)
                other = g_l[:].unsqueeze(2).to_broadcast([P, K, E, E])
                own = g_l[:].unsqueeze(3).to_broadcast([P, K, E, E])
                dve.tensor_tensor(g_gt[:], other, own, ALU.is_gt)
                link(dve.tensor_tensor(g_eq[:], other, own, ALU.is_equal))
                link(dve.tensor_tensor(g_eqt[:].rearrange("p k i j -> p k (i j)"), g_eq[:].rearrange("p k i j -> p k (i j)"),
                                       cst("tri").unsqueeze(1).to_broadcast([P, K, E * E]), ALU.mult))
                link(dve.tensor_tensor(g_cmp[:], g_gt[:], g_eqt[:], ALU.add))
                link(dve.tensor_reduce(g_rank[:], g_cmp[:], AX_X, ALU.add))
                dve.tensor_scalar(g_top[:], g_rank[:], 1.5, None, ALU.is_lt)
                link(dve.tensor_scalar(g_idle[:], g_max[:], 0.0, None, ALU.is_le))
                link(dve.tensor_tensor(g_put[:], g_top[:], g_idle[:].unsqueeze(2).to_broadcast([P, K, E]), ALU.mult))
                link(dve.tensor_tensor(g_mask[:], g_act[:], g_put[:], ALU.max))
                dve.wait_ge(s["gexp_ready"], m + 1)
                link(dve.tensor_tensor(g_w[:], g_ex[:], g_mask[:], ALU.mult))
                link(dve.tensor_reduce(g_sum[:], g_w[:], AX_X, ALU.add))
                link(dve.reciprocal(g_rs[:], g_sum[:]))
                link(dve.tensor_tensor(g_rw[:], g_w[:], g_rs[:].unsqueeze(2).to_broadcast([P, K, E]), ALU.mult))
                if m:
                    dve.wait_ge(s["rwT_psum"], m)
                link(dve.tensor_copy(rw_parts[:, :, 0, :], g_rw[:]))
                link(dve.tensor_tensor(g_r1[:], g_rw[:], rw_parts[:, :, 0, :], ALU.subtract))
                link(dve.tensor_copy(rw_parts[:, :, 1, :], g_r1[:]))
                dve.tensor_tensor(rw_parts[:, :, 2, :], g_r1[:], rw_parts[:, :, 1, :],
                                  ALU.subtract).then_inc(s["rwparts_ready"], 1)

            def norms_ffn(b):
                dve.wait_ge(s["x2p_ready"], K * (b + 1))
                layer_norm(x2[:, b], x2p[:, b], None)
                layer_norm(nrm[:, b], x2[:, b], "nrm_ready")

            for i in range(K * B + 1):
                if i < K * B:
                    x_softmax(i)
                if i:
                    x_finish(i - 1)
                if i == K:
                    norms_ffn(0)
                if i == K + 2:
                    gate(0, 0)

            def weigh_qkv(b, e):
                g = E * b + e
                dve.wait_ge(s["rwb_psum"], g + 1)
                dve.wait_ge(s["nT_ready"], b + 1)
                if g >= 2:
                    dve.wait_ge(s["xe_used"], g - 1)
                dve.tensor_tensor(xe[:, g % 2, :], nT[:, b, :], bank(2 + g % 2), ALU.mult).then_inc(s["xe_ready"], 1)

            for e in range(2):
                weigh_qkv(0, e)
            norms_ffn(1)
            for e in range(2, 5):
                weigh_qkv(0, e)
            gate(0, 1)
            for e in range(5, E):
                weigh_qkv(0, e)
            for e in range(E):
                weigh_qkv(1, e)

            def a_rowmax(b, i):
                m = K * b + i
                dve.wait_ge(s["as_psum"], m + 1)
                link(dve.tensor_reduce(a_max[:, i:i + 1], ps[:, i, 0:P * (i + 1)], AX_X, ALU.max))
                dve.tensor_scalar(a_nmax[:, i:i + 1], a_max[:, i:i + 1], -SCALE_A, None, ALU.mult).then_inc(s["amax_ready"], 1)

            def a_normalise(b, i):
                m = K * b + i
                dve.wait_ge(s["aexp_done"], m + 1)
                link(dve.reciprocal(a_rec[:, i:i + 1], a_sum[:, i:i + 1]))
                w = P * (i + 1)
                dve.tensor_scalar(ap_[:, i, 0:w], ap_[:, i, 0:w], a_rec[:, i:i + 1], None, ALU.mult).then_inc(s["ap_ready"], 1)

            for i in range(K):
                a_rowmax(0, i)
            for i in range(K):
                a_normalise(0, i)
            for i in range(K):
                a_rowmax(1, i)
            for i in range(K):
                a_normalise(1, i)

            def weigh_o(b, e):
                g = E * b + e
                dve.wait_ge(s["rwo_psum"], g + 1)
                dve.wait_ge(s["att_ready"], b + 1)
                if g >= 2:
                    dve.wait_ge(s["oe_used"], g - 1)
                else:
                    dve.wait_ge(s["xe_used"], E * B)
                dve.tensor_tensor(xe[:, g % 2, :], attnT[:, b, :], bank(2 + g % 2), ALU.mult).then_inc(s["oe_ready"], 1)

            def residual(b):
                dve.wait_ge(s["oe_used"], E * (b + 1))
                dve.tensor_tensor(hs[:, b].rearrange("p k c -> p (k c)"), x2[:, b].rearrange("p k c -> p (k c)"), bank(4 + b),
                                  ALU.add).then_inc(s["hs_ready"], 1)
                dve.wait_ge(s["hs_ready"], b + 1)
                dve.tensor_tensor(hx[:, b], hs[:, b], x2[:, b], ALU.add)
                layer_norm(nrm[:, b], hs[:, b], "nrm_ready")

            for e in range(E):
                weigh_o(0, e)
            weigh_o(1, 0)
            residual(0)
            for e in range(1, E):
                weigh_o(1, e)
            gate(1, 0)

            def weigh_moe(b, e):
                g = E * b + e
                dve.wait_ge(s["rwm_psum"], g + 1)
                dve.wait_ge(s["inter_ready"], g + 1)
                if g >= 2:
                    dve.wait_ge(s["ge_used"], g - 1)
                dve.tensor_tensor(scaled[:, g % 2, :], inter[:, g % 2, :], bank(g % 2), ALU.mult).then_inc(s["ge_ready"], 1)

            def last_norm(b):
                dve.wait_ge(s["ge_used"], E * (b + 1))
                link(dve.tensor_tensor(x3p[:, b].rearrange("p k c -> p (k c)"), hx[:, b].rearrange("p k c -> p (k c)"),
                                       bank(4 + b), ALU.add))
                layer_norm(x3[:, b], x3p[:, b], "x3_ready")

            weigh_moe(0, 0)
            residual(1)
            for e in range(1, 4):
                weigh_moe(0, e)
            gate(1, 1)
            for e in range(4, E):
                weigh_moe(0, e)
            weigh_moe(1, 0)
            last_norm(0)
            for e in range(1, E):
                weigh_moe(1, e)
            last_norm(1)

        @block.scalar
        def _(act):
            for b in range(B):
                for h in range(HV):
                    act.wait_ge(s["win_psum"], 2 * HV * b + HV + h + 1)
                    act.activation(zT[:, b, h, :], bank(2 + HV + h), ACT.Silu).then_inc(s["z_ready"], 1)
            act.wait_ge(ld["conv"], 32)
            for b in range(B):
                for g in range(HV):
                    act.wait_ge(s["conv_psum"], HV * b + g + 1)
                    act.activation(uT[:, b, g, :], bank(6 + g), ACT.Silu, bias=conv_b[:, g:g + 1]).then_inc(s["u_ready"], 1)
            act.activation(exp_a[:], a_log, ACT.Exp).then_inc(s["expa_ready"], 1)
            act.activation(gate_s[:], gates_in, ACT.Exp, scale=-1.0).then_inc(s["gexpneg_ready"], 1)
            for b in range(B):
                for h in range(HV):
                    act.wait_ge(s["wdt_psum"], HV * b + h + 1)
                    act.activation(e_dt[:, b, h, :], bank(2 + HV * b + h), ACT.Exp, bias=b_dt[:, h:h + 1]).then_inc(s["e_ready"], 1)
            for b in range(B):
                act.wait_ge(s["ecap_ready"], b + 1)
                act.activation(log_dt[:, b], e_dt[:, b], ACT.Ln, bias=1.0).then_inc(s["log_ready"], 1)
            for b in range(B):
                act.wait_ge(s["ctxT_psum"], B)
                act.activation(ctxT[:, b, :], ps[:, 6, P * b:P * b + S2], ACT.Copy).then_inc(s["ctxT_ready"], 1)
            for b in range(B):
                act.wait_ge(s["kv_psum"], B)
                act.activation(kT[:, b, :], ps[:, 7, P * b:P * b + S2], ACT.Copy).then_inc(s["kv_ready"], 1)
                act.activation(v_sb[:, b, :], ps[0:S2, 7, 256 + P * b:256 + P * b + P], ACT.Copy).then_inc(s["kv_ready"], 1)
            for b in range(B):
                act.wait_ge(s["vrep_psum"], b + 1)
                flat = v_rep[:, b].rearrange("p j c -> p (j c)")
                act.activation(flat[:, 0:1024], ps[:, 0:2, :].rearrange("p a n -> p (a n)"), ACT.Copy)
                act.activation(flat[:, 1024:1280], ps[:, 6, 0:256], ACT.Copy).then_inc(s["vrep_ready"], 1)

            def scan_state(b, n, j):
                g = NS * b + n
                if b or not isinstance(n, int) or n >= 2:
                    act.wait_ge(s["scan_done"], 2 * (g - 1))
                for h in range(HV):
                    if isinstance(n, int):
                        scale = neg_a[:, h, n:n + 1]
                    else:
                        scale = neg_a[:, h, :][:, bass.ds(n, 1)]
                    act.activation(decay[:, j % 2, h, 1:], delta[:, b, h, 1:], ACT.Exp, scale=scale).then_inc(s["decay_ready"], 1)
                act.wait_ge(s["c_psum"], g + 1)
                if b or not isinstance(n, int) or n >= 2:
                    act.wait_ge(s["prod_done"], g - 1)
                act.activation(c_rep[:, j % 2, :], bank(2), ACT.Copy).then_inc(s["crep_ready"], 1)

            act.wait_ge(s["nega_ready"], 1)
            act.wait_ge(s["fills_ready"], 6)
            for b in range(B):
                act.wait_ge(s["delta_ready"], b + 1)
                if b == 0:
                    for n in range(U):
                        scan_state(0, n, n)
                with act.Fori(1 if b == 0 else 0, NS // U) as i:
                    for j in range(U):
                        scan_state(b, i * U + j, j)

            for b in range(B):
                act.wait_ge(s["x1T_psum"], b + 1)
                act.activation(x1T[:, b, :], bank(b), ACT.Copy).then_inc(s["x1T_ready"], 1)
            for b in range(B):
                act.wait_ge(s["q_psum"], b + 1)
                act.activation(qT[:, b, :], bank(2 + b), ACT.Copy, scale=SCALE_X).then_inc(s["qT_ready"], 1)

            def x_exp(i):
                act.wait_ge(s["xsub_done"], i + 1)
                act.activation(xp[:, i % 2, :], xp[:, i % 2, :], ACT.Exp).then_inc(s["xexp_done"], 1)

            def x_take(i):
                act.wait_ge(s["xpT_psum"], i + 1)
                if i:
                    act.wait_ge(s["xav_psum"], i)
                flat = xpT.rearrange("p j t -> p (j t)")
                full = P * (CH - 1)
                rows = heads_of(CH - 1)[2]
                act.activation(flat[:, 0:full], ps[:, 0:3, :].rearrange("p a n -> p (a n)")[:, 0:full], ACT.Copy)
                act.activation(flat[0:rows, full:full + P], ps[0:rows, 2, P:2 * P], ACT.Copy).then_inc(s["xpT_ready"], 1)

            def n_take(n, b):
                m = 2 * n + b
                act.wait_ge(s["nT_psum"], m + 1)
                act.activation(nT[:, b, :], bank(7), ACT.Identity, scale=ln_w[:, n:n + 1],
                               bias=ln_b[:, n:n + 1]).then_inc(s["nT_ready"], 1)
                act.wait_ge(s["nT_ready"], m + 1)
                act.activation(nsq[:, b, :], nT[:, b, :], ACT.Square).then_inc(s["nsq_ready"], 1)

            def gate_exp(m):
                act.wait_ge(s["gshift_ready"], m + 1)
                act.activation(g_ex[:], g_sh[:], ACT.Exp).then_inc(s["gexp_ready"], 1)

            def weights_take(n, b):
                act.wait_ge(s["rwT_psum"], 2 * n + b + 1)
                act.activation(rwT[:, n, b, :], ps[0:3 * E, 7, :].bitcast(BF16)[:, 0:T], ACT.Copy).then_inc(s["rwT_ready"], 1)

            for i in range(K * B + 1):
                if i < K * B:
                    x_exp(i)
                if i:
                    x_take(i - 1)
                if i == K + 1:
                    n_take(0, 0)
                if i == K + 2:
                    gate_exp(0)
                if i == K + 3:
                    weights_take(0, 0)
            n_take(0, 1)
            gate_exp(1)
            weights_take(0, 1)

            def take_qkv(b):
                act.wait_ge(s["xe_used"], E * (b + 1))
                act.activation(aqT[:, b, :], bank(4), ACT.Copy).then_inc(s["qkv_ready"], 1)
                act.activation(akT[:, b, :], bank(5), ACT.Copy).then_inc(s["qkv_ready"], 1)
                act.activation(av[:, b].rearrange("p k c -> p (k c)"), bank(6), ACT.Copy).then_inc(s["qkv_ready"], 1)

            for b in range(B):
                take_qkv(b)

            def a_exp(b, i):
                m = K * b + i
                act.wait_ge(s["amax_ready"], m + 1)
                if b:
                    act.wait_ge(s["apT_psum"], i + 1)
                w = P * (i + 1)
                act.activation(ap_[:, i, 0:w], ps[:, i, 0:w], ACT.Exp, bias=a_nmax[:, i:i + 1], scale=SCALE_A,
                               accum_out=a_sum[:, i:i + 1]).then_inc(s["aexp_done"], 1)

            def a_take(b):
                act.wait_ge(s["apT_psum"], K * (b + 1))
                if b:
                    act.wait_ge(s["att_psum"], 1)
                act.activation(apT[:, 0, :], bank(4), ACT.Copy).then_inc(s["apT_ready"], 1)
                act.activation(apT[:, 1, 0:T - P], bank(5)[:, 0:T - P], ACT.Copy).then_inc(s["apT_ready"], 1)
                act.activation(apT[:, 2, 0:2 * P], bank(6)[:, 0:2 * P], ACT.Copy)
                act.activation(apT[:, 3, 0:P], bank(6)[:, 2 * P:3 * P], ACT.Copy).then_inc(s["apT_ready"], 1)

            def att_take(b):
                act.wait_ge(s["att_psum"], b + 1)
                act.activation(attnT[:, b, :], bank(7), ACT.Copy).then_inc(s["att_ready"], 1)

            for i in range(K):
                a_exp(0, i)
            a_take(0)
            for i in range(K):
                a_exp(1, i)
            att_take(0)
            a_take(1)
            att_take(1)

            n_take(1, 0)
            gate_exp(2)
            weights_take(1, 0)

            def moe_gelu(b, e):
                g = E * b + e
                act.wait_ge(s["h_psum"], g + 1)
                if g >= 2:
                    act.wait_ge(s["ge_ready"], g - 1)
                act.activation(inter[:, g % 2, :], bank(2 + g % 2), ACT.Gelu).then_inc(s["inter_ready"], 1)

            for e in range(3):
                moe_gelu(0, e)
            n_take(1, 1)
            moe_gelu(0, 3)
            moe_gelu(0, 4)
            gate_exp(3)
            moe_gelu(0, 5)
            moe_gelu(0, 6)
            moe_gelu(0, 7)
            weights_take(1, 1)
            for e in range(E):
                moe_gelu(1, e)

        @block.gpsimd
        def _(pool):
            pool.memset(xsT[:, :, :, 0:TAPS - 1], 0.0).then_inc(s["fills_ready"], 1)
            pool.memset(decay[:, :, :, 0:1], 0.0).then_inc(s["fills_ready"], 1)
            pool.memset(ones[:], 1.0).then_inc(s["fills_ready"], 1)
            pool.memset(ones_bf[:], 1.0).then_inc(s["fills_ready"], 1)
            pool.memset(minus_half[:], -0.5).then_inc(s["fills_ready"], 1)
            pool.memset(mask_parts[:], 0.0).then_inc(s["fills_ready"], 1)
            pool.wait_ge(ld["masks"], 32)
            pool.wait_ge(ld["x"], 48)
            pool.tensor_copy(sel32[:], cst("sel32", 96).unsqueeze(2).to_broadcast([96, 32, P])).then_inc(s["sel_ready"], 1)
            pool.tensor_copy(sel8[:], cst("sel8", 3 * E).unsqueeze(2).to_broadcast([3 * E, E, P])).then_inc(s["sel_ready"], 1)
            pool.tensor_copy(causal_bf[:], cst("causal")).then_inc(s["sel_ready"], 1)
            pool.tensor_copy(ident_bf[:], ident).then_inc(s["sel_ready"], 1)
            pool.wait_ge(s["simss_ready"], 1)
            pool.wait_ge(s["fills_ready"], 6)
            pool.tensor_tensor(sim_rn[:].rearrange("p n e -> p (n e)"), sim_ss[:].rearrange("p n e -> p (n e)"),
                               minus_half[:], ALU.pow).then_inc(s["simrn_ready"], 1)
            for b in range(B):
                pool.wait_ge(s["kv_ready"], 2 * b + 1)
                pool.tensor_tensor(k_diag[:, b, :].rearrange("p (h t) -> p h t", h=NH),
                                   kT[:, b, :].unsqueeze(1).to_broadcast([P, NH, S2]),
                                   cst("headof").unsqueeze(2).to_broadcast([P, NH, S2]),
                                   ALU.mult).then_inc(s["kdiag_ready"], 1)
                pool.wait_ge(s["vrep_ready"], b + 1)
                wide = v_diag[:, b].rearrange("p j (h d) -> p (j h) d", d=HD1)
                pool.tensor_tensor(wide[:, :, 0:HD], v_rep[:, b].rearrange("p j (h d) -> p (j h) d", d=HD),
                                   cst("pairhead").unsqueeze(2).to_broadcast([P, CH * NH, HD]),
                                   ALU.mult).then_inc(s["vdiag_ready"], 1)
                pool.tensor_copy(wide[:, :, HD], cst("pairhead")).then_inc(s["vdiag_ready"], 1)

            def scan_state(b, n, j):
                g = NS * b + n
                pool.wait_ge(s["scan_done"], 2 * g + 2)
                pool.wait_ge(s["crep_ready"], g + 1)
                if b or not isinstance(n, int) or n >= 2:
                    pool.wait_ge(s["sum_done"], g - 1)
                pool.tensor_tensor(prod[:, j % 2], states[:, j % 2],
                                   c_rep[:, j % 2, :].unsqueeze(1).to_broadcast([P, HV, T]),
                                   ALU.mult).then_inc(s["prod_done"], 1)

            for b in range(B):
                if b == 0:
                    for n in range(U):
                        scan_state(0, n, n)
                with pool.Fori(1 if b == 0 else 0, NS // U) as i:
                    for j in range(U):
                        scan_state(b, i * U + j, j)

            norms, gates_done = [0], [0]

            def norm_root():
                norms[0] += 1
                pool.wait_ge(s["var_ready"], norms[0])
                pool.tensor_tensor(rstd[:], var_eps[:], minus_half[:, 0:K], ALU.pow).then_inc(s["rstd_ready"], 1)

            def gate_root():
                gates_done[0] += 1
                pool.wait_ge(s["norm_ready"], gates_done[0])
                pool.tensor_tensor(g_rn[:], g_ss[:], minus_half[:, 0:K], ALU.pow).then_inc(s["rnorm_ready"], 1)

            norm_root()
            norm_root()
            for b in range(B):
                norm_root()
                norm_root()
                gate_root()
            for b in range(B):
                norm_root()
                gate_root()
            norm_root()
            norm_root()

        return nc


_WHOLE = ["x", "ctx_1024", "mask_BxS2_ik0", "L0_attn_W_in", "L0_attn_conv_k", "L0_attn_W_x", "L0_attn_W_dt", "L0_attn_W_out",
          "L0_xattn_Wq", "L0_xattn_Wk", "L0_xattn_Wv", "L0_ffn_q_proj", "L0_ffn_k_proj", "L0_ffn_v_proj",
          "L0_ffn_o_proj", "L0_ffn_w1", "L0_ffn_w2"]


def small_columns(inputs):
    def halves(name, n=HV):
        return np.asarray(inputs[name]).reshape(n, P).T

    a_log = np.asarray(inputs["L0_attn_A_log"]).reshape(HV, P, NS).transpose(1, 0, 2).reshape(P, HV * NS)
    columns = [halves("L0_attn_conv_b"), halves("L0_attn_b_dt"), halves("L0_attn_D"),
               halves("L0_ffn_ln1_w", 1), halves("L0_ffn_ln2_w", 1), halves("L0_ffn_ln1_b", 1), halves("L0_ffn_ln2_b", 1),
               a_log, np.asarray(inputs["L0_ffn_smha_sim"]), np.asarray(inputs["L0_ffn_moe_sim"])]
    columns += [np.broadcast_to(np.asarray(inputs[n]), (P, E)) for n in ("L0_ffn_smha_gates", "L0_ffn_moe_gates")]
    return np.ascontiguousarray(np.concatenate(columns, axis=1))


def kernel(**inputs):
    import concourse.bacc as bacc
    from concourse.bass_utils import run_bass_kernel_spmd

    nc = bacc.Bacc("TRN2", target_bir_lowering=False, num_devices=1)
    arrays, aps = {}, {}
    for name in _WHOLE:
        value = np.ascontiguousarray(inputs[name])
        arrays[f"in_{name}"] = value
        aps[name] = nc.dram_tensor(f"in_{name}", value.shape, mybir.dt.from_np(value.dtype), kind="ExternalInput").ap()
    arrays["in_consts"] = shape_constants()
    arrays["in_small"] = small_columns(inputs)
    aps["small"] = nc.dram_tensor("in_small", [P, SMALL_COLS], F32, kind="ExternalInput").ap()
    aps["consts"] = nc.dram_tensor("in_consts", [P, CONST_COLS], F32, kind="ExternalInput").ap()
    out = nc.dram_tensor("out_y", [B, T, C], F32, kind="ExternalOutput").ap()
    decoder_layer(nc, aps, out)
    got = run_bass_kernel_spmd(nc, [arrays], core_ids=[0])
    return got.results[0]["out_y"]
```

```python
from contextlib import ExitStack

import numpy as np

import concourse.bass as bass
from concourse import mybir

F32 = mybir.dt.float32
BF16 = mybir.dt.bfloat16
I32 = mybir.dt.int32
ALU = mybir.AluOpType
ACT = mybir.ActivationFunctionType
AX_X = mybir.AxisListType.X

P = 128
B, T, C = 2, 512, 128
K = T // P
DI = 256
HV = DI // P
NS = 16
DTR = 64
TAPS = 4
NH, HD = 16, 8
S2 = 77
FLAT = NH * S2
CH = -(-FLAT // P)
HD1 = HD + 1
HC = 3
E = 8
NEG = 1.0e9
LN_EPS = 1e-5
DT_MIN, DT_MAX = 0.001, 0.1
SOFTPLUS_CAP = 0.2
U = 4

WIDTHS = {"ident": P, "causal": P, "sel32": 32, "sel8": E, "tri": E * E, "headof": NH, "xcausal": S2,
          "pairhead": CH * HC}
AT = {}
_at = 0
for _name, _width in WIDTHS.items():
    AT[_name] = (_at, _at + _width)
    _at += _width
PAIR_COLS = CH * P
CONST_COLS = _at + PAIR_COLS
AT["pairtok"] = (_at, CONST_COLS)
CONST_FIRST = AT["causal"][0]




def chunk(j):
    return min(P * j // S2, NH - HC), min(P, FLAT - P * j)


SMALL_COLS = 3 * HV + 4 + HV * NS + 4 * E


def shape_constants():
    c = np.zeros((P, CONST_COLS), np.float32)
    p = np.arange(P)[:, None]

    def put(name, values):
        c[:values.shape[0], AT[name][0]:AT[name][1]] = values

    put("ident", (p == np.arange(P)).astype(np.float32))
    put("causal", np.where(np.arange(P) > p, -1e30, 0.0).astype(np.float32))
    put("sel32", (p % 32 == np.arange(32)).astype(np.float32))
    put("sel8", ((p % E == np.arange(E)) & (p < 3 * E)).astype(np.float32))
    i, j = np.arange(E * E) // E, np.arange(E * E) % E
    put("tri", np.broadcast_to((j < i).astype(np.float32), (P, E * E)))
    put("headof", (p // HD == np.arange(NH)).astype(np.float32))
    put("xcausal", np.where(np.arange(S2) > p, -NEG, 0.0).astype(np.float32))
    flat = P * np.arange(CH)[None, :] + p
    first = np.array([chunk(j)[0] for j in range(CH)])
    put("pairhead", ((flat // S2 - first)[:, :, None] == np.arange(HC)).astype(np.float32).reshape(P, CH * HC))
    f = np.arange(CH * P)
    put("pairtok", ((f % S2 == np.arange(S2)[:, None]) & (f < FLAT)).astype(np.float32))
    return c


def decoder_layer(nc, a, out):
    with ExitStack() as ctx:
        def sb(name, shape, dt=F32):
            return ctx.enter_context(nc.sbuf_tensor(name, shape, dt))

        def sem(name):
            return ctx.enter_context(nc.semaphore(name))

        ps = ctx.enter_context(nc.psum_tensor("ps", [P, 8, 512], F32))

        def bank(i, rows=P):
            return ps[0:rows, i, :]

        const = sb("const", [P, CONST_COLS - PAIR_COLS])

        def cst(name, rows=P):
            return const[0:rows, AT[name][0]:AT[name][1]]

        ident = cst("ident")
        ident_bf = sb("ident_bf", [P, P], BF16)
        causal_bf = sb("causal_bf", [P, P], BF16)
        sel32 = sb("sel32", [96, 32, P], BF16)
        sel8 = sb("sel8", [3 * E, E, P], BF16)
        ones = sb("ones", [P, P])
        ones_bf = sb("ones_bf", [96, P], BF16)
        minus_half = sb("minus_half", [P, 2 * E])
        w_in = sb("w_in", [P, 2 * DI])
        conv_k = sb("conv_k", [P, TAPS, DI])
        w_x = sb("w_x", [P, HV, DTR + 2 * NS])
        w_dt = sb("w_dt", [DTR, DI])
        w_out = sb("w_out", [P, HV, C])
        small = sb("small", [P, SMALL_COLS])
        conv_b, b_dt, skip_d = (small[:, i * HV:(i + 1) * HV] for i in range(3))
        ln_w, ln_b = small[:, 6:8], small[:, 8:10]
        a_log = small[:, 10:42].rearrange("p (h n) -> p h n", h=HV)
        sim = small[:, 42:58].rearrange("p (n e) -> p n e", n=2)
        gates_in = small[:, 58:74].rearrange("p (n e) -> p n e", n=2)
        neg_a = sb("neg_a", [P, HV, NS])
        exp_a = sb("exp_a", [P, HV, NS])
        diag_d = sb("diag_d", [P, HV, P])
        wq = sb("wq", [P, P])
        wk = sb("wk", [P, P])
        wv = sb("wv", [P, P])
        sim_sq = sb("sim_sq", [P, 2, E])
        sim_rn = sb("sim_rn", [P, 2, E])
        sim_ss = sb("sim_ss", [P, 2, E])
        simn = sb("simn", [P, 2, E])
        gates = sb("gates", [P, 2, E])
        gate_s = sb("gate_s", [P, 2, E])
        w_q = sb("w_q", [P, E, P])
        w_k = sb("w_k", [P, E, P])
        w_v = sb("w_v", [P, E, P])
        w_o = sb("w_o", [P, E, P])
        w_1 = sb("w_1", [P, E, P])
        w_2 = sb("w_2", [P, E, P])

        x = sb("x", [P, B, K, C])
        xT = sb("xT", [P, B, T])
        xsT = sb("xsT", [P, B, HV, TAPS - 1 + T])
        zT = sb("zT", [P, B, HV, T])
        uT = sb("uT", [P, B, HV, T])
        bc_parts = sb("bc_parts", [96, B, T], BF16)
        e_dt = sb("e_dt", [P, B, HV, T])
        log_dt = sb("log_dt", [P, B, HV, T])
        r_dt = sb("r_dt", [P, HV, T])
        delta = sb("delta", [P, B, HV, T])
        du = sb("du", [P, B, HV, T])
        decay = sb("decay", [P, 2, HV, T])
        states = sb("states", [P, 2, HV, T])
        c_rep = sb("c_rep", [P, 2, T])
        prod = sb("prod", [P, 2, HV, T])
        x1 = sb("x1", [P, B, K, C])
        ctx_sb = sb("ctx_sb", [S2, B, C])
        ctxT = sb("ctxT", [P, B, S2])
        kT = sb("kT", [P, B, S2])
        v_sb = sb("v_sb", [S2, B, P])
        xp = sb("xp", [P, 2, FLAT])
        xpT_odd = sb("xpT_odd", [P, CH, P])
        k_diag = sb("k_diag", [P, B, FLAT])
        v_diag = sb("v_diag", [P, B, CH, HC * HD1])
        mask_i = sb("mask_i", [1, B, S2], I32)
        mask_f = sb("mask_f", [1, B, S2])
        mask_rest = sb("mask_rest", [64, B, S2])
        mask_small = sb("mask_small", [96, B, S2], BF16)
        mask_parts = sb("mask_parts", [96, B, FLAT], BF16)
        xs_max = sb("xs_max", [P, NH])
        xrec = sb("xrec", [P, NH])
        xav = sb("xav", [P, P])
        stats = sb("stats", [P, K, 6])
        mv = sb("mv", [P, K, 2])
        var_eps = sb("var_eps", [P, K])
        rstd = sb("rstd", [P, K])
        g_ss = sb("g_ss", [P, K])
        g_rn = sb("g_rn", [P, K])
        g_l0 = sb("g_l0", [P, K, E])
        g_l = sb("g_l", [P, K, E])
        g_gt = sb("g_gt", [P, K, E, E])
        g_eq = sb("g_eq", [P, K, E, E])
        g_eqt = sb("g_eqt", [P, K, E, E])
        g_cmp = sb("g_cmp", [P, K, E, E])
        g_rank = sb("g_rank", [P, K, E])
        g_top = sb("g_top", [P, K, E])
        g_relu = sb("g_relu", [P, K, E])
        g_act = sb("g_act", [P, K, E])
        g_max = sb("g_max", [P, K])
        g_idle = sb("g_idle", [P, K])
        g_put = sb("g_put", [P, K, E])
        g_mask = sb("g_mask", [P, K, E])
        g_sh = sb("g_sh", [P, K, E])
        g_ex = sb("g_ex", [P, K, E])
        g_w = sb("g_w", [P, K, E])
        g_sum = sb("g_sum", [P, K])
        g_rs = sb("g_rs", [P, K])
        g_rw = sb("g_rw", [P, K, E])
        g_r1 = sb("g_r1", [P, K, E])
        rw_parts = sb("rw_parts", [P, K, 3, E], BF16)
        rwT = sb("rwT", [3 * E, 2, B, T], BF16)
        a_max = sb("a_max", [P, K])
        a_nmax = sb("a_nmax", [P, K])
        a_sum = sb("a_sum", [P, K])
        a_rec = sb("a_rec", [P, K])

        ap_ = e_dt[:].rearrange("p b h t -> p (b h) t")
        apT = log_dt[:].rearrange("p b h t -> p (b h) t")
        inter = states[:].rearrange("p i h t -> p (i h) t")
        scaled = c_rep
        xe = prod[:].rearrange("p i h t -> p (i h) t")
        hs = du[:, 0].rearrange("p h (k c) -> p h k c", c=C)
        hx = du[:, 1].rearrange("p h (k c) -> p h k c", c=C)
        x3p = delta[:, 0].rearrange("p h (k c) -> p h k c", c=C)
        x3 = delta[:, 1].rearrange("p h (k c) -> p h k c", c=C)
        x1T = xT
        gT = r_dt
        aqT = zT[:, 0]
        akT = zT[:, 1]
        av = uT[:, 0].rearrange("p h (k c) -> p h k c", c=C)
        attnT = uT[:, 1]
        nT = decay[:, 0]
        nsq = decay[:, 1]
        x1p = xsT[:].rearrange("p b h t -> p (b h t)")[:, 0:B * T].rearrange("p (b k c) -> p b k c", b=B, c=C)
        x2p = xsT[:].rearrange("p b h t -> p (b h t)")[:, B * T:2 * B * T].rearrange("p (b k c) -> p b k c", b=B, c=C)
        xs_masked = delta[:].rearrange("p b h t -> p (b h t)")[:, 0:FLAT]
        xpT = [du[:].rearrange("p b h t -> p (b h t)")[:, 0:CH * P].rearrange("p (j t) -> p j t", t=P), xpT_odd[:]]
        x2 = x
        dt_raw = prod[0:DTR, 0]
        bc_rest = c_rep[:, 0, :]
        nrm = conv_k[:].rearrange("p a o -> p (a o)").rearrange("p (b k c) -> p b k c", b=B, c=C)
        pairtok = states[0:S2].rearrange("p i h t -> p (i h t)")[:, 0:PAIR_COLS]
        qT = c_rep
        SCALE_X = float(HD) ** -0.5
        SCALE_A = float(P) ** -0.5

        H_BANKS = (2, 3, 6)

        def a_bank(b, i):
            return (0, 1, 0, 1)[i] if b == 0 else (0, 1, 5, 6)[i]

        ld = {n: sem("ld_" + n) for n in ("x", "win", "conv", "small", "ctx", "masks", "qkv", "o", "moe")}
        s = {n: sem(n) for n in (
            "xT_psum", "xT_ready", "win_psum", "xs_ready", "z_ready", "conv_psum", "u_ready", "dbc_psum", "dtraw_ready",
            "bc_ready", "wdt_psum", "e_ready", "ecap_ready", "log_ready", "delta_ready", "fills_ready", "sel_ready",
            "diag_ready", "nega_ready", "b_psum", "c_psum", "dbu_done", "decay_ready", "scan_done", "crep_ready",
            "prod_done", "sum_done", "g_ready", "wout_psum", "x1p_ready", "dve_chain", "var_ready",
            "rstd_ready", "x1_ready", "x1T_psum", "x1T_ready", "q_psum", "qT_ready", "ctxT_psum", "ctxT_ready",
            "kv_psum", "kv_ready", "vrep_psum", "kdiag_ready", "vdiag_ready", "masks_ready", "masksmall_ready",
            "xs_psum", "xsub_done", "xexp_done", "xpT_psum", "xpT_ready", "xav_psum", "x2p_ready",
            "nrm_ready", "nT_psum", "nT_ready", "nsq_ready", "logit_psum", "norm_ready", "rnorm_ready", "gshift_ready",
            "gexp_ready", "rwparts_ready", "rwT_psum", "rwT_ready", "simsq_ready", "simss_psum", "simss_ready",
            "simrn_ready", "simn_ready", "gexpneg_ready", "gates_ready", "rwb_psum", "xe_ready", "xe_used", 
            "qkv_ready", "as_psum", "amax_ready", "aexp_done", "ap_ready", "apT_psum", "apT_ready", "att_psum",
            "att_ready", "rwo_psum", "oe_ready", "oe_used", "hs_ready", "h_psum", "inter_ready", "rwm_psum",
            "ge_ready", "ge_used", "hx_ready", "moe_psum", "x3_ready", "stored", "expa_ready")}

        block = ctx.enter_context(nc.Block())

        @block.sync
        def _(sp):
            cc = a["consts"]
            sp.dma_start(x[:, 0], a["x"][0].rearrange("(k p) c -> p k c", p=P)).then_inc(ld["x"], 16)
            sp.dma_start(const[:, 0:CONST_FIRST], cc[:, 0:CONST_FIRST]).then_inc(ld["x"], 16)
            sp.dma_start(x[:, 1], a["x"][1].rearrange("(k p) c -> p k c", p=P)).then_inc(ld["x"], 16)
            sp.dma_start(w_in[:], a["L0_attn_W_in"]).then_inc(ld["win"], 16)
            sp.dma_start(conv_k[:], a["L0_attn_conv_k"].rearrange("k i o -> i k o")).then_inc(ld["conv"], 16)
            sp.dma_start(small[:], a["small"]).then_inc(ld["conv"], 16)
            sp.dma_start(w_x[:], a["L0_attn_W_x"].rearrange("(h p) n -> p h n", p=P)).then_inc(ld["small"], 16)
            sp.dma_start(w_dt[:], a["L0_attn_W_dt"]).then_inc(ld["small"], 16)
            sp.dma_start(w_out[:], a["L0_attn_W_out"].rearrange("(h p) n -> p h n", p=P)).then_inc(ld["small"], 16)
            sp.dma_start(const[:, CONST_FIRST:], cc[:, CONST_FIRST:CONST_COLS - PAIR_COLS]).then_inc(ld["masks"], 16)
            sp.dma_start(pairtok, cc[0:S2, CONST_COLS - PAIR_COLS:]).then_inc(ld["ctx"], 16)
            sp.dma_start(mask_i[:], a["mask_BxS2_ik0"].rearrange("(a b) n -> a b n", a=1)).then_inc(ld["masks"], 16)
            sp.dma_start(ctx_sb[:], a["ctx_1024"].rearrange("b n c -> n b c")).then_inc(ld["ctx"], 16)
            for dst, name in ((wq, "Wq"), (wk, "Wk"), (wv, "Wv")):
                sp.dma_start(dst[:], a["L0_xattn_" + name]).then_inc(ld["ctx"], 16)
            for dst, name, n in ((w_q, "q_proj", "qkv"), (w_k, "k_proj", "qkv"), (w_v, "v_proj", "qkv"),
                                 (w_o, "o_proj", "o"), (w_1, "w1", "moe"), (w_2, "w2", "moe")):
                sp.dma_start(dst[:], a["L0_ffn_" + name].rearrange("e i o -> i e o")).then_inc(ld[n], 16)
            sp.wait_ge(s["masksmall_ready"], 1)
            sp.wait_ge(s["fills_ready"], 6)
            for part in range(0, 96, 32):
                for b in range(B):
                    sp.dma_start(mask_parts[part:part + 1, b, :].rearrange("p (h t) -> p h t", h=NH),
                                 mask_small[part:part + 1, b, :].unsqueeze(1).to_broadcast([1, NH, S2])
                                 ).then_inc(s["masks_ready"], 16)
            for b in range(B):
                sp.wait_ge(s["x3_ready"], b + 1)
                sp.dma_start(out[b].rearrange("(k p) c -> p k c", p=P), x3[:, b]).then_inc(s["stored"], 16)
            sp.wait_ge(s["stored"], 16 * B)

        @block.tensor
        def _(pe):
            def transposes(dst, src):
                for k in range(K):
                    last = pe.transpose(dst[:, P * k:P * k + P], src[:, k, :], ident)
                return last

            for b in range(B):
                pe.wait_ge(ld["x"], 48)
                transposes(bank(b), x[:, b]).then_inc(s["xT_psum"], 1)
            pe.wait_ge(ld["ctx"], 80)

            def context_t():
                for b in range(B):
                    pe.transpose(ps[:, 6 + b, 0:S2], ctx_sb[:, b, :], ident[0:S2, 0:S2]).then_inc(s["ctxT_psum"], 1)

            def project_in(b):
                pe.wait_ge(s["xT_ready"], b + 1)
                for j in range(2 * HV):
                    if b:
                        pe.wait_ge(s["xs_ready"] if j < HV else s["z_ready"], j % HV + 1)
                    pe.matmul(bank(2 + j), w_in[:, P * j:P * j + P], xT[:, b, :], start=True,
                              stop=True).then_inc(s["win_psum"], 1)

            def context_kv():
                for b in range(B):
                    pe.wait_ge(s["ctxT_ready"], b + 1)
                    pe.matmul(ps[:, 6 + b, 128:128 + S2], wk[:], ctxT[:, b, :], start=True, stop=True)
                    pe.matmul(ps[0:S2, 6 + b, 256:256 + P], ctxT[:, b, :], wv[:], start=True,
                              stop=True).then_inc(s["kv_psum"], 1)

            def convolve(b):
                for g in range(HV):
                    pe.wait_ge(s["xs_ready"], HV * b + g + 1)
                    if b:
                        pe.wait_ge(s["u_ready"], g + 1)
                    else:
                        pe.wait_ge(s["kv_ready"], 2 * g + 2)
                    for t in range(TAPS):
                        mm = pe.matmul(bank(6 + g), conv_k[:, t, P * g:P * g + P], xsT[:, b, g, t:t + T],
                                       start=(t == 0), stop=(t == TAPS - 1))
                    mm.then_inc(s["conv_psum"], 1)

            pe.wait_ge(ld["win"], 16)
            context_t()
            project_in(0)
            context_kv()
            pe.wait_ge(ld["conv"], 32)
            pe.wait_ge(s["fills_ready"], 6)
            convolve(0)
            project_in(1)
            convolve(1)
            pe.wait_ge(s["simsq_ready"], 1)
            pe.wait_ge(s["xs_ready"], HV * B)
            pe.matmul(ps[:, 2, 0:2 * E], ones[:], sim_sq[:, :, :].rearrange("p n e -> p (n e)"), start=True,
                      stop=True).then_inc(s["simss_psum"], 1)
            pe.wait_ge(ld["small"], 48)
            for b in range(B):
                pe.wait_ge(s["u_ready"], HV * (b + 1))
                for h in range(HV):
                    mm = pe.matmul(bank(b, 96), w_x[:, h, :], uT[:, b, h, :], start=(h == 0), stop=(h == HV - 1))
                mm.then_inc(s["dbc_psum"], 1)
            pe.wait_ge(s["z_ready"], HV * B)
            pe.wait_ge(s["simss_ready"], 1)
            for b in range(B):
                pe.wait_ge(s["dtraw_ready"], b + 1)
                for h in range(HV):
                    pe.matmul(bank(2 + HV * b + h), w_dt[:, P * h:P * h + P], dt_raw[:, b, :], start=True,
                              stop=True).then_inc(s["wdt_psum"], 1)
            pe.wait_ge(s["kv_ready"], 2 * B)
            for b in range(B):
                for j in range(CH):
                    h0 = chunk(j)[0]
                    mm = pe.matmul(ps[:, 6 + b, HC * HD * j:HC * HD * (j + 1)], pairtok[:, P * j:P * j + P],
                                   v_sb[:, b, HD * h0:HD * (h0 + HC)], start=True, stop=True)
                mm.then_inc(s["vrep_psum"], 1)

            pe.wait_ge(s["vdiag_ready"], B + 1)
            pe.wait_ge(s["bc_ready"], B)
            pe.wait_ge(s["e_ready"], HV * B)
            pe.wait_ge(s["sel_ready"], 4)

            def spread(b, n, j):
                g = NS * b + n
                if b or not isinstance(n, int) or n >= 2:
                    pe.wait_ge(s["dbu_done"], 2 * (g - 1))
                pe.matmul(bank(j % 2), sel32[:, n, :], bc_parts[:, b, :], start=True, stop=True).then_inc(s["b_psum"], 1)
                if b or not isinstance(n, int) or n >= 1:
                    pe.wait_ge(s["crep_ready"], g)
                pe.matmul(bank(2), sel32[:, NS:2 * NS, :][:, n, :], bc_parts[:, b, :], start=True,
                          stop=True).then_inc(s["c_psum"], 1)

            def skip_term(b):
                for h in range(HV):
                    pe.matmul(bank(6 + h), diag_d[:, h, :], uT[:, b, h, :], start=True, stop=False,
                              skip_group_check=True)

            def add_state(b, n, j, stop=False):
                pe.wait_ge(s["prod_done"], NS * b + n + 1)
                for h in range(HV):
                    mm = pe.matmul(bank(6 + h), ident, prod[:, j % 2, h, :], start=False, stop=stop,
                                   skip_group_check=True)
                mm.then_inc(s["sum_done"], 1)

            def project_out(b):
                pe.wait_ge(s["g_ready"], HV * (b + 1))
                for k in range(K):
                    for h in range(HV):
                        mm = pe.matmul(ps[:, 3 + 4 * b, P * k:P * k + P], gT[:, h, P * k:P * k + P], w_out[:, h, :],
                                       start=(h == 0), stop=(h == HV - 1))
                mm.then_inc(s["wout_psum"], 1)

            def x1_transposes(b):
                pe.wait_ge(s["x1_ready"], b + 1)
                transposes(bank(3 + 4 * b), x1[:, b]).then_inc(s["x1T_psum"], 1)

            def x_query(b):
                pe.wait_ge(s["x1T_ready"], b + 1)
                pe.matmul(bank(3 + 4 * b), wq[:], x1T[:, b, :], start=True, stop=True).then_inc(s["q_psum"], 1)

            pe.wait_ge(s["diag_ready"], HV)
            skip_term(0)
            for n in range(2):
                spread(0, n, n)
            with pe.Fori(0, (NS - 2) // 2) as i:
                for j in range(2):
                    spread(0, i * 2 + (2 + j), j)
                    add_state(0, i * 2 + j, j)
            for n in range(NS - 2, NS):
                spread(1, n - (NS - 2), n)
                add_state(0, n, n, stop=(n == NS - 1))
            for n in range(2 * U):
                spread(1, n + 2, n)
                if n == 0:
                    pe.wait_ge(s["g_ready"], HV)
                    skip_term(1)
                add_state(1, n, n)
                if n == 1:
                    project_out(0)
                if n == 2 * U - 3:
                    x1_transposes(0)
            with pe.Fori(U, (NS - 2) // 2) as i:
                for j in range(2):
                    spread(1, i * 2 + (2 + j), j)
                    add_state(1, i * 2 + j, j)
            x_query(0)
            for n in range(NS - 2, NS):
                add_state(1, n, n, stop=(n == NS - 1))

            pe.wait_ge(s["kdiag_ready"], B)
            pe.wait_ge(s["masks_ready"], 16 * 3 * B)

            def x_scores(i):
                b, k = divmod(i, K)
                pe.wait_ge(s["qT_ready"], b + 1)
                if i >= 2:
                    pe.wait_ge(s["xpT_ready"], i - 1)
                elif i == 0:
                    pe.wait_ge(s["dbu_done"], HV * NS * B)
                    pe.wait_ge(s["crep_ready"], NS * B)
                else:
                    pe.wait_ge(s["scan_done"], HV * NS * B)
                for c in range(0, FLAT, 512):
                    w = min(512, FLAT - c)
                    at = 3 * (i % 2) + c // 512
                    pe.matmul(ps[:, at, 0:w], qT[:, b, P * k:P * k + P], k_diag[:, b, c:c + w],
                              start=True, stop=False)
                    mm = pe.matmul(ps[:, at, 0:w], ones_bf[:], mask_parts[:, b, c:c + w],
                                   start=False, stop=True)
                mm.then_inc(s["xs_psum"], 1)

            def x_transposes(i):
                pe.wait_ge(s["xexp_done"], i + 1)
                for j in range(CH):
                    rows = chunk(j)[1]
                    mm = pe.transpose(ps[0:rows, 3 * (i % 2) + j // 4, P * (j % 4):P * (j % 4) + P],
                                      xp[:, i % 2, P * j:P * j + rows], ident)
                mm.then_inc(s["xpT_psum"], 1)

            def x_values(i):
                b = i // K
                pe.wait_ge(s["xpT_ready"], i + 1)
                if i:
                    pe.wait_ge(s["x2p_ready"], i)
                for j in range(CH):
                    h0, rows = chunk(j)
                    mm = pe.matmul(ps[:, 6, HD1 * h0:HD1 * (h0 + HC)], xpT[i % 2][0:rows, j, :],
                                   v_diag[0:rows, b, j, :], start=(j == 0), stop=True, skip_group_check=True)
                mm.then_inc(s["xav_psum"], 1)

            def n_transposes(n, b):
                m = 2 * n + b
                pe.wait_ge(s["nrm_ready"], m + 1)
                if m:
                    pe.wait_ge(s["rwT_ready"], m)
                if n:
                    pe.wait_ge(s["att_ready"], B)
                transposes(bank(7), nrm[:, b]).then_inc(s["nT_psum"], 1)

            def logits(n, b):
                m = 2 * n + b
                pe.wait_ge(s["nsq_ready"], m + 1)
                pe.wait_ge(s["simn_ready"], 1)
                for k in range(K):
                    pe.matmul(ps[:, 7, 9 * k:9 * k + E], nT[:, b, P * k:P * k + P], simn[:, n, :], start=True, stop=True)
                    mm = pe.matmul(ps[:, 7, 9 * k + E:9 * k + 9], nsq[:, b, P * k:P * k + P], ones[:, 0:1],
                                   start=True, stop=True)
                mm.then_inc(s["logit_psum"], 1)

            def weights_t(n, b):
                m = 2 * n + b
                pe.wait_ge(s["rwparts_ready"], m + 1)
                for k in range(K):
                    mm = pe.transpose(ps[0:3 * E, 7, :].bitcast(BF16)[:, P * k:P * k + P],
                                      rw_parts[:, k, :, :].rearrange("p t e -> p (t e)"), ident_bf[:])
                mm.then_inc(s["rwT_psum"], 1)

            def spread_weight(dst, n, b, e):
                return pe.matmul(dst, sel8[:, e, :], rwT[:, n, b, :], start=True, stop=True)

            for i in range(K * B + 2):
                if i < K * B:
                    x_scores(i)
                if i == 0:
                    project_out(1)
                if 1 <= i <= K * B:
                    x_transposes(i - 1)
                if i >= 2:
                    x_values(i - 2)
                if i == 1:
                    x1_transposes(1)
                if i == 2:
                    x_query(1)
                if i == K + 3:
                    n_transposes(0, 0)
                if i == K + 4:
                    logits(0, 0)
            weights_t(0, 0)

            pe.wait_ge(ld["qkv"], 48)

            def spread_qkv(b, e):
                g = E * b + e
                pe.wait_ge(s["rwT_ready"], b + 1)
                if g >= 2:
                    pe.wait_ge(s["xe_ready"], g - 1)
                spread_weight(bank(2 + g % 2), 0, b, e).then_inc(s["rwb_psum"], 1)

            def qkv(b, e):
                g = E * b + e
                pe.wait_ge(s["xe_ready"], g + 1)
                if b and e == 0:
                    pe.wait_ge(s["qkv_ready"], 3)
                if g == 0:
                    pe.wait_ge(s["x2p_ready"], K * B)
                st, sp_ = e == 0, e == E - 1
                pe.matmul(bank(4), w_q[:, e, :], xe[:, g % 4, :], start=st, stop=sp_)
                pe.matmul(bank(5), w_k[:, e, :], xe[:, g % 4, :], start=st, stop=sp_)
                for k in range(K):
                    mm = pe.matmul(ps[:, 6, P * k:P * k + P], xe[:, g % 4, P * k:P * k + P], w_v[:, e, :],
                                   start=(st and k == 0), stop=sp_, skip_group_check=True)
                mm.then_inc(s["xe_used"], 1)

            def batch_of(b, spread_one, work, between, ahead):
                for e in range(ahead):
                    spread_one(b, e)
                for e in range(E):
                    if e + ahead < E:
                        spread_one(b, e + ahead)
                    work(b, e)
                    if e in between:
                        between[e]()

            def a_scores(b, i):
                pe.wait_ge(s["qkv_ready"], 3 * (b + 1))
                if b == 0 and i >= 2:
                    pe.wait_ge(s["apT_ready"], i - 1)
                if b and i < 2:
                    pe.wait_ge(s["apT_ready"], K)
                w = P * (i + 1)
                at = a_bank(b, i)
                pe.matmul(ps[:, at, 0:w], aqT[:, b, P * i:P * i + P], akT[:, b, 0:w], start=True, stop=True)
                pe.matmul(ps[:, at, w - P:w], ident_bf[:], causal_bf[:], start=False, stop=True,
                          skip_group_check=True).then_inc(s["as_psum"], 1)

            def a_transposes(b, i):
                pe.wait_ge(s["ap_ready"], K * b + i + 1)
                for j in range(i + 1):
                    mm = pe.transpose(ps[:, a_bank(b, i), P * j:P * j + P], ap_[:, i, P * j:P * j + P], ident)
                mm.then_inc(s["apT_psum"], 1)

            def a_values(b, i):
                pe.wait_ge(s["apT_ready"], K * b + i + 1)
                if b:
                    pe.wait_ge(s["att_ready"], 1)
                else:
                    pe.wait_ge(s["rwT_ready"], B)
                for j in range(i + 1):
                    mm = pe.matmul(ps[:, 7, P * i:P * i + P], av[:, b, j, :], apT[:, i, P * j:P * j + P],
                                   start=(j == 0), stop=(j == i), skip_group_check=True)
                mm.then_inc(s["att_psum"], 1)

            def attend(b, *steps):
                for what, i in steps:
                    what(b, i)

            S_, T_, V_ = a_scores, a_transposes, a_values
            batch_of(0, spread_qkv, qkv, {0: lambda: n_transposes(0, 1), 2: lambda: logits(0, 1),
                                          6: lambda: weights_t(0, 1)}, 1)
            batch_of(1, spread_qkv, qkv, {0: lambda: attend(0, (S_, 0), (S_, 1)), 1: lambda: attend(0, (T_, 0), (T_, 1)),
                                          2: lambda: attend(0, (V_, 0), (V_, 1), (S_, 2), (S_, 3)),
                                          3: lambda: attend(0, (T_, 2), (T_, 3)),
                                          4: lambda: attend(0, (V_, 2), (V_, 3))}, 1)

            pe.wait_ge(ld["o"], 16)

            def spread_o(b, e):
                g = E * b + e
                if g >= 2:
                    pe.wait_ge(s["oe_ready"], g - 1)
                else:
                    pe.wait_ge(s["xe_ready"], E * B)
                spread_weight(bank(2 + g % 2), 0, b, e).then_inc(s["rwo_psum"], 1)

            def o_proj(b, e):
                g = E * b + e
                pe.wait_ge(s["oe_ready"], g + 1)
                if e == 0:
                    if b:
                        pe.wait_ge(s["apT_ready"], K * B)
                    else:
                        pe.wait_ge(s["qkv_ready"], 3 * B)
                for k in range(K):
                    mm = pe.matmul(ps[:, 4 + b, P * k:P * k + P], xe[:, g % 4, P * k:P * k + P], w_o[:, e, :],
                                   start=(e == 0 and k == 0), stop=(e == E - 1), skip_group_check=True)
                mm.then_inc(s["oe_used"], 1)

            batch_of(0, spread_o, o_proj, {0: lambda: attend(1, (S_, 0), (S_, 1), (S_, 2), (S_, 3)),
                                           2: lambda: attend(1, (T_, 0), (T_, 1)), 3: lambda: attend(1, (T_, 2), (T_, 3)),
                                           5: lambda: attend(1, (V_, 0), (V_, 1), (V_, 2), (V_, 3))}, 2)
            batch_of(1, spread_o, o_proj, {4: lambda: n_transposes(1, 0), 6: lambda: logits(1, 0)}, 2)

            pe.wait_ge(ld["moe"], 32)

            def moe_up(b, e):
                g = E * b + e
                if g >= 3:
                    pe.wait_ge(s["inter_ready"], g - 2)
                else:
                    pe.wait_ge(s["oe_ready"], E * B)
                    pe.wait_ge(s["nT_ready"], B + 1)
                if b:
                    pe.wait_ge(s["nT_ready"], 2 * B)
                pe.matmul(bank(H_BANKS[g % 3]), w_1[:, e, :], nT[:, b, :], start=True, stop=True).then_inc(s["h_psum"], 1)

            def moe_weight(b, e):
                g = E * b + e
                pe.wait_ge(s["rwT_ready"], B + b + 1)
                if g >= 2:
                    pe.wait_ge(s["ge_ready"], g - 1)
                spread_weight(bank(g % 2), 1, b, e).then_inc(s["rwm_psum"], 1)

            def moe_down(b, e):
                g = E * b + e
                pe.wait_ge(s["ge_ready"], g + 1)
                if e == 0:
                    pe.wait_ge(s["hs_ready"], b + 1)
                for k in range(K):
                    mm = pe.matmul(ps[:, 4 + b, P * k:P * k + P], scaled[:, g % 2, P * k:P * k + P], w_2[:, e, :],
                                   start=(e == 0 and k == 0), stop=(e == E - 1), skip_group_check=True)
                mm.then_inc(s["ge_used"], 1)

            between = {0: lambda: n_transposes(1, 1), 2: lambda: logits(1, 1), 6: lambda: weights_t(1, 1)}
            for g in range(2):
                moe_up(0, g)
            weights_t(1, 0)
            moe_weight(0, 0)
            for g in range(E * B):
                if g + 2 < E * B:
                    moe_up(*divmod(g + 2, E))
                if g + 1 < E * B:
                    moe_weight(*divmod(g + 1, E))
                moe_down(*divmod(g, E))
                if g in between:
                    between[g]()

        @block.vector
        def _(dve):
            chain = [0]

            def link(ins):
                chain[0] += 1
                ins.then_inc(s["dve_chain"], 1)
                dve.wait_ge(s["dve_chain"], chain[0])

            for b in range(B):
                dve.wait_ge(s["xT_psum"], b + 1)
                dve.tensor_copy(xT[:, b, :], bank(b)).then_inc(s["xT_ready"], 1)

            def conv_input(b):
                for g in range(HV):
                    dve.wait_ge(s["win_psum"], 2 * HV * b + g + 1)
                    dve.tensor_copy(xsT[:, b, g, TAPS - 1:], bank(2 + g)).then_inc(s["xs_ready"], 1)

            conv_input(0)
            dve.wait_ge(ld["masks"], 32)
            dve.tensor_copy(sel32[:], cst("sel32", 96).unsqueeze(2).to_broadcast([96, 32, P])).then_inc(s["sel_ready"], 1)
            conv_input(1)
            dve.wait_ge(ld["conv"], 32)
            for h in range(HV):
                dve.tensor_scalar(diag_d[:, h, :], ident, skip_d[:, h:h + 1], None, ALU.mult).then_inc(s["diag_ready"], 1)
            dve.tensor_tensor(sim_sq[:], sim, sim, ALU.mult).then_inc(s["simsq_ready"], 1)
            link(dve.tensor_copy(mask_f[:], mask_i[:]))
            link(dve.tensor_scalar(mask_f[:], mask_f[:], -1.0, NEG, ALU.add, ALU.mult))
            link(dve.tensor_copy(mask_small[0:1], mask_f[:]))
            link(dve.tensor_tensor(mask_rest[32:33], mask_f[:], mask_small[0:1], ALU.subtract))
            link(dve.tensor_copy(mask_small[32:33], mask_rest[32:33]))
            dve.tensor_tensor(mask_small[64:65], mask_rest[32:33], mask_small[32:33],
                              ALU.subtract).then_inc(s["masksmall_ready"], 1)
            dve.wait_ge(s["simss_psum"], 1)
            dve.tensor_scalar(sim_ss[:].rearrange("p n e -> p (n e)"), ps[:, 2, 0:2 * E], 1e-24, None,
                              ALU.max).then_inc(s["simss_ready"], 1)
            for b in range(B):
                dve.wait_ge(s["dbc_psum"], b + 1)
                dve.tensor_copy(dt_raw[:, b, :], bank(b)[0:DTR]).then_inc(s["dtraw_ready"], 1)
                bc = bank(b)[DTR:96]
                link(dve.tensor_copy(bc_parts[0:32, b, :], bc))
                link(dve.tensor_tensor(bc_rest[32:64, :], bc, bc_parts[0:32, b, :], ALU.subtract))
                link(dve.tensor_copy(bc_parts[32:64, b, :], bc_rest[32:64, :]))
                dve.tensor_tensor(bc_parts[64:96, b, :], bc_rest[32:64, :], bc_parts[32:64, b, :],
                                  ALU.subtract).then_inc(s["bc_ready"], 1)
            dve.wait_ge(s["expa_ready"], 1)
            dve.tensor_scalar(neg_a[:], exp_a[:], -1.0, None, ALU.mult).then_inc(s["nega_ready"], 1)
            dve.wait_ge(s["gexpneg_ready"], 1)
            link(dve.tensor_scalar(gate_s[:], gate_s[:], 1.0, None, ALU.add))
            dve.reciprocal(gates[:], gate_s[:]).then_inc(s["gates_ready"], 1)

            def softplus(b):
                dve.wait_ge(s["e_ready"], HV * (b + 1))
                dve.tensor_scalar(e_dt[:, b], e_dt[:, b], SOFTPLUS_CAP, None, ALU.min).then_inc(s["ecap_ready"], 1)
                dve.wait_ge(s["ecap_ready"], b + 1)
                link(dve.tensor_scalar(r_dt[:], e_dt[:, b], 1.0, -1.0, ALU.add, ALU.add))
                link(dve.tensor_tensor(r_dt[:], e_dt[:, b], r_dt[:], ALU.subtract))
                dve.wait_ge(s["log_ready"], b + 1)
                link(dve.tensor_tensor(r_dt[:], log_dt[:, b], r_dt[:], ALU.add))
                dve.tensor_scalar(delta[:, b], r_dt[:], DT_MIN, DT_MAX, ALU.max, ALU.min).then_inc(s["delta_ready"], 1)
                dve.wait_ge(s["delta_ready"], b + 1)
                link(dve.tensor_tensor(du[:, b], delta[:, b], uT[:, b], ALU.mult))

            softplus(0)
            for b in range(B):
                dve.wait_ge(s["vrep_psum"], b + 1)
                dve.tensor_tensor(v_diag[:, b].rearrange("p j (h d) -> p (j h) d", d=HD1)[:, :, 0:HD],
                                  ps[:, 6 + b, 0:CH * HC * HD].rearrange("p (j d) -> p j d", d=HD),
                                  cst("pairhead").unsqueeze(2).to_broadcast([P, CH * HC, HD]),
                                  ALU.mult).then_inc(s["vdiag_ready"], 1)
            dve.tensor_copy(v_diag[:].rearrange("p b j (h d) -> p b (j h) d", d=HD1)[:, :, :, HD],
                            cst("pairhead").unsqueeze(1).to_broadcast([P, B, CH * HC])).then_inc(s["vdiag_ready"], 1)
            softplus(1)
            dve.wait_ge(s["simrn_ready"], 1)
            dve.tensor_tensor(simn[:], sim, sim_rn[:], ALU.mult).then_inc(s["simn_ready"], 1)

            def scan_state(b, n, j):
                g = NS * b + n
                dve.wait_ge(s["b_psum"], g + 1)
                for h in range(HV):
                    if b or not isinstance(n, int) or n >= 1:
                        dve.wait_ge(s["scan_done"], 2 * g - 1 + h)
                    dve.tensor_tensor(bank(4 + h), du[:, b, h, :], bank(j % 2), ALU.mult).then_inc(s["dbu_done"], 1)
                for h in range(HV):
                    dve.wait_ge(s["dbu_done"], 2 * g + 1 + h)
                    dve.wait_ge(s["decay_ready"], 2 * g + 1 + h)
                    if h == 0 and (b or not isinstance(n, int) or n >= 2):
                        dve.wait_ge(s["prod_done"], g - 1)
                    dve.tensor_tensor_scan(states[:, j % 2, h, :], decay[:, j % 2, h, :], bank(4 + h), 0.0, ALU.mult,
                                           ALU.add).then_inc(s["scan_done"], 1)

            def gated(b):
                dve.wait_ge(s["sum_done"], NS * (b + 1))
                if b:
                    dve.wait_ge(s["wout_psum"], 1)
                for h in range(HV):
                    dve.tensor_tensor(gT[:, h, :], zT[:, b, h, :], bank(6 + h), ALU.mult).then_inc(s["g_ready"], 1)

            roots = [0]

            def norm_stats(src):
                for k in range(K):
                    last = dve.bn_stats(stats[:, k, :], src[:, k, :])
                link(last)
                for k in range(K):
                    last = dve.bn_aggr(mv[:, k, :], stats[:, k, :])
                link(last)
                dve.tensor_scalar(var_eps[:], mv[:, :, 1], LN_EPS, None, ALU.add).then_inc(s["var_ready"], 1)

            def norm_apply(dst, src, ready):
                roots[0] += 1
                dve.wait_ge(s["rstd_ready"], roots[0])
                for k in range(K):
                    last = dve.tensor_scalar(dst[:, k, :], src[:, k, :], mv[:, k, 0:1], rstd[:, k:k + 1], ALU.subtract,
                                             ALU.mult)
                if ready is None:
                    link(last)
                else:
                    last.then_inc(s[ready], 1)

            def mixer_residual(b):
                dve.wait_ge(s["wout_psum"], b + 1)
                link(dve.tensor_tensor(x1p[:, b].rearrange("p k c -> p (k c)"), x[:, b].rearrange("p k c -> p (k c)"),
                                       bank(3 + 4 * b), ALU.add))
                norm_stats(x1p[:, b])

            for n in range(U):
                scan_state(0, n, n)
            with dve.Fori(1, NS // U) as i:
                for j in range(U):
                    scan_state(0, i * U + j, j)
            for n in range(2 * U):
                scan_state(1, n, n)
                if n == 1:
                    gated(0)
                if n == 3:
                    mixer_residual(0)
                if n == 4:
                    norm_apply(x1[:, 0], x1p[:, 0], "x1_ready")
            with dve.Fori(2, NS // U) as i:
                for j in range(U):
                    scan_state(1, i * U + j, j)
            gated(1)

            def x_softmax(i):
                b, k = divmod(i, K)
                dve.wait_ge(s["xs_psum"], i + 1)
                at = 3 * (i % 2)
                scores = ps[:, at:at + 3, :].rearrange("p a n -> p (a n)")[:, 0:FLAT].rearrange("p (h t) -> p h t", h=NH)
                if k == 0:
                    masked = xs_masked.rearrange("p (h t) -> p h t", h=NH)
                    link(dve.tensor_tensor(masked, scores, cst("xcausal").unsqueeze(1).to_broadcast([P, NH, S2]), ALU.add))
                    scores = masked
                link(dve.tensor_reduce(xs_max[:], scores, AX_X, ALU.max))
                if i >= 2:
                    dve.wait_ge(s["xpT_psum"], i - 1)
                dve.tensor_tensor(xp[:, i % 2, :].rearrange("p (h t) -> p h t", h=NH), scores,
                                  xs_max[:].unsqueeze(2).to_broadcast([P, NH, S2]), ALU.subtract).then_inc(s["xsub_done"], 1)

            def x_finish(i):
                b, k = divmod(i, K)
                dve.wait_ge(s["xav_psum"], i + 1)
                heads = ps[:, 6, 0:NH * HD1].rearrange("p (h d) -> p h d", h=NH)
                link(dve.reciprocal(xrec[:], heads[:, :, HD]))
                link(dve.tensor_tensor(xav[:].rearrange("p (h d) -> p h d", h=NH), heads[:, :, 0:HD],
                                       xrec[:].unsqueeze(2).to_broadcast([P, NH, HD]), ALU.mult))
                dve.tensor_tensor(x2p[:, b, k, :], xav[:], x1[:, b, k, :], ALU.add).then_inc(s["x2p_ready"], 1)

            got = ps[:, 7, 0:9 * K].rearrange("p (k e) -> p k e", k=K)

            def gate_norm(n, b):
                dve.wait_ge(s["logit_psum"], 2 * n + b + 1)
                dve.tensor_scalar(g_ss[:], got[:, :, E], 1e-24, None, ALU.max).then_inc(s["norm_ready"], 1)

            def gate_logits(n, b):
                dve.wait_ge(s["rnorm_ready"], 2 * n + b + 1)
                link(dve.tensor_tensor(g_l0[:], got[:, :, 0:E], g_rn[:].unsqueeze(2).to_broadcast([P, K, E]), ALU.mult))
                dve.wait_ge(s["gates_ready"], 1)
                link(dve.tensor_tensor(g_l[:], g_l0[:], gates[:, n, :].unsqueeze(1).to_broadcast([P, K, E]), ALU.subtract))
                dve.tensor_scalar(g_act[:], g_l[:], 0.0, None, ALU.is_gt)
                link(dve.tensor_scalar(g_relu[:], g_l[:], 0.0, None, ALU.max))
                link(dve.tensor_reduce(g_max[:], g_relu[:], AX_X, ALU.max))
                dve.tensor_tensor(g_sh[:], g_relu[:], g_max[:].unsqueeze(2).to_broadcast([P, K, E]),
                                  ALU.subtract).then_inc(s["gshift_ready"], 1)

            def gate_ranks():
                other = g_l[:].unsqueeze(2).to_broadcast([P, K, E, E])
                own = g_l[:].unsqueeze(3).to_broadcast([P, K, E, E])
                dve.tensor_tensor(g_gt[:], other, own, ALU.is_gt)
                link(dve.tensor_tensor(g_eq[:], other, own, ALU.is_equal))
                link(dve.tensor_tensor(g_eqt[:].rearrange("p k i j -> p k (i j)"), g_eq[:].rearrange("p k i j -> p k (i j)"),
                                       cst("tri").unsqueeze(1).to_broadcast([P, K, E * E]), ALU.mult))
                link(dve.tensor_tensor(g_cmp[:], g_gt[:], g_eqt[:], ALU.add))
                link(dve.tensor_reduce(g_rank[:], g_cmp[:], AX_X, ALU.add))
                dve.tensor_scalar(g_top[:], g_rank[:], 1.5, None, ALU.is_lt)
                link(dve.tensor_scalar(g_idle[:], g_max[:], 0.0, None, ALU.is_le))
                link(dve.tensor_tensor(g_put[:], g_top[:], g_idle[:].unsqueeze(2).to_broadcast([P, K, E]), ALU.mult))
                link(dve.tensor_tensor(g_mask[:], g_act[:], g_put[:], ALU.max))

            def gate_weights(n, b):
                m = 2 * n + b
                dve.wait_ge(s["gexp_ready"], m + 1)
                link(dve.tensor_tensor(g_w[:], g_ex[:], g_mask[:], ALU.mult))
                link(dve.tensor_reduce(g_sum[:], g_w[:], AX_X, ALU.add))
                link(dve.reciprocal(g_rs[:], g_sum[:]))
                link(dve.tensor_tensor(g_rw[:], g_w[:], g_rs[:].unsqueeze(2).to_broadcast([P, K, E]), ALU.mult))
                if m:
                    dve.wait_ge(s["rwT_psum"], m)
                link(dve.tensor_copy(rw_parts[:, :, 0, :], g_rw[:]))
                link(dve.tensor_tensor(g_r1[:], g_rw[:], rw_parts[:, :, 0, :], ALU.subtract))
                link(dve.tensor_copy(rw_parts[:, :, 1, :], g_r1[:]))
                dve.tensor_tensor(rw_parts[:, :, 2, :], g_r1[:], rw_parts[:, :, 1, :],
                                  ALU.subtract).then_inc(s["rwparts_ready"], 1)

            for i in range(K * B + 2):
                if i >= 3:
                    x_finish(i - 3)
                if i == K + 2:
                    dve.wait_ge(s["x2p_ready"], K)
                    norm_stats(x2p[:, 0])
                if i == K + 3:
                    norm_apply(nrm[:, 0], x2[:, 0], "nrm_ready")
                if i < K * B:
                    x_softmax(i)
                if i == 0:
                    mixer_residual(1)
                if i == 1:
                    norm_apply(x1[:, 1], x1p[:, 1], "x1_ready")
                if i == K + 2:
                    norm_apply(x2[:, 0], x2p[:, 0], None)
                    norm_stats(x2[:, 0])
            gate_norm(0, 0)
            x_finish(K * B - 1)
            gate_logits(0, 0)
            gate_ranks()
            gate_weights(0, 0)

            def weigh_qkv(b, e):
                g = E * b + e
                dve.wait_ge(s["rwb_psum"], g + 1)
                dve.wait_ge(s["nT_ready"], b + 1)
                if g >= 4:
                    dve.wait_ge(s["xe_used"], g - 3)
                dve.tensor_tensor(xe[:, g % 4, :], nT[:, b, :], bank(2 + g % 2), ALU.mult).then_inc(s["xe_ready"], 1)

            dve.wait_ge(s["x2p_ready"], K * B)
            norm_stats(x2p[:, 1])
            weigh_qkv(0, 0)
            norm_apply(x2[:, 1], x2p[:, 1], None)
            norm_stats(x2[:, 1])
            weigh_qkv(0, 1)
            norm_apply(nrm[:, 1], x2[:, 1], "nrm_ready")
            weigh_qkv(0, 2)
            weigh_qkv(0, 3)
            gate_norm(0, 1)
            weigh_qkv(0, 4)
            gate_logits(0, 1)
            weigh_qkv(0, 5)
            gate_ranks()
            weigh_qkv(0, 6)
            gate_weights(0, 1)
            weigh_qkv(0, 7)

            def a_rowmax(b, i):
                dve.wait_ge(s["as_psum"], K * b + i + 1)
                link(dve.tensor_reduce(a_max[:, i:i + 1], ps[:, a_bank(b, i), 0:P * (i + 1)], AX_X, ALU.max))
                dve.tensor_scalar(a_nmax[:, i:i + 1], a_max[:, i:i + 1], -SCALE_A, None, ALU.mult).then_inc(s["amax_ready"], 1)

            def a_normalise(b, i):
                dve.wait_ge(s["aexp_done"], K * b + i + 1)
                link(dve.reciprocal(a_rec[:, i:i + 1], a_sum[:, i:i + 1]))
                w = P * (i + 1)
                dve.tensor_scalar(ap_[:, i, 0:w], ap_[:, i, 0:w], a_rec[:, i:i + 1], None, ALU.mult).then_inc(s["ap_ready"], 1)

            weigh_qkv(1, 0)
            weigh_qkv(1, 1)
            a_rowmax(0, 0)
            a_rowmax(0, 1)
            weigh_qkv(1, 2)
            a_normalise(0, 0)
            a_normalise(0, 1)
            weigh_qkv(1, 3)
            a_rowmax(0, 2)
            a_rowmax(0, 3)
            weigh_qkv(1, 4)
            a_normalise(0, 2)
            a_normalise(0, 3)
            for e in range(5, E):
                weigh_qkv(1, e)

            def weigh_o(b, e):
                g = E * b + e
                dve.wait_ge(s["rwo_psum"], g + 1)
                dve.wait_ge(s["att_ready"], b + 1)
                if g >= 4:
                    dve.wait_ge(s["oe_used"], g - 3)
                else:
                    dve.wait_ge(s["xe_used"], E * B - 3 + g)
                dve.tensor_tensor(xe[:, g % 4, :], attnT[:, b, :], bank(2 + g % 2), ALU.mult).then_inc(s["oe_ready"], 1)

            def attention_residual(b):
                dve.wait_ge(s["oe_used"], E * (b + 1))
                dve.tensor_tensor(hs[:, b].rearrange("p k c -> p (k c)"), x2[:, b].rearrange("p k c -> p (k c)"), bank(4 + b),
                                  ALU.add).then_inc(s["hs_ready"], 1)
                dve.wait_ge(s["hs_ready"], b + 1)
                norm_stats(hs[:, b])

            weigh_o(0, 0)
            weigh_o(0, 1)
            weigh_o(0, 2)
            for i in range(K):
                a_rowmax(1, i)
            weigh_o(0, 3)
            a_normalise(1, 0)
            a_normalise(1, 1)
            weigh_o(0, 4)
            a_normalise(1, 2)
            a_normalise(1, 3)
            for e in range(5, E):
                weigh_o(0, e)
            weigh_o(1, 0)
            weigh_o(1, 1)
            attention_residual(0)
            weigh_o(1, 2)
            norm_apply(nrm[:, 0], hs[:, 0], "nrm_ready")
            for e in range(3, E):
                weigh_o(1, e)
            gate_norm(1, 0)
            attention_residual(1)
            gate_logits(1, 0)
            gate_ranks()
            gate_weights(1, 0)
            norm_apply(nrm[:, 1], hs[:, 1], "nrm_ready")

            def weigh_moe(b, e):
                g = E * b + e
                dve.wait_ge(s["rwm_psum"], g + 1)
                dve.wait_ge(s["inter_ready"], g + 1)
                if g >= 2:
                    dve.wait_ge(s["ge_used"], g - 1)
                dve.tensor_tensor(scaled[:, g % 2, :], inter[:, g % 4, :], bank(g % 2), ALU.mult).then_inc(s["ge_ready"], 1)

            def last_norm(b):
                dve.wait_ge(s["ge_used"], E * (b + 1))
                dve.wait_ge(s["hx_ready"], b + 1)
                link(dve.tensor_tensor(x3p[:, b].rearrange("p k c -> p (k c)"), hx[:, b].rearrange("p k c -> p (k c)"),
                                       bank(4 + b), ALU.add))
                norm_stats(x3p[:, b])

            for e in range(3):
                weigh_moe(0, e)
            gate_norm(1, 1)
            weigh_moe(0, 3)
            gate_logits(1, 1)
            weigh_moe(0, 4)
            gate_ranks()
            weigh_moe(0, 5)
            gate_weights(1, 1)
            weigh_moe(0, 6)
            weigh_moe(0, 7)
            weigh_moe(1, 0)
            last_norm(0)
            weigh_moe(1, 1)
            norm_apply(x3[:, 0], x3p[:, 0], "x3_ready")
            for e in range(2, E):
                weigh_moe(1, e)
            last_norm(1)
            norm_apply(x3[:, 1], x3p[:, 1], "x3_ready")

        @block.scalar
        def _(act):
            for b in range(B):
                act.wait_ge(s["ctxT_psum"], b + 1)
                act.activation(ctxT[:, b, :], ps[:, 6 + b, 0:S2], ACT.Copy).then_inc(s["ctxT_ready"], 1)

            def gate_branch(b):
                for h in range(HV):
                    act.wait_ge(s["win_psum"], 2 * HV * b + HV + h + 1)
                    act.activation(zT[:, b, h, :], bank(2 + HV + h), ACT.Silu).then_inc(s["z_ready"], 1)

            def conv_out(b):
                for g in range(HV):
                    act.wait_ge(s["conv_psum"], HV * b + g + 1)
                    act.activation(uT[:, b, g, :], bank(6 + g), ACT.Silu, bias=conv_b[:, g:g + 1]).then_inc(s["u_ready"], 1)

            gate_branch(0)
            for b in range(B):
                act.wait_ge(s["kv_psum"], b + 1)
                act.activation(kT[:, b, :], ps[:, 6 + b, 128:128 + S2], ACT.Copy).then_inc(s["kv_ready"], 1)
                act.activation(v_sb[:, b, :], ps[0:S2, 6 + b, 256:256 + P], ACT.Copy).then_inc(s["kv_ready"], 1)
            act.wait_ge(ld["conv"], 32)
            conv_out(0)
            gate_branch(1)
            conv_out(1)
            act.activation(exp_a[:], a_log, ACT.Exp).then_inc(s["expa_ready"], 1)
            act.activation(gate_s[:], gates_in, ACT.Exp, scale=-1.0).then_inc(s["gexpneg_ready"], 1)
            for b in range(B):
                for h in range(HV):
                    act.wait_ge(s["wdt_psum"], HV * b + h + 1)
                    act.activation(e_dt[:, b, h, :], bank(2 + HV * b + h), ACT.Exp, bias=b_dt[:, h:h + 1]).then_inc(s["e_ready"], 1)
                act.wait_ge(s["ecap_ready"], b + 1)
                act.activation(log_dt[:, b], e_dt[:, b], ACT.Ln, bias=1.0).then_inc(s["log_ready"], 1)

            def scan_state(b, n, j):
                g = NS * b + n
                if b or not isinstance(n, int) or n >= 2:
                    act.wait_ge(s["scan_done"], 2 * (g - 1))
                for h in range(HV):
                    if isinstance(n, int):
                        scale = neg_a[:, h, n:n + 1]
                    else:
                        scale = neg_a[:, h, :][:, bass.ds(n, 1)]
                    act.activation(decay[:, j % 2, h, 1:], delta[:, b, h, 1:], ACT.Exp, scale=scale).then_inc(s["decay_ready"], 1)
                act.wait_ge(s["c_psum"], g + 1)
                if b or not isinstance(n, int) or n >= 2:
                    act.wait_ge(s["prod_done"], g - 1)
                act.activation(c_rep[:, j % 2, :], bank(2), ACT.Copy).then_inc(s["crep_ready"], 1)

            def x1T_take(b):
                act.wait_ge(s["x1T_psum"], b + 1)
                act.activation(x1T[:, b, :], bank(3 + 4 * b), ACT.Copy).then_inc(s["x1T_ready"], 1)

            def query_take(b):
                act.wait_ge(s["q_psum"], b + 1)
                act.wait_ge(s["prod_done"], NS * B - 1 + b)
                act.activation(qT[:, b, :], bank(3 + 4 * b), ACT.Copy, scale=SCALE_X).then_inc(s["qT_ready"], 1)

            act.wait_ge(s["nega_ready"], 1)
            act.wait_ge(s["fills_ready"], 6)
            act.wait_ge(s["delta_ready"], 1)
            for n in range(U):
                scan_state(0, n, n)
            with act.Fori(1, NS // U) as i:
                for j in range(U):
                    scan_state(0, i * U + j, j)
            act.wait_ge(s["delta_ready"], B)
            for n in range(2 * U):
                scan_state(1, n, n)
            x1T_take(0)
            with act.Fori(2, NS // U) as i:
                for j in range(U):
                    scan_state(1, i * U + j, j)
            query_take(0)

            def x_exp(i):
                act.wait_ge(s["xsub_done"], i + 1)
                act.activation(xp[:, i % 2, :], xp[:, i % 2, :], ACT.Exp).then_inc(s["xexp_done"], 1)

            def x_take(i):
                act.wait_ge(s["xpT_psum"], i + 1)
                if i >= 2:
                    act.wait_ge(s["xav_psum"], i - 1)
                full, rows, at = P * (CH - 1), chunk(CH - 1)[1], 3 * (i % 2)
                act.activation(xpT[i % 2].rearrange("p j t -> p (j t)")[:, 0:full],
                               ps[:, at:at + 3, :].rearrange("p a n -> p (a n)")[:, 0:full], ACT.Copy)
                act.activation(xpT[i % 2][0:rows, CH - 1, :], ps[0:rows, at + 2, P:2 * P], ACT.Copy).then_inc(s["xpT_ready"], 1)

            def n_take(n, b):
                m = 2 * n + b
                act.wait_ge(s["nT_psum"], m + 1)
                act.activation(nT[:, b, :], bank(7), ACT.Identity, scale=ln_w[:, n:n + 1],
                               bias=ln_b[:, n:n + 1]).then_inc(s["nT_ready"], 1)
                act.wait_ge(s["nT_ready"], m + 1)
                act.activation(nsq[:, b, :], nT[:, b, :], ACT.Square).then_inc(s["nsq_ready"], 1)

            def gate_exp(m):
                act.wait_ge(s["gshift_ready"], m + 1)
                act.activation(g_ex[:], g_sh[:], ACT.Exp).then_inc(s["gexp_ready"], 1)

            def weights_take(n, b):
                act.wait_ge(s["rwT_psum"], 2 * n + b + 1)
                act.activation(rwT[:, n, b, :], ps[0:3 * E, 7, :].bitcast(BF16)[:, 0:T], ACT.Copy).then_inc(s["rwT_ready"], 1)

            for i in range(K * B + 1):
                if i:
                    x_take(i - 1)
                if i < K * B:
                    x_exp(i)
                if i == 1:
                    x1T_take(1)
                if i == 2:
                    query_take(1)
                if i == K + 3:
                    n_take(0, 0)
            gate_exp(0)
            weights_take(0, 0)
            n_take(0, 1)
            gate_exp(1)
            weights_take(0, 1)

            def take_qkv(b):
                act.wait_ge(s["xe_used"], E * (b + 1))
                act.activation(aqT[:, b, :], bank(4), ACT.Copy).then_inc(s["qkv_ready"], 1)
                act.activation(akT[:, b, :], bank(5), ACT.Copy).then_inc(s["qkv_ready"], 1)
                act.activation(av[:, b].rearrange("p k c -> p (k c)"), bank(6), ACT.Copy).then_inc(s["qkv_ready"], 1)

            def a_exp(b, i):
                act.wait_ge(s["amax_ready"], K * b + i + 1)
                if b:
                    act.wait_ge(s["apT_psum"], i + 1)
                w = P * (i + 1)
                act.activation(ap_[:, i, 0:w], ps[:, a_bank(b, i), 0:w], ACT.Exp, bias=a_nmax[:, i:i + 1], scale=SCALE_A,
                               accum_out=a_sum[:, i:i + 1]).then_inc(s["aexp_done"], 1)

            def a_take(b, i):
                act.wait_ge(s["apT_psum"], K * b + i + 1)
                if b:
                    act.wait_ge(s["att_psum"], i + 1)
                w = P * (i + 1)
                act.activation(apT[:, i, 0:w], ps[:, a_bank(b, i), 0:w], ACT.Copy).then_inc(s["apT_ready"], 1)

            def att_take(b):
                act.wait_ge(s["att_psum"], K * (b + 1))
                act.activation(attnT[:, b, :], bank(7), ACT.Copy).then_inc(s["att_ready"], 1)

            take_qkv(0)
            for pair in range(0, K, 2):
                for i in range(pair, pair + 2):
                    a_exp(0, i)
                for i in range(pair, pair + 2):
                    a_take(0, i)
            att_take(0)
            take_qkv(1)
            for i in range(K):
                a_exp(1, i)
            for i in range(K):
                a_take(1, i)
            att_take(1)

            def moe_gelu(b, e):
                g = E * b + e
                act.wait_ge(s["h_psum"], g + 1)
                if g >= 4:
                    act.wait_ge(s["ge_ready"], g - 3)
                act.activation(inter[:, g % 4, :], bank(H_BANKS[g % 3]), ACT.Gelu).then_inc(s["inter_ready"], 1)

            n_take(1, 0)
            gate_exp(2)
            moe_gelu(0, 0)
            moe_gelu(0, 1)
            weights_take(1, 0)
            moe_gelu(0, 2)
            n_take(1, 1)
            for e in range(3, 6):
                moe_gelu(0, e)
            gate_exp(3)
            moe_gelu(0, 6)
            moe_gelu(0, 7)
            moe_gelu(1, 0)
            weights_take(1, 1)
            for e in range(1, E):
                moe_gelu(1, e)

        @block.gpsimd
        def _(pool):
            pool.memset(xsT[:, :, :, 0:TAPS - 1], 0.0).then_inc(s["fills_ready"], 1)
            pool.memset(decay[:, :, :, 0:1], 0.0).then_inc(s["fills_ready"], 1)
            pool.memset(ones[:], 1.0).then_inc(s["fills_ready"], 1)
            pool.memset(ones_bf[:], 1.0).then_inc(s["fills_ready"], 1)
            pool.memset(minus_half[:], -0.5).then_inc(s["fills_ready"], 1)
            pool.memset(mask_parts[:], 0.0).then_inc(s["fills_ready"], 1)
            pool.wait_ge(ld["masks"], 32)
            pool.wait_ge(ld["x"], 48)
            pool.tensor_copy(sel8[:], cst("sel8", 3 * E).unsqueeze(2).to_broadcast([3 * E, E, P])).then_inc(s["sel_ready"], 1)
            pool.tensor_copy(causal_bf[:], cst("causal")).then_inc(s["sel_ready"], 1)
            pool.tensor_copy(ident_bf[:], ident).then_inc(s["sel_ready"], 1)
            for b in range(B):
                pool.wait_ge(s["kv_ready"], 2 * b + 1)
                pool.tensor_tensor(k_diag[:, b, :].rearrange("p (h t) -> p h t", h=NH),
                                   kT[:, b, :].unsqueeze(1).to_broadcast([P, NH, S2]),
                                   cst("headof").unsqueeze(2).to_broadcast([P, NH, S2]),
                                   ALU.mult).then_inc(s["kdiag_ready"], 1)
            pool.wait_ge(s["simss_ready"], 1)
            pool.wait_ge(s["fills_ready"], 6)
            pool.tensor_tensor(sim_rn[:].rearrange("p n e -> p (n e)"), sim_ss[:].rearrange("p n e -> p (n e)"),
                               minus_half[:], ALU.pow).then_inc(s["simrn_ready"], 1)

            def scan_state(b, n, j):
                g = NS * b + n
                pool.wait_ge(s["scan_done"], 2 * g + 2)
                pool.wait_ge(s["crep_ready"], g + 1)
                if b or not isinstance(n, int) or n >= 2:
                    pool.wait_ge(s["sum_done"], g - 1)
                pool.tensor_tensor(prod[:, j % 2], states[:, j % 2],
                                   c_rep[:, j % 2, :].unsqueeze(1).to_broadcast([P, HV, T]),
                                   ALU.mult).then_inc(s["prod_done"], 1)

            norms, gates_done = [0], [0]

            def norm_root():
                norms[0] += 1
                pool.wait_ge(s["var_ready"], norms[0])
                pool.tensor_tensor(rstd[:], var_eps[:], minus_half[:, 0:K], ALU.pow).then_inc(s["rstd_ready"], 1)

            def gate_root():
                gates_done[0] += 1
                pool.wait_ge(s["norm_ready"], gates_done[0])
                pool.tensor_tensor(g_rn[:], g_ss[:], minus_half[:, 0:K], ALU.pow).then_inc(s["rnorm_ready"], 1)

            def residual_sum(b):
                pool.wait_ge(s["hs_ready"], b + 1)
                pool.tensor_tensor(hx[:, b], hs[:, b], x2[:, b], ALU.add).then_inc(s["hx_ready"], 1)

            for n in range(U):
                scan_state(0, n, n)
            with pool.Fori(1, NS // U) as i:
                for j in range(U):
                    scan_state(0, i * U + j, j)
            for n in range(2 * U):
                scan_state(1, n, n)
                if n == 3:
                    norm_root()
            with pool.Fori(2, NS // U) as i:
                for j in range(U):
                    scan_state(1, i * U + j, j)
            for _ in range(3):
                norm_root()
            gate_root()
            norm_root()
            norm_root()
            gate_root()
            norm_root()
            residual_sum(0)
            gate_root()
            norm_root()
            residual_sum(1)
            gate_root()
            norm_root()
            norm_root()

        return nc


_WHOLE = ["x", "ctx_1024", "mask_BxS2_ik0", "L0_attn_W_in", "L0_attn_conv_k", "L0_attn_W_x", "L0_attn_W_dt", "L0_attn_W_out",
          "L0_xattn_Wq", "L0_xattn_Wk", "L0_xattn_Wv", "L0_ffn_q_proj", "L0_ffn_k_proj", "L0_ffn_v_proj",
          "L0_ffn_o_proj", "L0_ffn_w1", "L0_ffn_w2"]


def small_columns(inputs):
    def halves(name, n=HV):
        return np.asarray(inputs[name]).reshape(n, P).T

    a_log = np.asarray(inputs["L0_attn_A_log"]).reshape(HV, P, NS).transpose(1, 0, 2).reshape(P, HV * NS)
    columns = [halves("L0_attn_conv_b"), halves("L0_attn_b_dt"), halves("L0_attn_D"),
               halves("L0_ffn_ln1_w", 1), halves("L0_ffn_ln2_w", 1), halves("L0_ffn_ln1_b", 1), halves("L0_ffn_ln2_b", 1),
               a_log, np.asarray(inputs["L0_ffn_smha_sim"]), np.asarray(inputs["L0_ffn_moe_sim"])]
    columns += [np.broadcast_to(np.asarray(inputs[n]), (P, E)) for n in ("L0_ffn_smha_gates", "L0_ffn_moe_gates")]
    return np.ascontiguousarray(np.concatenate(columns, axis=1))


def kernel(**inputs):
    import concourse.bacc as bacc
    from concourse.bass_utils import run_bass_kernel_spmd

    nc = bacc.Bacc("TRN2", target_bir_lowering=False, num_devices=1)
    arrays, aps = {}, {}
    for name in _WHOLE:
        value = np.ascontiguousarray(inputs[name])
        arrays[f"in_{name}"] = value
        aps[name] = nc.dram_tensor(f"in_{name}", value.shape, mybir.dt.from_np(value.dtype), kind="ExternalInput").ap()
    arrays["in_consts"] = shape_constants()
    arrays["in_small"] = small_columns(inputs)
    aps["small"] = nc.dram_tensor("in_small", [P, SMALL_COLS], F32, kind="ExternalInput").ap()
    aps["consts"] = nc.dram_tensor("in_consts", [P, CONST_COLS], F32, kind="ExternalInput").ap()
    out = nc.dram_tensor("out_y", [B, T, C], F32, kind="ExternalOutput").ap()
    decoder_layer(nc, aps, out)
    got = run_bass_kernel_spmd(nc, [arrays], core_ids=[0])
    return got.results[0]["out_y"]
```

```python
from contextlib import ExitStack

import numpy as np

import concourse.bass as bass
from concourse import mybir

F32 = mybir.dt.float32
BF16 = mybir.dt.bfloat16
I32 = mybir.dt.int32
ALU = mybir.AluOpType
ACT = mybir.ActivationFunctionType
AX_X = mybir.AxisListType.X

P = 128
B, T, C = 2, 512, 128
K = T // P
DI = 256
HV = DI // P
NS = 16
DTR = 64
TAPS = 4
NH, HD = 16, 8
S2 = 77
FLAT = NH * S2
CH = -(-FLAT // P)
HD1 = HD + 1
HC = 3
E = 8
NEG = 1.0e9
LN_EPS = 1e-5
DT_MIN, DT_MAX = 0.001, 0.1
SOFTPLUS_CAP = 0.2
LEAST = 2.0 ** -126
U = 4

WIDTHS = {"ident": P, "causal": P, "sel32": 32, "sel8": E, "tri": E * E, "headof": NH, "xcausal": S2,
          "pairhead": CH * HC}
AT = {}
_at = 0
for _name, _width in WIDTHS.items():
    AT[_name] = (_at, _at + _width)
    _at += _width
PAIR_COLS = CH * P
CONST_COLS = _at + PAIR_COLS
AT["pairtok"] = (_at, CONST_COLS)
CONST_FIRST = AT["causal"][0]


def chunk(j):
    return min(P * j // S2, NH - HC), min(P, FLAT - P * j)


SMALL_COLS = 3 * HV + 4 + HV * NS + 4 * E


def shape_constants():
    c = np.zeros((P, CONST_COLS), np.float32)
    p = np.arange(P)[:, None]

    def put(name, values):
        c[:values.shape[0], AT[name][0]:AT[name][1]] = values

    put("ident", (p == np.arange(P)).astype(np.float32))
    put("causal", np.where(np.arange(P) > p, -1e30, 0.0).astype(np.float32))
    put("sel32", (p % 32 == np.arange(32)).astype(np.float32))
    put("sel8", ((p % E == np.arange(E)) & (p < 3 * E)).astype(np.float32))
    i, j = np.arange(E * E) // E, np.arange(E * E) % E
    put("tri", np.broadcast_to(np.where(j < i, -LEAST, 0.0).astype(np.float32), (P, E * E)))
    put("headof", (p // HD == np.arange(NH)).astype(np.float32))
    put("xcausal", np.where(np.arange(S2) > p, -NEG, 0.0).astype(np.float32))
    flat = P * np.arange(CH)[None, :] + p
    first = np.array([chunk(j)[0] for j in range(CH)])
    put("pairhead", ((flat // S2 - first)[:, :, None] == np.arange(HC)).astype(np.float32).reshape(P, CH * HC))
    f = np.arange(CH * P)
    put("pairtok", ((f % S2 == np.arange(S2)[:, None]) & (f < FLAT)).astype(np.float32))
    return c


def decoder_layer(nc, a, out):
    with ExitStack() as ctx:
        def sb(name, shape, dt=F32):
            return ctx.enter_context(nc.sbuf_tensor(name, shape, dt))

        def sem(name):
            return ctx.enter_context(nc.semaphore(name))

        ps = ctx.enter_context(nc.psum_tensor("ps", [P, 8, 512], F32))

        def bank(i, rows=P):
            return ps[0:rows, i, :]

        const = sb("const", [P, CONST_COLS - PAIR_COLS])

        def cst(name, rows=P):
            return const[0:rows, AT[name][0]:AT[name][1]]

        ident = cst("ident")
        ident_bf = sb("ident_bf", [P, P], BF16)
        causal_bf = sb("causal_bf", [P, P], BF16)
        sel32 = sb("sel32", [96, 32, P], BF16)
        sel8 = sb("sel8", [3 * E, E, P], BF16)
        ones = sb("ones", [P, P])
        ones_bf = sb("ones_bf", [96, P], BF16)
        minus_half = sb("minus_half", [P, 2 * E])
        w_in = sb("w_in", [P, 2 * DI])
        conv_k = sb("conv_k", [P, TAPS, DI])
        w_x = sb("w_x", [P, HV, DTR + 2 * NS])
        w_dt = sb("w_dt", [DTR, DI])
        w_out = sb("w_out", [P, HV, C])
        small = sb("small", [P, SMALL_COLS])
        conv_b, b_dt, skip_d = (small[:, i * HV:(i + 1) * HV] for i in range(3))
        ln_w, ln_b = small[:, 6:8], small[:, 8:10]
        a_log = small[:, 10:42].rearrange("p (h n) -> p h n", h=HV)
        sim = small[:, 42:58].rearrange("p (n e) -> p n e", n=2)
        gates_in = small[:, 58:74].rearrange("p (n e) -> p n e", n=2)
        neg_a = sb("neg_a", [P, HV, NS])
        exp_a = sb("exp_a", [P, HV, NS])
        diag_d = sb("diag_d", [P, HV, P])
        wq = sb("wq", [P, P])
        wk = sb("wk", [P, P])
        wv = sb("wv", [P, P])
        sim_sq = sb("sim_sq", [P, 2, E])
        sim_rn = sb("sim_rn", [P, 2, E])
        sim_ss = sb("sim_ss", [P, 2, E])
        simn = sb("simn", [P, 2, E])
        gates = sb("gates", [P, 2, E])
        gate_s = sb("gate_s", [P, 2, E])
        w_q = sb("w_q", [P, E, P])
        w_k = sb("w_k", [P, E, P])
        w_v = sb("w_v", [P, E, P])
        w_o = sb("w_o", [P, E, P])
        w_1 = sb("w_1", [P, E, P])
        w_2 = sb("w_2", [P, E, P])

        x = sb("x", [P, B, K, C])
        xT = sb("xT", [P, B, T])
        xsT = sb("xsT", [P, B, HV, TAPS - 1 + T])
        zT = sb("zT", [P, B, HV, T])
        uT = sb("uT", [P, B, HV, T])
        bc_parts = sb("bc_parts", [96, B, T], BF16)
        e_dt = sb("e_dt", [P, B, HV, T])
        log_dt = sb("log_dt", [P, B, HV, T])
        r_dt = sb("r_dt", [P, B, HV, T])
        delta = sb("delta", [P, B, HV, T])
        du = sb("du", [P, B, HV, T])
        decay = sb("decay", [P, 2, HV, T])
        states = sb("states", [P, 2, HV, T])
        d_bu = sb("d_bu", [P, HV, T])
        c_rep = sb("c_rep", [P, 2, T])
        prod = sb("prod", [P, 2, HV, T])
        x1 = sb("x1", [P, B, K, C])
        ctx_sb = sb("ctx_sb", [S2, B, C])
        ctxT = sb("ctxT", [P, B, S2])
        kT = sb("kT", [P, B, S2])
        v_sb = sb("v_sb", [S2, B, P])
        xp = sb("xp", [P, 2, FLAT])
        xpT_odd = sb("xpT_odd", [P, CH, P])
        k_diag = sb("k_diag", [P, B, FLAT])
        v_diag = sb("v_diag", [P, B, CH, HC * HD1])
        mask_i = sb("mask_i", [1, B, S2], I32)
        mask_f = sb("mask_f", [1, B, S2])
        mask_rest = sb("mask_rest", [64, B, S2])
        mask_small = sb("mask_small", [96, B, S2], BF16)
        mask_parts = sb("mask_parts", [96, B, FLAT], BF16)
        xs_max = sb("xs_max", [P, 2, NH])
        xrec = sb("xrec", [P, NH])
        xav = sb("xav", [P, P])
        stats = sb("stats", [P, K, 6])
        mv = sb("mv", [P, K, 2])
        var_eps = sb("var_eps", [P, 2 * K])
        rstd = sb("rstd", [P, 2 * K])
        g_ss = sb("g_ss", [P, K])
        g_rn = sb("g_rn", [P, K])
        g_l0 = sb("g_l0", [P, K, E])
        g_l = sb("g_l", [P, K, E])
        g_gt = sb("g_gt", [P, K, E, E])
        g_cmp = sb("g_cmp", [P, K, E, E])
        g_rank = sb("g_rank", [P, K, E])
        g_top = sb("g_top", [P, K, E])
        g_relu = sb("g_relu", [P, K, E])
        g_act = sb("g_act", [P, K, E])
        g_max = sb("g_max", [P, K])
        g_idle = sb("g_idle", [P, K])
        g_put = sb("g_put", [P, K, E])
        g_mask = sb("g_mask", [P, K, E])
        g_sh = sb("g_sh", [P, K, E])
        g_ex = sb("g_ex", [P, K, E])
        g_w = sb("g_w", [P, K, E])
        g_sum = sb("g_sum", [P, K])
        g_rs = sb("g_rs", [P, K])
        g_rw = sb("g_rw", [P, 2, B, K, E])
        g_r1 = sb("g_r1", [P, K, E])
        rw_parts = sb("rw_parts", [P, K, 3, E], BF16)
        rwT = sb("rwT", [3 * E, B, T], BF16)
        a_max = sb("a_max", [P, K])
        a_nmax = sb("a_nmax", [P, K])
        a_sum = sb("a_sum", [P, K])
        a_rec = sb("a_rec", [P, K])

        ap_ = e_dt[:].rearrange("p b h t -> p (b h) t")
        apT = log_dt[:].rearrange("p b h t -> p (b h) t")
        inter = states[:].rearrange("p i h t -> p (i h) t")
        xe = prod[:].rearrange("p i h t -> p (i h) t")
        hs = du[:, 0].rearrange("p h (k c) -> p h k c", c=C)
        hx = du[:, 1].rearrange("p h (k c) -> p h k c", c=C)
        x3p = delta[:, 0].rearrange("p h (k c) -> p h k c", c=C)
        x3 = delta[:, 1].rearrange("p h (k c) -> p h k c", c=C)
        x1T = xT
        gT = r_dt[:, 0]
        aqT = zT[:, 0]
        akT = zT[:, 1]
        av = uT[:, 0].rearrange("p h (k c) -> p h k c", c=C)
        attnT = uT[:, 1]
        nT = decay[:, 0]
        nsq = decay[:, 1]
        x1p = xsT[:].rearrange("p b h t -> p (b h t)")[:, 0:B * T].rearrange("p (b k c) -> p b k c", b=B, c=C)
        x2p = xsT[:].rearrange("p b h t -> p (b h t)")[:, B * T:2 * B * T].rearrange("p (b k c) -> p b k c", b=B, c=C)
        xs_masked = delta[:].rearrange("p b h t -> p (b h t)")[:, 0:FLAT]
        xpT = [du[:].rearrange("p b h t -> p (b h t)")[:, 0:CH * P].rearrange("p (j t) -> p j t", t=P), xpT_odd[:]]
        x2 = x
        dt_raw = prod[0:DTR, 0]
        bc_rest = d_bu[:, 0, :]
        nrm = conv_k[:].rearrange("p a o -> p (a o)").rearrange("p (b k c) -> p b k c", b=B, c=C)
        pairtok = xp[0:S2].rearrange("p i n -> p (i n)")[:, 0:PAIR_COLS]
        qT = [w_in[:], c_rep[:, 1, :]]
        bu_bufs = [d_bu[:]] + [buf.rearrange("p (h t) -> p h t", h=HV) for buf in (
            xp[:].rearrange("p i n -> p (i n)")[:, PAIR_COLS:PAIR_COLS + HV * T],
            conv_k[:].rearrange("p a o -> p (a o)"),
            xsT[:].rearrange("p b h t -> p (b h t)")[:, HV * T:2 * HV * T])]
        pair_of_head = cst("pairhead").rearrange("p (j h) -> p j h", h=HC)
        SCALE_X = float(HD) ** -0.5
        SCALE_A = float(P) ** -0.5

        H_BANKS = (3, 4, 5, 6)

        def x_bank(i):
            return 0 if i % 2 else 3

        def dbc_bank(b):
            return 5 if b else 0

        def dt_bank(b, h):
            return (2 + h, 4 - h)[b]

        def xav_bank(i):
            return 0 if i == K * B - 1 else 6

        def a_bank(b, i):
            return (0, 1, 0, 1)[i] if b == 0 else (2, 3, 5, 6)[i]

        def att_bank(b):
            return 4 if b else 7

        def product_bank(m):
            return m % 2 if m < E else m % 3

        ld = {n: sem("ld_" + n) for n in ("x0", "x1", "win", "conv", "small", "ctx", "masks", "qkv", "o", "moe")}
        s = {n: sem(n) for n in (
            "xT_psum", "xT_ready", "win_psum", "xs_ready", "z_ready", "conv_psum", "u_ready", "dbc_psum",
            "dtraw_ready", "bc_ready", "wdt_psum", "e_ready", "ecap_ready", "rdt_ready", "w_ready", "log_ready",
            "delta_ready", "fills_ready", "warm_ready", "sel_ready", "diag_ready", "nega_ready", "b_psum", "c_psum",
            "dbu_done", "decay_ready", "scan_done", "crep_ready", "prod_done", "sum_done", "g_ready", "wout_psum",
            "dve_chain", "var_ready", "rstd_ready", "x1_ready", "x1T_psum", "x1T_ready", "q_psum", "qT_ready",
            "ctxT_psum", "ctxT_ready", "kv_psum", "kv_ready", "vrep_psum", "kdiag_ready", "vdiag_ready",
            "masks_ready", "masksmall_ready", "xs_psum", "xsub_done", "xexp_done", "xpT_psum", "xpT_ready",
            "xav_psum", "x2p_ready", "nrm_ready", "nT_psum", "nT_ready", "nsq_ready", "logit_psum", "norm_ready",
            "rnorm_ready", "gshift_ready", "gexp_ready", "rwparts_ready", "rwT_psum", "rwT_ready", "simsq_ready",
            "simss_psum", "simss_ready", "simrn_ready", "simn_ready", "gexpneg_ready", "gates_ready", "rwb_psum",
            "xe_ready", "xe_used", "qkv_ready", "q_k_psum", "as_psum", "amax_ready", "aexp_done", "ap_ready",
            "apT_psum", "apT_ready", "att_psum", "att_ready", "down_psum", "acc_done", "h_psum", "inter_ready",
            "hx_ready", "x3_ready", "stored", "expa_ready")}

        block = ctx.enter_context(nc.Block())

        @block.sync
        def _(sp):
            cc = a["consts"]
            sp.dma_start(x[:, 0], a["x"][0].rearrange("(k p) c -> p k c", p=P)).then_inc(ld["x0"], 16)
            sp.dma_start(const[:, 0:CONST_FIRST], cc[:, 0:CONST_FIRST]).then_inc(ld["x0"], 16)
            sp.dma_start(w_in[:], a["L0_attn_W_in"]).then_inc(ld["win"], 16)
            sp.dma_start(x[:, 1], a["x"][1].rearrange("(k p) c -> p k c", p=P)).then_inc(ld["x1"], 16)
            sp.dma_start(conv_k[:], a["L0_attn_conv_k"].rearrange("k i o -> i k o")).then_inc(ld["conv"], 16)
            sp.dma_start(small[:], a["small"]).then_inc(ld["conv"], 16)
            sp.dma_start(w_x[:], a["L0_attn_W_x"].rearrange("(h p) n -> p h n", p=P)).then_inc(ld["small"], 16)
            sp.dma_start(w_dt[:], a["L0_attn_W_dt"]).then_inc(ld["small"], 16)
            sp.dma_start(w_out[:], a["L0_attn_W_out"].rearrange("(h p) n -> p h n", p=P)).then_inc(ld["small"], 16)
            sp.dma_start(const[:, CONST_FIRST:], cc[:, CONST_FIRST:CONST_COLS - PAIR_COLS]).then_inc(ld["masks"], 16)
            sp.dma_start(pairtok, cc[0:S2, CONST_COLS - PAIR_COLS:]).then_inc(ld["ctx"], 16)
            sp.dma_start(mask_i[:], a["mask_BxS2_ik0"].rearrange("(a b) n -> a b n", a=1)).then_inc(ld["masks"], 16)
            sp.dma_start(ctx_sb[:], a["ctx_1024"].rearrange("b n c -> n b c")).then_inc(ld["ctx"], 16)
            for dst, name in ((wq, "Wq"), (wk, "Wk"), (wv, "Wv")):
                sp.dma_start(dst[:], a["L0_xattn_" + name]).then_inc(ld["ctx"], 16)
            for dst, name, n in ((w_q, "q_proj", "qkv"), (w_k, "k_proj", "qkv"), (w_v, "v_proj", "qkv"),
                                 (w_o, "o_proj", "o"), (w_1, "w1", "moe"), (w_2, "w2", "moe")):
                sp.dma_start(dst[:], a["L0_ffn_" + name].rearrange("e i o -> i e o")).then_inc(ld[n], 16)
            sp.wait_ge(s["masksmall_ready"], 1)
            sp.wait_ge(s["fills_ready"], 5)
            for part in range(0, 96, 32):
                for b in range(B):
                    sp.dma_start(mask_parts[part:part + 1, b, :].rearrange("p (h t) -> p h t", h=NH),
                                 mask_small[part:part + 1, b, :].unsqueeze(1).to_broadcast([1, NH, S2])
                                 ).then_inc(s["masks_ready"], 16)
            for b in range(B):
                sp.wait_ge(s["x3_ready"], b + 1)
                sp.dma_start(out[b].rearrange("(k p) c -> p k c", p=P), x3[:, b]).then_inc(s["stored"], 16)
            sp.wait_ge(s["stored"], 16 * B)

        @block.tensor
        def _(pe):
            def transposes(dst, src):
                for k in range(K):
                    last = pe.transpose(dst[:, P * k:P * k + P], src[:, k, :], ident)
                return last

            def x_transposes_in(b):
                pe.wait_ge(ld["x1"] if b else ld["x0"], 16 if b else 32)
                transposes(bank(b), x[:, b]).then_inc(s["xT_psum"], 1)

            def context_t():
                pe.wait_ge(ld["ctx"], 80)
                for b in range(B):
                    pe.wait_ge(s["xT_ready"], b + 1)
                    pe.transpose(ps[:, b, 0:S2], ctx_sb[:, b, :], ident[0:S2, 0:S2]).then_inc(s["ctxT_psum"], 1)

            def project_in(b):
                pe.wait_ge(s["xT_ready"], b + 1)
                for j in range(2 * HV):
                    if b:
                        pe.wait_ge(s["xs_ready"] if j < HV else s["z_ready"], j % HV + 1)
                    pe.matmul(bank(2 + j), w_in[:, P * j:P * j + P], xT[:, b, :], start=True,
                              stop=True).then_inc(s["win_psum"], 1)

            def context_kv():
                for b in range(B):
                    pe.wait_ge(s["ctxT_ready"], b + 1)
                    pe.matmul(ps[:, b, 128:128 + S2], wk[:], ctxT[:, b, :], start=True, stop=True)
                    pe.matmul(ps[0:S2, b, 256:256 + P], ctxT[:, b, :], wv[:], start=True,
                              stop=True).then_inc(s["kv_psum"], 1)

            def convolve(b, groups=range(HV)):
                for g in groups:
                    pe.wait_ge(s["xs_ready"], HV * b + g + 1)
                    if b:
                        pe.wait_ge(s["u_ready"], g + 1)
                    for t in range(TAPS):
                        mm = pe.matmul(bank(6 + g), conv_k[:, t, P * g:P * g + P], xsT[:, b, g, t:t + T],
                                       start=(t == 0), stop=(t == TAPS - 1))
                    mm.then_inc(s["conv_psum"], 1)

            def project_dbc(b):
                pe.wait_ge(s["u_ready"], HV * (b + 1))
                if b:
                    pe.wait_ge(s["z_ready"], HV * B)
                else:
                    pe.wait_ge(s["kv_ready"], 2)
                for h in range(HV):
                    mm = pe.matmul(bank(dbc_bank(b), 96), w_x[:, h, :], uT[:, b, h, :], start=(h == 0), stop=(h == HV - 1))
                mm.then_inc(s["dbc_psum"], 1)

            def project_dt(b):
                pe.wait_ge(s["dtraw_ready"], b + 1)
                for h in range(HV):
                    pe.matmul(bank(dt_bank(b, h)), w_dt[:, P * h:P * h + P], dt_raw[:, b, :], start=True,
                              stop=True).then_inc(s["wdt_psum"], 1)

            def skip_term(b, start):
                for h in range(HV):
                    pe.matmul(bank(6 + h), diag_d[:, h, :], uT[:, b, h, :], start=start, stop=False,
                              skip_group_check=True)

            def spread_values():
                pe.wait_ge(s["bc_ready"], B)
                for j in range(CH):
                    h0, at = chunk(j)[0], B * HC * HD * j
                    mm = pe.matmul(ps[:, 5, at:at + B * HC * HD], pairtok[:, P * j:P * j + P],
                                   v_sb[:, :, HD * h0:HD * (h0 + HC)], start=True, stop=True)
                mm.then_inc(s["vrep_psum"], 1)

            def warm_up(n):
                for _ in range(n):
                    pe.matmul(ps[:, 7, 0:P], ones_bf[:], ones_bf[:], start=True, stop=True)

            pe.wait_ge(s["warm_ready"], 1)
            warm_up(26)
            x_transposes_in(0)
            warm_up(10)
            pe.wait_ge(ld["win"], 16)
            project_in(0)
            x_transposes_in(1)
            pe.wait_ge(ld["conv"], 32)
            pe.wait_ge(s["fills_ready"], 5)
            convolve(0)
            context_t()
            project_in(1)
            context_kv()
            pe.wait_ge(ld["small"], 48)
            pe.wait_ge(s["simsq_ready"], 1)
            pe.wait_ge(s["xs_ready"], HV + 1)
            pe.matmul(ps[:, 2, 0:2 * E], ones[:], sim_sq[:, :, :].rearrange("p n e -> p (n e)"), start=True,
                      stop=True).then_inc(s["simss_psum"], 1)
            project_dbc(0)
            convolve(1, [0])
            pe.wait_ge(s["simss_ready"], 1)
            pe.wait_ge(s["xs_ready"], HV * B)
            project_dt(0)
            convolve(1, [1])

            def spread_b(b, n, j):
                g = NS * b + n
                if b or not isinstance(n, int) or n >= 2:
                    pe.wait_ge(s["dbu_done"], g - 1)
                pe.matmul(bank(j % 2), sel32[:, n, :], bc_parts[:, b, :], start=True, stop=True).then_inc(s["b_psum"], 1)

            def spread_c(b, n):
                g = NS * b + n
                if b or not isinstance(n, int) or n >= 1:
                    pe.wait_ge(s["crep_ready"], g)
                pe.matmul(bank(2), sel32[:, NS:2 * NS, :][:, n, :], bc_parts[:, b, :], start=True,
                          stop=True).then_inc(s["c_psum"], 1)

            def add_state(b, n, j, start=False, stop=False):
                pe.wait_ge(s["prod_done"], NS * b + n + 1)
                for h in range(HV):
                    mm = pe.matmul(bank(6 + h), ident, prod[:, j % 2, h, :], start=start, stop=stop,
                                   skip_group_check=True)
                mm.then_inc(s["sum_done"], 1)

            def project_out(b, blocks=range(K)):
                pe.wait_ge(s["g_ready"], HV * (b + 1))
                pe.wait_ge(s["e_ready"], HV * B)
                for k in blocks:
                    for h in range(HV):
                        mm = pe.matmul(ps[:, 3 + 4 * b, P * k:P * k + P], gT[:, h, P * k:P * k + P], w_out[:, h, :],
                                       start=(h == 0), stop=(h == HV - 1))
                if k == K - 1:
                    mm.then_inc(s["wout_psum"], 1)

            def x1_transposes(b):
                pe.wait_ge(s["x1_ready"], b + 1)
                transposes(bank(3 + 4 * b), x1[:, b]).then_inc(s["x1T_psum"], 1)

            def x_query(b):
                pe.wait_ge(s["x1T_ready"], b + 1)
                pe.matmul(bank(3 + 4 * b), wq[:], x1T[:, b, :], start=True, stop=True).then_inc(s["q_psum"], 1)

            pe.wait_ge(s["bc_ready"], 1)
            pe.wait_ge(s["e_ready"], 1)
            pe.wait_ge(s["sel_ready"], 4)
            spread_b(0, 0, 0)
            spread_c(0, 0)
            pe.wait_ge(s["kv_ready"], 2 * B)
            spread_b(0, 1, 1)
            project_dbc(1)
            pe.wait_ge(s["diag_ready"], HV)
            skip_term(0, start=True)
            spread_c(0, 1)
            spread_b(0, 2, 2)
            pe.wait_ge(s["e_ready"], HV)
            project_dt(1)
            for n in range(2):
                spread_b(0, n + 3, n + 3)
                spread_c(0, n + 2)
                if n == 1:
                    spread_values()
                add_state(0, n, n)
            with pe.Fori(1, (NS - U) // 2) as i:
                for j in range(2):
                    spread_b(0, i * 2 + (3 + j), 3 + j)
                    spread_c(0, i * 2 + (2 + j))
                    add_state(0, i * 2 + j, j)
            for n in range(NS - U, NS):
                spread_b((n + 3) // NS, (n + 3) % NS, n + 3)
                spread_c((n + 2) // NS, (n + 2) % NS)
                add_state(0, n, n, stop=(n == NS - 1))
            rows_before = {0: [(3, 2), (4, 3)], 1: [(5, None)], 2: [(6, 4)], 3: [(None, 5)]}
            for n in range(2 * U):
                for b_row, c_row in rows_before.get(n, [(n + 3, n + 2)]):
                    if b_row is not None:
                        spread_b(1, b_row, b_row)
                    if c_row is not None:
                        spread_c(1, c_row)
                if n == 0:
                    pe.wait_ge(s["g_ready"], HV)
                if n in (2, 3):
                    project_out(0, range(2 * n - 4, 2 * n - 2))
                add_state(1, n, n, start=(n == 0))
                if n == 6:
                    skip_term(1, start=False)
                if n == 2 * U - 1:
                    x1_transposes(0)
            with pe.Fori(U, (NS - U) // 2) as i:
                for j in range(2):
                    spread_b(1, i * 2 + (3 + j), 3 + j)
                    spread_c(1, i * 2 + (2 + j))
                    add_state(1, i * 2 + j, j)

            def x_scores(i):
                b, k = divmod(i, K)
                pe.wait_ge(s["qT_ready"], b + 1)
                if i >= 2:
                    pe.wait_ge(s["xpT_ready"], i - 1)
                elif i == 1:
                    pe.wait_ge(s["dbu_done"], NS * B)
                    pe.wait_ge(s["crep_ready"], NS * B)
                for c in range(0, FLAT, 512):
                    w = min(512, FLAT - c)
                    at = x_bank(i) + c // 512
                    pe.matmul(ps[:, at, 0:w], qT[b][:, P * k:P * k + P], k_diag[:, b, c:c + w],
                              start=True, stop=False)
                    mm = pe.matmul(ps[:, at, 0:w], ones_bf[:], mask_parts[:, b, c:c + w],
                                   start=False, stop=True)
                mm.then_inc(s["xs_psum"], 1)

            def x_transposes(i):
                pe.wait_ge(s["xexp_done"], i + 1)
                for j in range(CH):
                    rows = chunk(j)[1]
                    mm = pe.transpose(ps[0:rows, x_bank(i) + j // 4, P * (j % 4):P * (j % 4) + P],
                                      xp[:, i % 2, P * j:P * j + rows], ident)
                mm.then_inc(s["xpT_psum"], 1)

            def x_values(i, chunks=range(CH)):
                b = i // K
                pe.wait_ge(s["xpT_ready"], i + 1)
                if 0 < i < K * B - 1:
                    pe.wait_ge(s["x2p_ready"], i)
                for j in chunks:
                    h0, rows = chunk(j)
                    mm = pe.matmul(ps[:, xav_bank(i), HD1 * h0:HD1 * (h0 + HC)], xpT[i % 2][0:rows, j, :],
                                   v_diag[0:rows, b, j, :], start=(j == 0), stop=True, skip_group_check=True)
                if j == CH - 1:
                    mm.then_inc(s["xav_psum"], 1)

            def n_transposes(n, b):
                m = 2 * n + b
                pe.wait_ge(s["nrm_ready"], m + 1)
                if m == 1:
                    pe.wait_ge(s["rwT_ready"], 1)
                if m == 2:
                    pe.wait_ge(s["att_ready"], 1)
                if m == 3:
                    pe.wait_ge(s["gshift_ready"], m)
                transposes(bank(7), nrm[:, b]).then_inc(s["nT_psum"], 1)

            def logits(n, b):
                m = 2 * n + b
                pe.wait_ge(s["nsq_ready"], m + 1)
                pe.wait_ge(s["simn_ready"], 1)
                for k in range(K):
                    pe.matmul(ps[:, 7, 9 * k:9 * k + E], nT[:, b, P * k:P * k + P], simn[:, n, :], start=True, stop=True)
                    mm = pe.matmul(ps[:, 7, 9 * k + E:9 * k + 9], nsq[:, b, P * k:P * k + P], ones[:, 0:1],
                                   start=True, stop=True)
                mm.then_inc(s["logit_psum"], 1)

            def weights_t(b):
                pe.wait_ge(s["rwparts_ready"], b + 1)
                for k in range(K):
                    mm = pe.transpose(ps[0:3 * E, 7, :].bitcast(BF16)[:, P * k:P * k + P],
                                      rw_parts[:, k, :, :].rearrange("p t e -> p (t e)"), ident_bf[:])
                mm.then_inc(s["rwT_psum"], 1)

            for n in range(NS - U, NS):
                if n + 3 < NS:
                    spread_b(1, n + 3, n + 3)
                if n + 2 < NS:
                    spread_c(1, n + 2)
                if n == NS - U:
                    x_query(0)
                add_state(1, n, n, stop=(n == NS - 1))
                if n == NS - 3:
                    pe.wait_ge(s["kdiag_ready"], B)
                    pe.wait_ge(s["vdiag_ready"], B + 1)
                    pe.wait_ge(s["masks_ready"], 16 * 3 * B)
                    x_scores(0)
            for i in range(1, K * B + 1):
                if i < K * B:
                    x_scores(i)
                if i == 1:
                    project_out(1)
                if i == 2:
                    x1_transposes(1)
                if i == K + 3:
                    n_transposes(0, 0)
                x_transposes(i - 1)
                if i >= 2:
                    x_values(i - 2)
                if i == 2:
                    x_query(1)
                if i == K + 3:
                    logits(0, 0)
            weights_t(0)

            def spread_qkv(g):
                pe.wait_ge(s["rwT_ready"], g // E + 1)
                if g >= 2:
                    pe.wait_ge(s["xe_ready"], g - 1)
                pe.matmul(bank(2 + g % 2), sel8[:, g % E, :], rwT[:, g // E, :], start=True,
                          stop=True).then_inc(s["rwb_psum"], 1)

            x_values(K * B - 1, range(CH // 2))
            spread_qkv(0)
            x_values(K * B - 1, range(CH // 2, CH))
            pe.wait_ge(ld["qkv"], 48)

            def qkv(b, e):
                g = E * b + e
                pe.wait_ge(s["xe_ready"], g + 1)
                st, sp_ = e == 0, e == E - 1
                if b and st:
                    pe.wait_ge(s["qkv_ready"], 1)
                mm = pe.matmul(bank(4), w_q[:, e, :], xe[:, g % 4, :], start=st, stop=sp_)
                if sp_:
                    mm.then_inc(s["q_k_psum"], 1)
                if b and st:
                    pe.wait_ge(s["qkv_ready"], 2)
                mm = pe.matmul(bank(5), w_k[:, e, :], xe[:, g % 4, :], start=st, stop=sp_)
                if sp_:
                    mm.then_inc(s["q_k_psum"], 1)
                if st:
                    pe.wait_ge(s["qkv_ready"] if b else s["x2p_ready"], 3 if b else K * B - 1)
                for k in range(K):
                    mm = pe.matmul(ps[:, 6, P * k:P * k + P], xe[:, g % 4, P * k:P * k + P], w_v[:, e, :],
                                   start=(st and k == 0), stop=sp_, skip_group_check=True)
                mm.then_inc(s["xe_used"], 1)

            def project_qkv(b, between):
                for e in range(E):
                    if E * b + e + 1 < E * B:
                        spread_qkv(E * b + e + 1)
                    qkv(b, e)
                    if e in between:
                        between[e]()

            def a_scores(b, i):
                pe.wait_ge(s["qkv_ready"], 3 * (b + 1))
                if b == 0 and i >= 2:
                    pe.wait_ge(s["apT_ready"], i - 1)
                if b and i < 2:
                    pe.wait_ge(s["xe_ready"], E * B)
                w = P * (i + 1)
                at = a_bank(b, i)
                pe.matmul(ps[:, at, 0:w], aqT[:, b, P * i:P * i + P], akT[:, b, 0:w], start=True, stop=True)
                pe.matmul(ps[:, at, w - P:w], ident_bf[:], causal_bf[:], start=False, stop=True,
                          skip_group_check=True).then_inc(s["as_psum"], 1)

            def a_transposes(b, i):
                pe.wait_ge(s["ap_ready"], K * b + i + 1)
                for j in range(i + 1):
                    mm = pe.transpose(ps[:, a_bank(b, i), P * j:P * j + P], ap_[:, i, P * j:P * j + P], ident)
                mm.then_inc(s["apT_psum"], 1)

            def a_values(b, i):
                pe.wait_ge(s["apT_ready"], K * b + i + 1)
                if b == 0:
                    pe.wait_ge(s["rwT_ready"], B)
                for j in range(i + 1):
                    mm = pe.matmul(ps[:, att_bank(b), P * i:P * i + P], av[:, b, j, :], apT[:, i, P * j:P * j + P],
                                   start=(j == 0), stop=(j == i), skip_group_check=True)
                mm.then_inc(s["att_psum"], 1)

            def attend(b, *steps):
                for what, i in steps:
                    what(b, i)

            S_, T_, V_ = a_scores, a_transposes, a_values
            def product_of(m, left, right):
                if m >= 2:
                    pe.wait_ge(s["acc_done"], K * (m - 1 if m < E else m - 2))
                for k in range(K):
                    mm = pe.matmul(ps[:, product_bank(m), P * k:P * k + P], left[:, P * k:P * k + P], right,
                                   start=(k == 0), stop=True, skip_group_check=True)
                mm.then_inc(s["down_psum"], 1)

            def project_o(b, *experts):
                if experts[0] == 0:
                    pe.wait_ge(ld["o"], 16)
                    pe.wait_ge(s["att_ready"], b + 1)
                for e in experts:
                    product_of(E * b + e, attnT[:, b, :], w_o[:, e, :])

            project_qkv(0, {0: lambda: n_transposes(0, 1), 2: lambda: logits(0, 1), 6: lambda: weights_t(1)})
            project_qkv(1, {0: lambda: attend(0, (S_, 0), (S_, 1)), 1: lambda: attend(0, (T_, 0), (T_, 1)),
                            2: lambda: attend(0, (V_, 0), (V_, 1), (S_, 2), (S_, 3)),
                            3: lambda: attend(0, (T_, 2), (T_, 3)), 4: lambda: attend(0, (V_, 2), (V_, 3)),
                            5: lambda: project_o(0, 0, 1), 6: lambda: project_o(0, 2, 3), 7: lambda: project_o(0, 4, 5)})
            attend(1, (S_, 0), (S_, 1), (S_, 2), (S_, 3))
            project_o(0, 6, 7)
            attend(1, (T_, 0), (T_, 1), (T_, 2), (T_, 3), (V_, 0), (V_, 1), (V_, 2), (V_, 3))
            project_o(1, 0, 1, 2, 3)
            n_transposes(1, 0)

            def moe_up(g):
                b, e = divmod(g, E)
                pe.wait_ge(s["nT_ready"], B + b + 1)
                if g >= 4:
                    pe.wait_ge(s["inter_ready"], g - 3)
                else:
                    pe.wait_ge(s["att_ready"], B)
                pe.matmul(bank(H_BANKS[g % 4]), w_1[:, e, :], nT[:, b, :], start=True, stop=True).then_inc(s["h_psum"], 1)

            def moe_down(g):
                pe.wait_ge(s["inter_ready"], g + 1)
                product_of(E * B + g, inter[:, g % 4, :], w_2[:, g % E, :])

            pe.wait_ge(ld["moe"], 32)
            for g in range(4):
                project_o(1, 4 + g)
                moe_up(g)
                if g == 0:
                    logits(1, 0)
            for g in range(E * B):
                moe_down(g)
                if g + 4 < E * B:
                    moe_up(g + 4)
                if g == 2:
                    n_transposes(1, 1)
                if g == 4:
                    logits(1, 1)

        @block.vector
        def _(dve):
            chain = [0]

            def link(ins, meanwhile=None):
                chain[0] += 1
                ins.then_inc(s["dve_chain"], 1)
                if meanwhile:
                    meanwhile()
                dve.wait_ge(s["dve_chain"], chain[0])

            def nothing(k):
                return None

            def x_take(b):
                dve.wait_ge(s["xT_psum"], b + 1)
                dve.tensor_copy(xT[:, b, :], bank(b)).then_inc(s["xT_ready"], 1)

            def conv_input(b):
                for g in range(HV):
                    dve.wait_ge(s["win_psum"], 2 * HV * b + g + 1)
                    dve.tensor_copy(xsT[:, b, g, TAPS - 1:], bank(2 + g)).then_inc(s["xs_ready"], 1)

            x_take(0)
            conv_input(0)
            x_take(1)
            dve.wait_ge(ld["masks"], 32)
            dve.tensor_copy(sel32[:], cst("sel32", 96).unsqueeze(2).to_broadcast([96, 32, P])).then_inc(s["sel_ready"], 1)
            dve.wait_ge(ld["conv"], 32)
            dve.tensor_tensor(sim_sq[:], sim, sim, ALU.mult).then_inc(s["simsq_ready"], 1)
            conv_input(1)
            for h in range(HV):
                dve.tensor_scalar(diag_d[:, h, :], ident, skip_d[:, h:h + 1], None, ALU.mult).then_inc(s["diag_ready"], 1)
            link(dve.tensor_copy(mask_f[:], mask_i[:]))
            link(dve.tensor_scalar(mask_f[:], mask_f[:], -1.0, NEG, ALU.add, ALU.mult))
            link(dve.tensor_copy(mask_small[0:1], mask_f[:]))
            link(dve.tensor_tensor(mask_rest[32:33], mask_f[:], mask_small[0:1], ALU.subtract))
            link(dve.tensor_copy(mask_small[32:33], mask_rest[32:33]))
            dve.tensor_tensor(mask_small[64:65], mask_rest[32:33], mask_small[32:33],
                              ALU.subtract).then_inc(s["masksmall_ready"], 1)
            def take_dbc(b):
                dve.wait_ge(s["dbc_psum"], b + 1)
                dve.tensor_copy(dt_raw[:, b, :], bank(dbc_bank(b))[0:DTR]).then_inc(s["dtraw_ready"], 1)
                bc = bank(dbc_bank(b))[DTR:96]
                link(dve.tensor_copy(bc_parts[0:32, b, :], bc))
                link(dve.tensor_tensor(bc_rest[32:64, :], bc, bc_parts[0:32, b, :], ALU.subtract))
                link(dve.tensor_copy(bc_parts[32:64, b, :], bc_rest[32:64, :]))
                dve.tensor_tensor(bc_parts[64:96, b, :], bc_rest[32:64, :], bc_parts[32:64, b, :],
                                  ALU.subtract).then_inc(s["bc_ready"], 1)

            def cap(b):
                dve.wait_ge(s["e_ready"], HV * (b + 1))
                dve.tensor_scalar(e_dt[:, b], e_dt[:, b], SOFTPLUS_CAP, None, ALU.min).then_inc(s["ecap_ready"], 1)

            def rounded(b):
                dve.wait_ge(s["ecap_ready"], b + 1)
                dve.tensor_scalar(r_dt[:, b], e_dt[:, b], 1.0, -1.0, ALU.add, ALU.add).then_inc(s["w_ready"], 1)

            def step_sizes(b):
                dve.wait_ge(s["log_ready"], b + 1)
                if b:
                    dve.wait_ge(s["rdt_ready"], 1)
                link(dve.tensor_tensor(log_dt[:, b], log_dt[:, b], r_dt[:, b], ALU.add))
                dve.tensor_scalar(delta[:, b], log_dt[:, b], DT_MIN, DT_MAX, ALU.max, ALU.min).then_inc(s["delta_ready"], 1)

            def steps_times_u(b):
                dve.wait_ge(s["delta_ready"], b + 1)
                link(dve.tensor_tensor(du[:, b], delta[:, b], uT[:, b], ALU.mult))

            take_dbc(0)
            dve.wait_ge(s["simss_psum"], 1)
            dve.tensor_scalar(sim_ss[:].rearrange("p n e -> p (n e)"), ps[:, 2, 0:2 * E], 1e-24, None,
                              ALU.max).then_inc(s["simss_ready"], 1)
            dve.wait_ge(s["expa_ready"], 1)
            dve.tensor_scalar(neg_a[:], exp_a[:], -1.0, None, ALU.mult).then_inc(s["nega_ready"], 1)
            dve.wait_ge(s["gexpneg_ready"], 1)
            link(dve.tensor_scalar(gate_s[:], gate_s[:], 1.0, None, ALU.add))
            dve.reciprocal(gates[:], gate_s[:]).then_inc(s["gates_ready"], 1)
            cap(0)
            rounded(0)
            dve.wait_ge(s["w_ready"], 1)
            link(dve.tensor_tensor(r_dt[:, 0], e_dt[:, 0], r_dt[:, 0], ALU.subtract))
            step_sizes(0)
            steps_times_u(0)

            def scan_input(b, n, j):
                g = NS * b + n
                dve.wait_ge(s["b_psum"], g + 1)
                if b or not isinstance(n, int) or n >= len(bu_bufs):
                    dve.wait_ge(s["scan_done"], g - 3)
                dve.tensor_tensor(bu_bufs[j % 4], du[:, b], bank(j % 2).unsqueeze(1).to_broadcast([P, HV, T]),
                                  ALU.mult).then_inc(s["dbu_done"], 1)

            def scan(g, j):
                dve.wait_ge(s["dbu_done"], g + 1)
                dve.wait_ge(s["decay_ready"], 2 * g + 2)
                if not isinstance(g, int) or g >= 2:
                    dve.wait_ge(s["prod_done"], g - 1)
                dve.tensor_tensor_scan(states[:, j % 2].rearrange("p h t -> p (h t)"),
                                       decay[:, j % 2].rearrange("p h t -> p (h t)"),
                                       bu_bufs[j % 4].rearrange("p h t -> p (h t)"), 0.0, ALU.mult,
                                       ALU.add).then_inc(s["scan_done"], 1)

            def gated(b):
                dve.wait_ge(s["sum_done"], NS * (b + 1))
                if b:
                    dve.wait_ge(s["wout_psum"], 1)
                for h in range(HV):
                    dve.tensor_tensor(gT[:, h, :], zT[:, b, h, :], bank(6 + h), ALU.mult).then_inc(s["g_ready"], 1)

            roots = [0]

            def norm_stats(src, n=1):
                for k in range(K):
                    last = dve.bn_stats(stats[:, k, :], src[:, k, :])
                link(last)
                for k in range(K):
                    last = dve.bn_aggr(mv[:, k, :], stats[:, k, :])
                link(last)
                if n == 2:
                    dve.tensor_scalar(var_eps[:, K:], mv[:, :, 1], 1.0 + LN_EPS, LN_EPS ** 2, ALU.mult, ALU.add)
                dve.tensor_scalar(var_eps[:, 0:K], mv[:, :, 1], LN_EPS, None, ALU.add).then_inc(s["var_ready"], 1)
                roots[0] += 1

            def norm_apply(dst, src, ready, twice=0):
                dve.wait_ge(s["rstd_ready"], roots[0])
                for k in range(K):
                    last = dve.tensor_scalar(dst[:, k, :], src[:, k, :], mv[:, k, 0:1],
                                             rstd[:, K * twice + k:K * twice + k + 1], ALU.subtract, ALU.mult)
                if ready:
                    last.then_inc(s[ready], 1)

            def mixer_residual(b):
                dve.wait_ge(s["wout_psum"], b + 1)
                link(dve.tensor_tensor(x1p[:, b].rearrange("p k c -> p (k c)"), x[:, b].rearrange("p k c -> p (k c)"),
                                       bank(3 + 4 * b), ALU.add))
                norm_stats(x1p[:, b])

            for n in range(2 * U):
                scan_input(0, n, n)
                if n:
                    scan(n - 1, n - 1)
                if n == 1:
                    dve.wait_ge(s["scan_done"], 1)
                    take_dbc(1)
                    dve.wait_ge(s["bc_ready"], B)
                if n == 2:
                    cap(1)
                    rounded(1)
                if n == 4:
                    dve.wait_ge(s["vrep_psum"], 1)
                    got_v = ps[:, 5, 0:CH * B * HC * HD].rearrange("p (j b h d) -> p j b h d", b=B, h=HC, d=HD)
                    for b in range(B):
                        dve.tensor_tensor(v_diag[:, b].rearrange("p j (h d) -> p j h d", d=HD1)[:, :, :, 0:HD],
                                          got_v[:, :, b], pair_of_head.unsqueeze(3).to_broadcast([P, CH, HC, HD]),
                                          ALU.mult).then_inc(s["vdiag_ready"], 1)
                    dve.tensor_copy(v_diag[:].rearrange("p b j (h d) -> p b (j h) d", d=HD1)[:, :, :, HD],
                                    cst("pairhead").unsqueeze(1).to_broadcast([P, B, CH * HC])).then_inc(s["vdiag_ready"], 1)
                    dve.wait_ge(s["simrn_ready"], 1)
                    dve.tensor_tensor(simn[:], sim, sim_rn[:], ALU.mult).then_inc(s["simn_ready"], 1)
                if n == 5:
                    step_sizes(1)
                if n == 6:
                    steps_times_u(1)
            with dve.Fori(2, NS // U) as i:
                for j in range(U):
                    scan_input(0, i * U + j, j)
                    scan(i * U + (j - 1), (j - 1) % U)
            for n in range(2 * U):
                scan_input(1, n, n)
                scan(NS + n - 1, NS + n - 1)
                if n == 2:
                    gated(0)
                if n == 6:
                    mixer_residual(0)
                if n == 7:
                    norm_apply(x1[:, 0], x1p[:, 0], "x1_ready")
            with dve.Fori(2, NS // U) as i:
                for j in range(U):
                    scan_input(1, i * U + j, j)
                    scan(i * U + (NS + j - 1), (j - 1) % U)
            scan(NS * B - 1, NS * B - 1)

            def x_softmax(i):
                b, k = divmod(i, K)
                dve.wait_ge(s["xs_psum"], i + 1)
                at = x_bank(i)
                scores = ps[:, at:at + 3, :].rearrange("p a n -> p (a n)")[:, 0:FLAT].rearrange("p (h t) -> p h t", h=NH)
                if k == 0:
                    masked = xs_masked.rearrange("p (h t) -> p h t", h=NH)
                    link(dve.tensor_tensor(masked, scores, cst("xcausal").unsqueeze(1).to_broadcast([P, NH, S2]), ALU.add))
                    scores = masked
                link(dve.tensor_reduce(xs_max[:, i % 2], scores, AX_X, ALU.max))
                if i >= 2:
                    dve.wait_ge(s["xpT_psum"], i - 1)
                dve.tensor_tensor(xp[:, i % 2, :].rearrange("p (h t) -> p h t", h=NH), scores,
                                  xs_max[:, i % 2].unsqueeze(2).to_broadcast([P, NH, S2]), ALU.subtract).then_inc(s["xsub_done"], 1)

            def x_finish(i):
                b, k = divmod(i, K)
                dve.wait_ge(s["xav_psum"], i + 1)
                heads = ps[:, xav_bank(i), 0:NH * HD1].rearrange("p (h d) -> p h d", h=NH)
                link(dve.reciprocal(xrec[:], heads[:, :, HD]))
                link(dve.tensor_tensor(xav[:].rearrange("p (h d) -> p h d", h=NH), heads[:, :, 0:HD],
                                       xrec[:].unsqueeze(2).to_broadcast([P, NH, HD]), ALU.mult))
                dve.tensor_tensor(x2p[:, b, k, :], xav[:], x1[:, b, k, :], ALU.add).then_inc(s["x2p_ready"], 1)

            got = ps[:, 7, 0:9 * K].rearrange("p (k e) -> p k e", k=K)

            def gate_norm(n, b):
                dve.wait_ge(s["logit_psum"], 2 * n + b + 1)
                dve.tensor_scalar(g_ss[:], got[:, :, E], 1e-24, None, ALU.max).then_inc(s["norm_ready"], 1)

            def gate_logits(n, b, other_work=nothing):
                dve.wait_ge(s["rnorm_ready"], 2 * n + b + 1)
                link(dve.tensor_tensor(g_l0[:], got[:, :, 0:E], g_rn[:].unsqueeze(2).to_broadcast([P, K, E]), ALU.mult),
                     lambda: other_work(0))
                dve.wait_ge(s["gates_ready"], 1)
                link(dve.tensor_tensor(g_l[:], g_l0[:], gates[:, n, :].unsqueeze(1).to_broadcast([P, K, E]), ALU.subtract),
                     lambda: other_work(1))
                dve.tensor_scalar(g_act[:], g_l[:], 0.0, None, ALU.is_gt)
                link(dve.tensor_scalar(g_relu[:], g_l[:], 0.0, None, ALU.max), lambda: other_work(2))
                link(dve.tensor_reduce(g_max[:], g_relu[:], AX_X, ALU.max), lambda: other_work(3))
                dve.tensor_tensor(g_sh[:], g_relu[:], g_max[:].unsqueeze(2).to_broadcast([P, K, E]),
                                  ALU.subtract).then_inc(s["gshift_ready"], 1)

            def gate_ranks(other_work=nothing):
                other = g_l[:].unsqueeze(2).to_broadcast([P, K, E, E])
                own = g_l[:].unsqueeze(3).to_broadcast([P, K, E, E])
                link(dve.tensor_tensor(g_gt[:], other, own, ALU.subtract), lambda: other_work(0))
                link(dve.tensor_tensor(g_cmp[:].rearrange("p k i j -> p k (i j)"), g_gt[:].rearrange("p k i j -> p k (i j)"),
                                       cst("tri").unsqueeze(1).to_broadcast([P, K, E * E]), ALU.is_gt),
                     lambda: other_work(1))
                link(dve.tensor_reduce(g_rank[:], g_cmp[:], AX_X, ALU.add), lambda: other_work(2))
                dve.tensor_scalar(g_top[:], g_rank[:], 1.5, None, ALU.is_lt)
                link(dve.tensor_scalar(g_idle[:], g_max[:], 0.0, None, ALU.is_le), lambda: other_work(3))
                link(dve.tensor_tensor(g_put[:], g_top[:], g_idle[:].unsqueeze(2).to_broadcast([P, K, E]), ALU.mult))
                link(dve.tensor_tensor(g_mask[:], g_act[:], g_put[:], ALU.max))

            def gate_weights(n, b, other_work=nothing):
                m = 2 * n + b
                dve.wait_ge(s["gexp_ready"], m + 1)
                link(dve.tensor_tensor(g_w[:], g_ex[:], g_mask[:], ALU.mult), lambda: other_work(0))
                link(dve.tensor_reduce(g_sum[:], g_w[:], AX_X, ALU.add), lambda: other_work(1))
                link(dve.reciprocal(g_rs[:], g_sum[:]), lambda: other_work(2))
                link(dve.tensor_tensor(g_rw[:, n, b], g_w[:], g_rs[:].unsqueeze(2).to_broadcast([P, K, E]), ALU.mult),
                     lambda: other_work(3))
                if n:
                    return
                if b:
                    dve.wait_ge(s["rwT_psum"], b)
                link(dve.tensor_copy(rw_parts[:, :, 0, :], g_rw[:, n, b]))
                link(dve.tensor_tensor(g_r1[:], g_rw[:, n, b], rw_parts[:, :, 0, :], ALU.subtract))
                link(dve.tensor_copy(rw_parts[:, :, 1, :], g_r1[:]))
                dve.tensor_tensor(rw_parts[:, :, 2, :], g_r1[:], rw_parts[:, :, 1, :],
                                  ALU.subtract).then_inc(s["rwparts_ready"], 1)

            for i in range(K * B + 1):
                if i >= 3:
                    x_finish(i - 3)
                if i == K + 2:
                    dve.wait_ge(s["x2p_ready"], K)
                    norm_stats(x2p[:, 0], 2)
                if i < K * B:
                    x_softmax(i)
                if i == 0:
                    gated(1)
                if i == 1:
                    mixer_residual(1)
                    norm_apply(x1[:, 1], x1p[:, 1], "x1_ready")
                if i == K + 2:
                    norm_apply(nrm[:, 0], x2p[:, 0], "nrm_ready", twice=1)
                    norm_apply(x2[:, 0], x2p[:, 0], None)
            gate_norm(0, 0)
            gate_logits(0, 0)
            gate_ranks()
            gate_weights(0, 0)
            x_finish(K * B - 2)

            def weigh_qkv(b, e):
                g = E * b + e
                dve.wait_ge(s["rwb_psum"], g + 1)
                dve.wait_ge(s["nT_ready"], b + 1)
                if g >= 4:
                    dve.wait_ge(s["xe_used"], g - 3)
                dve.tensor_tensor(xe[:, g % 4, :], nT[:, b, :], bank(2 + g % 2), ALU.mult).then_inc(s["xe_ready"], 1)

            weigh_qkv(0, 0)
            x_finish(K * B - 1)
            dve.wait_ge(s["x2p_ready"], K * B)
            norm_stats(x2p[:, 1], 2)
            weigh_qkv(0, 1)
            norm_apply(nrm[:, 1], x2p[:, 1], "nrm_ready", twice=1)
            norm_apply(x2[:, 1], x2p[:, 1], None)
            weigh_qkv(0, 2)
            weigh_qkv(0, 3)
            gate_norm(0, 1)
            weigh_qkv(0, 4)
            gate_logits(0, 1)
            weigh_qkv(0, 5)
            gate_ranks()
            weigh_qkv(0, 6)
            gate_weights(0, 1)
            weigh_qkv(0, 7)

            def a_rowmax(b, i):
                dve.wait_ge(s["as_psum"], K * b + i + 1)
                link(dve.tensor_reduce(a_max[:, i:i + 1], ps[:, a_bank(b, i), 0:P * (i + 1)], AX_X, ALU.max))
                dve.tensor_scalar(a_nmax[:, i:i + 1], a_max[:, i:i + 1], -SCALE_A, None, ALU.mult).then_inc(s["amax_ready"], 1)

            def a_normalise(b, i):
                dve.wait_ge(s["aexp_done"], K * b + i + 1)
                link(dve.reciprocal(a_rec[:, i:i + 1], a_sum[:, i:i + 1]))
                w = P * (i + 1)
                dve.tensor_scalar(ap_[:, i, 0:w], ap_[:, i, 0:w], a_rec[:, i:i + 1], None, ALU.mult).then_inc(s["ap_ready"], 1)

            weigh_qkv(1, 0)
            weigh_qkv(1, 1)
            a_rowmax(0, 0)
            a_rowmax(0, 1)
            weigh_qkv(1, 2)
            a_normalise(0, 0)
            a_normalise(0, 1)
            weigh_qkv(1, 3)
            a_rowmax(0, 2)
            a_rowmax(0, 3)
            weigh_qkv(1, 4)
            a_normalise(0, 2)
            a_normalise(0, 3)
            def accumulate_block(n, b, e, k):
                m = E * (B * n + b) + e
                dve.wait_ge(s["down_psum"], m + 1)
                if n and e == 0:
                    dve.wait_ge(s["hx_ready"], b + 1)
                if e:
                    dve.wait_ge(s["acc_done"], K * (m - 1) + k + 1)
                total = x3p if n else hs
                before = total if e else (hx if n else x2)
                dve.scalar_tensor_tensor(total[:, b, k, :], ps[:, product_bank(m), P * k:P * k + P],
                                         g_rw[:, n, b, k, e:e + 1], before[:, b, k, :], ALU.mult,
                                         ALU.add).then_inc(s["acc_done"], 1)

            def accumulate(n, b, e):
                for k in range(K):
                    accumulate_block(n, b, e, k)

            def blocks_of(n, b, e):
                return lambda k: accumulate_block(n, b, e, k)

            def sum_stats(n, b):
                dve.wait_ge(s["acc_done"], K * E * (B * n + b + 1))
                norm_stats((x3p if n else hs)[:, b])

            weigh_qkv(1, 5)
            weigh_qkv(1, 6)
            accumulate(0, 0, 0)
            accumulate(0, 0, 1)
            weigh_qkv(1, 7)
            for e in range(2, 6):
                accumulate(0, 0, e)
            for i in range(K):
                a_rowmax(1, i)
            for i in range(K):
                a_normalise(1, i)
            accumulate(0, 0, 6)
            accumulate(0, 0, 7)
            sum_stats(0, 0)
            accumulate(0, 1, 0)
            norm_apply(nrm[:, 0], hs[:, 0], "nrm_ready")
            for e in range(1, 5):
                accumulate(0, 1, e)
            gate_norm(1, 0)
            accumulate(0, 1, 5)
            gate_logits(1, 0, blocks_of(0, 1, 6))
            gate_ranks(blocks_of(0, 1, 7))
            gate_weights(1, 0)
            sum_stats(0, 1)
            accumulate(1, 0, 0)
            norm_apply(nrm[:, 1], hs[:, 1], "nrm_ready")
            for e in range(1, 4):
                accumulate(1, 0, e)
            accumulate(1, 0, 4)
            gate_norm(1, 1)
            gate_logits(1, 1, blocks_of(1, 0, 5))
            gate_ranks(blocks_of(1, 0, 6))
            gate_weights(1, 1, blocks_of(1, 0, 7))
            sum_stats(1, 0)
            accumulate(1, 1, 0)
            norm_apply(x3[:, 0], x3p[:, 0], "x3_ready")
            for e in range(1, E):
                accumulate(1, 1, e)
            sum_stats(1, 1)
            norm_apply(x3[:, 1], x3p[:, 1], "x3_ready")

        @block.scalar
        def _(act):
            def gate_branch(b):
                for h in range(HV):
                    act.wait_ge(s["win_psum"], 2 * HV * b + HV + h + 1)
                    act.activation(zT[:, b, h, :], bank(2 + HV + h), ACT.Silu).then_inc(s["z_ready"], 1)

            def conv_out(b):
                for g in range(HV):
                    act.wait_ge(s["conv_psum"], HV * b + g + 1)
                    act.activation(uT[:, b, g, :], bank(6 + g), ACT.Silu, bias=conv_b[:, g:g + 1]).then_inc(s["u_ready"], 1)

            gate_branch(0)
            act.wait_ge(ld["conv"], 32)
            conv_out(0)
            for b in range(B):
                act.wait_ge(s["ctxT_psum"], b + 1)
                act.activation(ctxT[:, b, :], ps[:, b, 0:S2], ACT.Copy).then_inc(s["ctxT_ready"], 1)
            gate_branch(1)
            for b in range(B):
                act.wait_ge(s["kv_psum"], b + 1)
                act.activation(kT[:, b, :], ps[:, b, 128:128 + S2], ACT.Copy).then_inc(s["kv_ready"], 1)
                act.activation(v_sb[:, b, :], ps[0:S2, b, 256:256 + P], ACT.Copy).then_inc(s["kv_ready"], 1)
            act.activation(exp_a[:], a_log, ACT.Exp).then_inc(s["expa_ready"], 1)
            act.activation(gate_s[:], gates_in, ACT.Exp, scale=-1.0).then_inc(s["gexpneg_ready"], 1)

            def dt_exp(b):
                for h in range(HV):
                    act.wait_ge(s["wdt_psum"], HV * b + h + 1)
                    act.activation(e_dt[:, b, h, :], bank(dt_bank(b, h)), ACT.Exp, bias=b_dt[:, h:h + 1]).then_inc(s["e_ready"], 1)

            def dt_log(b):
                act.wait_ge(s["ecap_ready"], b + 1)
                act.activation(log_dt[:, b], e_dt[:, b], ACT.Ln, bias=1.0).then_inc(s["log_ready"], 1)

            dt_exp(0)
            dt_log(0)
            conv_out(1)

            def scan_state(b, n, j):
                g = NS * b + n
                if b or not isinstance(n, int) or n >= 2:
                    act.wait_ge(s["scan_done"], g - 1)
                for h in range(HV):
                    if isinstance(n, int):
                        scale = neg_a[:, h, n:n + 1]
                    else:
                        scale = neg_a[:, h, :][:, bass.ds(n, 1)]
                    act.activation(decay[:, j % 2, h, 1:], delta[:, b, h, 1:], ACT.Exp, scale=scale).then_inc(s["decay_ready"], 1)
                act.wait_ge(s["c_psum"], g + 1)
                if b or not isinstance(n, int) or n >= 2:
                    act.wait_ge(s["prod_done"], g - 1)
                act.activation(c_rep[:, j % 2, :], bank(2), ACT.Copy).then_inc(s["crep_ready"], 1)

            def x1T_take(b):
                act.wait_ge(s["x1T_psum"], b + 1)
                act.activation(x1T[:, b, :], bank(3 + 4 * b), ACT.Copy).then_inc(s["x1T_ready"], 1)

            def query_take(b):
                act.wait_ge(s["q_psum"], b + 1)
                if b:
                    act.wait_ge(s["prod_done"], NS * B)
                act.activation(qT[b], bank(3 + 4 * b), ACT.Copy, scale=SCALE_X).then_inc(s["qT_ready"], 1)

            act.wait_ge(s["nega_ready"], 1)
            act.wait_ge(s["fills_ready"], 5)
            act.wait_ge(s["delta_ready"], 1)
            for n in range(U):
                scan_state(0, n, n)
                if n == 1:
                    dt_exp(1)
                if n == 3:
                    dt_log(1)
            with act.Fori(1, NS // U) as i:
                for j in range(U):
                    scan_state(0, i * U + j, j)
            act.wait_ge(s["delta_ready"], B)
            with act.Fori(0, NS // U - 1) as i:
                for j in range(U):
                    scan_state(1, i * U + j, j)
            x1T_take(0)
            for n in range(NS - U, NS):
                scan_state(1, n, n)
                if n == NS - 2:
                    query_take(0)

            def x_exp(i):
                act.wait_ge(s["xsub_done"], i + 1)
                act.activation(xp[:, i % 2, :], xp[:, i % 2, :], ACT.Exp).then_inc(s["xexp_done"], 1)

            def x_take(i):
                act.wait_ge(s["xpT_psum"], i + 1)
                if i >= 2:
                    act.wait_ge(s["xav_psum"], i - 1)
                full, rows, at = P * (CH - 1), chunk(CH - 1)[1], x_bank(i)
                act.activation(xpT[i % 2].rearrange("p j t -> p (j t)")[:, 0:full],
                               ps[:, at:at + 3, :].rearrange("p a n -> p (a n)")[:, 0:full], ACT.Copy)
                act.activation(xpT[i % 2][0:rows, CH - 1, :], ps[0:rows, at + 2, P:2 * P], ACT.Copy).then_inc(s["xpT_ready"], 1)

            def n_take(n, b):
                m = 2 * n + b
                act.wait_ge(s["nT_psum"], m + 1)
                act.activation(nT[:, b, :], bank(7), ACT.Identity, scale=ln_w[:, n:n + 1],
                               bias=ln_b[:, n:n + 1]).then_inc(s["nT_ready"], 1)
                act.wait_ge(s["nT_ready"], m + 1)
                act.activation(nsq[:, b, :], nT[:, b, :], ACT.Square).then_inc(s["nsq_ready"], 1)

            def gate_exp(m):
                act.wait_ge(s["gshift_ready"], m + 1)
                act.activation(g_ex[:], g_sh[:], ACT.Exp).then_inc(s["gexp_ready"], 1)

            def weights_take(b):
                act.wait_ge(s["rwT_psum"], b + 1)
                act.activation(rwT[:, b, :], ps[0:3 * E, 7, :].bitcast(BF16)[:, 0:T], ACT.Copy).then_inc(s["rwT_ready"], 1)

            for i in range(K * B + 1):
                if i == K + 3:
                    n_take(0, 0)
                if i == 2:
                    x1T_take(1)
                if i == 3:
                    query_take(1)
                if i:
                    x_take(i - 1)
                if i < K * B:
                    x_exp(i)
            gate_exp(0)
            weights_take(0)
            n_take(0, 1)
            gate_exp(1)
            weights_take(1)

            def take_qkv(b):
                act.wait_ge(s["q_k_psum"], 2 * b + 1)
                act.activation(aqT[:, b, :], bank(4), ACT.Copy).then_inc(s["qkv_ready"], 1)
                act.wait_ge(s["q_k_psum"], 2 * b + 2)
                act.activation(akT[:, b, :], bank(5), ACT.Copy).then_inc(s["qkv_ready"], 1)
                act.wait_ge(s["xe_used"], E * (b + 1))
                act.activation(av[:, b].rearrange("p k c -> p (k c)"), bank(6), ACT.Copy).then_inc(s["qkv_ready"], 1)

            def a_exp(b, i):
                act.wait_ge(s["amax_ready"], K * b + i + 1)
                if b:
                    act.wait_ge(s["apT_psum"], i + 1)
                w = P * (i + 1)
                act.activation(ap_[:, i, 0:w], ps[:, a_bank(b, i), 0:w], ACT.Exp, bias=a_nmax[:, i:i + 1], scale=SCALE_A,
                               accum_out=a_sum[:, i:i + 1]).then_inc(s["aexp_done"], 1)

            def a_take(b, i):
                act.wait_ge(s["apT_psum"], K * b + i + 1)
                if b:
                    act.wait_ge(s["att_psum"], i + 1)
                w = P * (i + 1)
                act.activation(apT[:, i, 0:w], ps[:, a_bank(b, i), 0:w], ACT.Copy).then_inc(s["apT_ready"], 1)

            def att_take(b):
                act.wait_ge(s["att_psum"], K * (b + 1))
                act.activation(attnT[:, b, :], bank(att_bank(b)), ACT.Copy).then_inc(s["att_ready"], 1)

            take_qkv(0)
            for pair in range(0, K, 2):
                for i in range(pair, pair + 2):
                    a_exp(0, i)
                for i in range(pair, pair + 2):
                    a_take(0, i)
            att_take(0)
            take_qkv(1)
            for i in range(K):
                a_exp(1, i)
            a_take(1, 0)
            a_take(1, 1)
            a_take(1, 2)
            a_take(1, 3)
            att_take(1)
            n_take(1, 0)

            def moe_gelu(g):
                act.wait_ge(s["h_psum"], g + 1)
                if g >= 4:
                    act.wait_ge(s["down_psum"], E * B + g - 3)
                act.activation(inter[:, g % 4, :], bank(H_BANKS[g % 4]), ACT.Gelu).then_inc(s["inter_ready"], 1)

            gate_exp(2)
            for g in range(7):
                moe_gelu(g)
            n_take(1, 1)
            for g in range(7, 8):
                moe_gelu(g)
            gate_exp(3)
            for g in range(8, E * B):
                moe_gelu(g)

        @block.gpsimd
        def _(pool):
            pool.memset(ones_bf[:], 1.0).then_inc(s["warm_ready"], 1)
            pool.memset(xsT[:, :, :, 0:TAPS - 1], 0.0).then_inc(s["fills_ready"], 1)
            pool.memset(decay[:, :, :, 0:1], 0.0).then_inc(s["fills_ready"], 1)
            pool.memset(ones[:], 1.0).then_inc(s["fills_ready"], 1)
            pool.memset(minus_half[:], -0.5).then_inc(s["fills_ready"], 1)
            pool.memset(mask_parts[:], 0.0).then_inc(s["fills_ready"], 1)
            pool.wait_ge(ld["masks"], 32)
            pool.wait_ge(ld["x0"], 32)
            pool.tensor_copy(sel8[:], cst("sel8", 3 * E).unsqueeze(2).to_broadcast([3 * E, E, P])).then_inc(s["sel_ready"], 1)
            pool.tensor_copy(causal_bf[:], cst("causal")).then_inc(s["sel_ready"], 1)
            pool.tensor_copy(ident_bf[:], ident).then_inc(s["sel_ready"], 1)
            for b in range(B):
                pool.wait_ge(s["kv_ready"], 2 * b + 1)
                pool.tensor_tensor(k_diag[:, b, :].rearrange("p (h t) -> p h t", h=NH),
                                   kT[:, b, :].unsqueeze(1).to_broadcast([P, NH, S2]),
                                   cst("headof").unsqueeze(2).to_broadcast([P, NH, S2]),
                                   ALU.mult).then_inc(s["kdiag_ready"], 1)
            pool.wait_ge(s["simss_ready"], 1)
            pool.wait_ge(s["fills_ready"], 5)
            pool.tensor_tensor(sim_rn[:].rearrange("p n e -> p (n e)"), sim_ss[:].rearrange("p n e -> p (n e)"),
                               minus_half[:], ALU.pow).then_inc(s["simrn_ready"], 1)
            def scan_state(b, n, j):
                g = NS * b + n
                pool.wait_ge(s["scan_done"], g + 1)
                pool.wait_ge(s["crep_ready"], g + 1)
                if b or not isinstance(n, int) or n >= 2:
                    pool.wait_ge(s["sum_done"], g - 1)
                pool.tensor_tensor(prod[:, j % 2], states[:, j % 2],
                                   c_rep[:, j % 2, :].unsqueeze(1).to_broadcast([P, HV, T]),
                                   ALU.mult).then_inc(s["prod_done"], 1)

            norms, gates_done = [0], [0]

            def norm_root(n=1):
                norms[0] += 1
                pool.wait_ge(s["var_ready"], norms[0])
                pool.tensor_tensor(rstd[:, 0:n * K], var_eps[:, 0:n * K], minus_half[:, 0:n * K], ALU.pow).then_inc(s["rstd_ready"], 1)

            def gate_root():
                gates_done[0] += 1
                pool.wait_ge(s["norm_ready"], gates_done[0])
                pool.tensor_tensor(g_rn[:], g_ss[:], minus_half[:, 0:K], ALU.pow).then_inc(s["rnorm_ready"], 1)

            def residual_sum(b):
                pool.wait_ge(s["acc_done"], K * E * (b + 1))
                pool.tensor_tensor(hx[:, b], hs[:, b], x2[:, b], ALU.add).then_inc(s["hx_ready"], 1)

            pool.wait_ge(s["wdt_psum"], HV * B)
            for n in range(U):
                scan_state(0, n, n)
                if n == 2:
                    pool.wait_ge(s["w_ready"], B)
                    pool.tensor_tensor(r_dt[:, 1], e_dt[:, 1], r_dt[:, 1], ALU.subtract).then_inc(s["rdt_ready"], 1)
            with pool.Fori(1, NS // U) as i:
                for j in range(U):
                    scan_state(0, i * U + j, j)
            for n in range(2 * U):
                scan_state(1, n, n)
                if n == 5:
                    norm_root()
            with pool.Fori(2, NS // U) as i:
                for j in range(U):
                    scan_state(1, i * U + j, j)
            norm_root()
            for b in range(B):
                norm_root(2)
                gate_root()
            norm_root()
            residual_sum(0)
            gate_root()
            norm_root()
            residual_sum(1)
            gate_root()
            norm_root()
            norm_root()

        return nc


_WHOLE = ["x", "ctx_1024", "mask_BxS2_ik0", "L0_attn_W_in", "L0_attn_conv_k", "L0_attn_W_x", "L0_attn_W_dt", "L0_attn_W_out",
          "L0_xattn_Wq", "L0_xattn_Wk", "L0_xattn_Wv", "L0_ffn_q_proj", "L0_ffn_k_proj", "L0_ffn_v_proj",
          "L0_ffn_o_proj", "L0_ffn_w1", "L0_ffn_w2"]


def small_columns(inputs):
    def halves(name, n=HV):
        return np.asarray(inputs[name]).reshape(n, P).T

    a_log = np.asarray(inputs["L0_attn_A_log"]).reshape(HV, P, NS).transpose(1, 0, 2).reshape(P, HV * NS)
    columns = [halves("L0_attn_conv_b"), halves("L0_attn_b_dt"), halves("L0_attn_D"),
               halves("L0_ffn_ln1_w", 1), halves("L0_ffn_ln2_w", 1), halves("L0_ffn_ln1_b", 1), halves("L0_ffn_ln2_b", 1),
               a_log, np.asarray(inputs["L0_ffn_smha_sim"]), np.asarray(inputs["L0_ffn_moe_sim"])]
    columns += [np.broadcast_to(np.asarray(inputs[n]), (P, E)) for n in ("L0_ffn_smha_gates", "L0_ffn_moe_gates")]
    return np.ascontiguousarray(np.concatenate(columns, axis=1))


def kernel(**inputs):
    import concourse.bacc as bacc
    from concourse.bass_utils import run_bass_kernel_spmd

    nc = bacc.Bacc("TRN2", target_bir_lowering=False, num_devices=1)
    arrays, aps = {}, {}
    for name in _WHOLE:
        value = np.ascontiguousarray(inputs[name])
        arrays[f"in_{name}"] = value
        aps[name] = nc.dram_tensor(f"in_{name}", value.shape, mybir.dt.from_np(value.dtype), kind="ExternalInput").ap()
    arrays["in_consts"] = shape_constants()
    arrays["in_small"] = small_columns(inputs)
    aps["small"] = nc.dram_tensor("in_small", [P, SMALL_COLS], F32, kind="ExternalInput").ap()
    aps["consts"] = nc.dram_tensor("in_consts", [P, CONST_COLS], F32, kind="ExternalInput").ap()
    out = nc.dram_tensor("out_y", [B, T, C], F32, kind="ExternalOutput").ap()
    decoder_layer(nc, aps, out)
    got = run_bass_kernel_spmd(nc, [arrays], core_ids=[0])
    return got.results[0]["out_y"]
```
